# Optimizing a Trainium2 kernel written in Bass

```python
import numpy as np
import jax
import jax.numpy as jnp

def _softmax(x, axis=-1):
    return jax.nn.softmax(x, axis=axis)

def _gelu(x):
    return jax.nn.gelu(x, approximate=True)

def _silu(x):
    return jax.nn.silu(x)

def _sigmoid(x):
    return jax.nn.sigmoid(x)

def _layernorm(x, axis=-1, eps=1e-05):
    m = jnp.mean(x, axis=axis, keepdims=True)
    v = jnp.var(x, axis=axis, keepdims=True)
    return (x - m) / jnp.sqrt(v + eps)

def _scatter_add(tgt, idx, src, axis=0):
    return tgt.at[idx].add(src)

def _segment_sum(src, seg, n):
    return jax.ops.segment_sum(src, seg, n)
kernel_name = 'mk_audio_tower_d2_tok_audfeat512_r4_ba1c73'

def setup_inputs(seed: int=0):
    np.random.seed(seed)
    _w = jnp.asarray

    def _rec_inputs():
        import jax
        import jax.numpy as jnp
        _rk = jax.random.key(seed)
        x = 7.22013e-05 + 1.00017 * jax.random.normal(jax.random.fold_in(_rk, 1), (32, 750, 64), jnp.float32)
        return x
    x = _rec_inputs()

    def _L0_tok_setup():
        import jax, jax.numpy as jnp
        import numpy as np
        PATCH_LEN = 16
        STRIDE = 8
        D_MODEL = 128
        IN_CH = 64

        def _patch_embed(x, W, b, gamma, beta):
            B, S, C = x.shape
            n_patches = (S - PATCH_LEN) // STRIDE + 1
            idx = jnp.arange(n_patches)[:, None] * STRIDE + jnp.arange(PATCH_LEN)[None, :]
            patches = x[:, idx, :]
            patches = jnp.transpose(patches, (0, 1, 3, 2)).reshape(B, n_patches, C * PATCH_LEN)
            y = jnp.einsum('bpf,fd->bpd', patches, W) + b
            mu = jnp.mean(y, axis=-1, keepdims=True)
            var = jnp.mean(jnp.square(y - mu), axis=-1, keepdims=True)
            y = (y - mu) * jax.lax.rsqrt(var + 1e-05)
            return y * gamma + beta
        key = jax.random.key(seed)
        k1, k2, k3 = jax.random.split(key, 3)
        B, S, C = (32, 1024, IN_CH)
        x = jax.random.normal(k1, (B, S, C), dtype=jnp.float32)
        fan_in = PATCH_LEN * C
        bound = 1.0 / np.sqrt(fan_in)
        W = jax.random.uniform(k2, (fan_in, D_MODEL), minval=-bound, maxval=bound, dtype=jnp.float32)
        b = jax.random.uniform(k3, (D_MODEL,), minval=-bound, maxval=bound, dtype=jnp.float32)
        gamma = jnp.ones((D_MODEL,), dtype=jnp.float32)
        beta = jnp.zeros((D_MODEL,), dtype=jnp.float32)
        return {'x': x, 'W': W, 'b': b, 'gamma': gamma, 'beta': beta}
    _L0_tok_all = _L0_tok_setup()
    _L0_tok_in = {k: v for k, v in _L0_tok_all.items() if k in ('W', 'b', 'gamma', 'beta')}
    del _L0_tok_all

    def _L0_attn_setup():
        import jax, jax.numpy as jnp
        import numpy as np
        B, T, D_X, D_H, N_STATE, D_K, D_V = (2, 512, 128, 128, 16, 64, 64)

        def _linear_params(key, d_in, d_out):
            kw, kb = jax.random.split(key)
            lim = 1.0 / np.sqrt(d_in)
            W = jax.random.uniform(kw, (d_in, d_out), minval=-lim, maxval=lim, dtype=jnp.float32)
            b = jax.random.uniform(kb, (d_out,), minval=-lim, maxval=lim, dtype=jnp.float32)
            return (W, b)

        def _reference_tuple_inner(x_seq, A_log, ln_gamma, ln_beta, delta_W, delta_b, B_W, B_b, C_W, C_b, D_W, D_b, D_scale, key_W, key_b, recall_W, recall_b, gate_W, gate_b, M):
            Bsz, Tlen, _ = x_seq.shape
            d_h, n = A_log.shape
            mu = jnp.mean(x_seq, axis=-1, keepdims=True)
            var = jnp.mean(jnp.square(x_seq - mu), axis=-1, keepdims=True)
            x_ssm = (x_seq - mu) * jax.lax.rsqrt(var + 1e-05) * ln_gamma + ln_beta
            delta = jnp.minimum(jax.nn.softplus(x_ssm @ delta_W + delta_b), 0.5)
            A_cont = -jnp.exp(A_log)
            DeltaA = delta[..., None] * A_cont
            A_bar = jnp.clip(jnp.exp(DeltaA), 0.0, 1.0)
            injection = jnp.where(jnp.abs(A_cont) > 0.0001, jnp.expm1(DeltaA) / A_cont, delta[..., None])
            B_cont = jax.nn.silu(x_ssm @ B_W + B_b).reshape(Bsz, Tlen, d_h, n)
            B_cont = 0.5 * (B_cont - jnp.mean(B_cont, axis=(0, 1), keepdims=True))
            B_bar = jnp.nan_to_num(injection * B_cont, nan=0.0, posinf=1000.0, neginf=-1000.0)
            A_shift = jnp.concatenate([jnp.ones((Bsz, 1, d_h, n), x_seq.dtype), A_bar[:, :-1]], axis=1)
            pps = jnp.exp(jnp.cumsum(jnp.log(jnp.maximum(A_shift, 1e-06)), axis=1))
            h_seq = jnp.cumsum(B_bar * pps, axis=1) / pps
            C_coeff = jax.nn.silu(x_ssm @ C_W + C_b).reshape(Bsz, Tlen, d_h, n)
            h_out = jnp.einsum('btdn,btdn->btd', h_seq, C_coeff)
            y_ssm = h_out + D_scale * (x_seq @ D_W + D_b)
            k = y_ssm @ key_W + key_b
            v_hat = k @ M
            h_mem = v_hat @ recall_W + recall_b
            gate = jax.nn.sigmoid(y_ssm @ gate_W + gate_b)
            y = y_ssm + gate * h_mem
            return (y, h_seq)
        key = jax.random.key(seed)
        ks = jax.random.split(key, 10)
        x_seq = jax.random.normal(ks[0], (B, T, D_X), dtype=jnp.float32)
        delta_W, delta_b = _linear_params(ks[1], D_X, 1)
        B_W, B_b = _linear_params(ks[2], D_X, D_H * N_STATE)
        C_W, C_b = _linear_params(ks[3], D_X, D_H * N_STATE)
        D_W, D_b = _linear_params(ks[4], D_X, D_H)
        key_W, key_b = _linear_params(ks[5], D_H, D_K)
        recall_W, recall_b = _linear_params(ks[6], D_V, D_H)
        gate_W, gate_b = _linear_params(ks[7], D_H, 1)
        M = jax.random.normal(ks[8], (D_K, D_V), dtype=jnp.float32) * 0.02
        return {'x_seq': x_seq, 'A_log': jnp.full((D_H, N_STATE), -5.0, dtype=jnp.float32), 'ln_gamma': jnp.ones((D_H,), jnp.float32), 'ln_beta': jnp.zeros((D_H,), jnp.float32), 'delta_W': delta_W, 'delta_b': delta_b, 'B_W': B_W, 'B_b': B_b, 'C_W': C_W, 'C_b': C_b, 'D_W': D_W, 'D_b': D_b, 'D_scale': jnp.ones((D_H,), jnp.float32), 'key_W': key_W, 'key_b': key_b, 'recall_W': recall_W, 'recall_b': recall_b, 'gate_W': gate_W, 'gate_b': gate_b, 'M': M}
    _L0_attn_all = _L0_attn_setup()
    _L0_attn_in = {k: v for k, v in _L0_attn_all.items() if k in ('A_log', 'ln_gamma', 'ln_beta', 'delta_W', 'delta_b', 'B_W', 'B_b', 'C_W', 'C_b', 'D_W', 'D_b', 'D_scale', 'key_W', 'key_b', 'recall_W', 'recall_b', 'gate_W', 'gate_b', 'M')}
    del _L0_attn_all

    def _L0_ffn_setup():
        import jax, jax.numpy as jnp
        import numpy as np
        EPS = 1e-09
        LN_EPS = 1e-05

        def _layernorm(x, gamma):
            x = x.astype(jnp.float32)
            mu = jnp.mean(x, axis=-1, keepdims=True)
            var = jnp.var(x, axis=-1, keepdims=True)
            return (x - mu) * jax.lax.rsqrt(var + LN_EPS) * gamma
        key = jax.random.key(seed)
        ks = jax.random.split(key, 5)
        b, n, d, e, h = (4, 256, 128, 6, 512)
        x = jax.random.normal(ks[0], (b, n, d), dtype=jnp.float32)
        w_gating = jax.random.normal(ks[1], (d, e), dtype=jnp.float32)
        std1 = 1.0 / np.sqrt(h)
        std2 = 1.0 / np.sqrt(d)
        w1 = jax.random.uniform(ks[2], (e, d, h), jnp.float32, -std1, std1)
        w2 = jax.random.uniform(ks[3], (e, h, d), jnp.float32, -std2, std2)
        gamma = jnp.ones((d,), dtype=jnp.float32)
        return {'x': x, 'w_gating': w_gating, 'gamma': gamma, 'w1': w1, 'w2': w2}
    _L0_ffn_all = _L0_ffn_setup()
    _L0_ffn_in = {k: v for k, v in _L0_ffn_all.items() if k in ('w_gating', 'gamma', 'w1', 'w2')}
    del _L0_ffn_all

    def _L1_attn_setup():
        import jax, jax.numpy as jnp
        import numpy as np
        K = 7
        H = 16
        DIM = 128
        D = DIM // H
        SCALE = D ** (-0.5)
        key = jax.random.key(seed)
        k0, k1, k2, k3 = jax.random.split(key, 4)
        B, L, C = (2, 4096, DIM)
        x = jax.random.normal(k0, (B, L, C), jnp.float32)
        qkv_w = jax.random.normal(k1, (3 * C, C), jnp.float32) * 0.02
        qkv_b = jnp.zeros((3 * C,), jnp.float32)
        rpb = jax.random.normal(k2, (H, 2 * K - 1), jnp.float32) * 0.02
        proj_w = jax.random.normal(k3, (C, C), jnp.float32) * 0.02
        proj_b = jnp.zeros((C,), jnp.float32)
        return {'x': x, 'qkv_w': qkv_w, 'qkv_b': qkv_b, 'rpb': rpb, 'proj_w': proj_w, 'proj_b': proj_b}
    _L1_attn_all = _L1_attn_setup()
    _L1_attn_in = {k: v for k, v in _L1_attn_all.items() if k in ('qkv_w', 'qkv_b', 'rpb', 'proj_w', 'proj_b')}
    del _L1_attn_all

    def _L1_ffn_setup():
        import jax, jax.numpy as jnp
        import numpy as np
        N_CONST = 6
        PARTITIONS_OF_6 = [(6,), (5, 1), (4, 2), (4, 1, 1), (3, 3), (3, 2, 1), (3, 1, 1, 1), (2, 2, 2), (2, 2, 1, 1), (2, 1, 1, 1, 1), (1, 1, 1, 1, 1, 1)]
        N_EXPERTS = 6
        TOP_K = 2

        def _partition_weights():
            w = np.zeros((len(PARTITIONS_OF_6), N_EXPERTS), dtype=np.float32)
            for i, partition in enumerate(PARTITIONS_OF_6):
                for j, part in enumerate(partition):
                    if j < N_EXPERTS:
                        w[i, j] = part / N_CONST
            return jnp.asarray(w)
        key = jax.random.key(seed)
        ks = jax.random.split(key, 6)
        B, S, D, F, E, P = (32, 512, 128, 341, 6, 11)
        scale_in = 1.0 / np.sqrt(D)
        scale_hid = 1.0 / np.sqrt(F)
        return {'x': jax.random.normal(ks[0], (B, S, D), dtype=jnp.float32), 'router_w': jax.random.normal(ks[1], (P, D), dtype=jnp.float32) * scale_in, 'W1': jax.random.normal(ks[2], (E, D, F), dtype=jnp.float32) * scale_in, 'b1': jax.random.normal(ks[3], (E, F), dtype=jnp.float32) * 0.01, 'W2': jax.random.normal(ks[4], (E, F, D), dtype=jnp.float32) * scale_hid, 'b2': jax.random.normal(ks[5], (E, D), dtype=jnp.float32) * 0.01}
    _L1_ffn_all = _L1_ffn_setup()
    _L1_ffn_in = {k: v for k, v in _L1_ffn_all.items() if k in ('router_w', 'W1', 'b1', 'W2', 'b2')}
    del _L1_ffn_all
    return {'x': x, 'L0_tok_W': _L0_tok_in['W'], 'L0_tok_b': _L0_tok_in['b'], 'L0_tok_gamma': _L0_tok_in['gamma'], 'L0_tok_beta': _L0_tok_in['beta'], 'L0_attn_A_log': _L0_attn_in['A_log'], 'L0_attn_ln_gamma': _L0_attn_in['ln_gamma'], 'L0_attn_ln_beta': _L0_attn_in['ln_beta'], 'L0_attn_delta_W': _L0_attn_in['delta_W'], 'L0_attn_delta_b': _L0_attn_in['delta_b'], 'L0_attn_B_W': _L0_attn_in['B_W'], 'L0_attn_B_b': _L0_attn_in['B_b'], 'L0_attn_C_W': _L0_attn_in['C_W'], 'L0_attn_C_b': _L0_attn_in['C_b'], 'L0_attn_D_W': _L0_attn_in['D_W'], 'L0_attn_D_b': _L0_attn_in['D_b'], 'L0_attn_D_scale': _L0_attn_in['D_scale'], 'L0_attn_key_W': _L0_attn_in['key_W'], 'L0_attn_key_b': _L0_attn_in['key_b'], 'L0_attn_recall_W': _L0_attn_in['recall_W'], 'L0_attn_recall_b': _L0_attn_in['recall_b'], 'L0_attn_gate_W': _L0_attn_in['gate_W'], 'L0_attn_gate_b': _L0_attn_in['gate_b'], 'L0_attn_M': _L0_attn_in['M'], 'L0_ffn_w_gating': _L0_ffn_in['w_gating'], 'L0_ffn_gamma': _L0_ffn_in['gamma'], 'L0_ffn_w1': _L0_ffn_in['w1'], 'L0_ffn_w2': _L0_ffn_in['w2'], 'L1_attn_qkv_w': _L1_attn_in['qkv_w'], 'L1_attn_qkv_b': _L1_attn_in['qkv_b'], 'L1_attn_rpb': _L1_attn_in['rpb'], 'L1_attn_proj_w': _L1_attn_in['proj_w'], 'L1_attn_proj_b': _L1_attn_in['proj_b'], 'L1_ffn_router_w': _L1_ffn_in['router_w'], 'L1_ffn_W1': _L1_ffn_in['W1'], 'L1_ffn_b1': _L1_ffn_in['b1'], 'L1_ffn_W2': _L1_ffn_in['W2'], 'L1_ffn_b2': _L1_ffn_in['b2']}

def reference(x, L0_tok_W, L0_tok_b, L0_tok_gamma, L0_tok_beta, L0_attn_A_log, L0_attn_ln_gamma, L0_attn_ln_beta, L0_attn_delta_W, L0_attn_delta_b, L0_attn_B_W, L0_attn_B_b, L0_attn_C_W, L0_attn_C_b, L0_attn_D_W, L0_attn_D_b, L0_attn_D_scale, L0_attn_key_W, L0_attn_key_b, L0_attn_recall_W, L0_attn_recall_b, L0_attn_gate_W, L0_attn_gate_b, L0_attn_M, L0_ffn_w_gating, L0_ffn_gamma, L0_ffn_w1, L0_ffn_w2, L1_attn_qkv_w, L1_attn_qkv_b, L1_attn_rpb, L1_attn_proj_w, L1_attn_proj_b, L1_ffn_router_w, L1_ffn_W1, L1_ffn_b1, L1_ffn_W2, L1_ffn_b2):
    import jax
    import jax.numpy as jnp

    def _L0_tok_ref(x, W, b, gamma, beta):
        import jax, jax.numpy as jnp
        import numpy as np
        PATCH_LEN = 16
        STRIDE = 8
        D_MODEL = 128
        IN_CH = 64

        def _patch_embed(x, W, b, gamma, beta):
            B, S, C = x.shape
            n_patches = (S - PATCH_LEN) // STRIDE + 1
            idx = jnp.arange(n_patches)[:, None] * STRIDE + jnp.arange(PATCH_LEN)[None, :]
            patches = x[:, idx, :]
            patches = jnp.transpose(patches, (0, 1, 3, 2)).reshape(B, n_patches, C * PATCH_LEN)
            y = jnp.einsum('bpf,fd->bpd', patches, W) + b
            mu = jnp.mean(y, axis=-1, keepdims=True)
            var = jnp.mean(jnp.square(y - mu), axis=-1, keepdims=True)
            y = (y - mu) * jax.lax.rsqrt(var + 1e-05)
            return y * gamma + beta
        return _patch_embed(x, W, b, gamma, beta)

    def _L0_attn_ref(x_seq, A_log, ln_gamma, ln_beta, delta_W, delta_b, B_W, B_b, C_W, C_b, D_W, D_b, D_scale, key_W, key_b, recall_W, recall_b, gate_W, gate_b, M):
        import jax, jax.numpy as jnp
        import numpy as np
        B, T, D_X, D_H, N_STATE, D_K, D_V = (2, 512, 128, 128, 16, 64, 64)

        def _linear_params(key, d_in, d_out):
            kw, kb = jax.random.split(key)
            lim = 1.0 / np.sqrt(d_in)
            W = jax.random.uniform(kw, (d_in, d_out), minval=-lim, maxval=lim, dtype=jnp.float32)
            b = jax.random.uniform(kb, (d_out,), minval=-lim, maxval=lim, dtype=jnp.float32)
            return (W, b)

        def _reference_tuple_inner(x_seq, A_log, ln_gamma, ln_beta, delta_W, delta_b, B_W, B_b, C_W, C_b, D_W, D_b, D_scale, key_W, key_b, recall_W, recall_b, gate_W, gate_b, M):
            Bsz, Tlen, _ = x_seq.shape
            d_h, n = A_log.shape
            mu = jnp.mean(x_seq, axis=-1, keepdims=True)
            var = jnp.mean(jnp.square(x_seq - mu), axis=-1, keepdims=True)
            x_ssm = (x_seq - mu) * jax.lax.rsqrt(var + 1e-05) * ln_gamma + ln_beta
            delta = jnp.minimum(jax.nn.softplus(x_ssm @ delta_W + delta_b), 0.5)
            A_cont = -jnp.exp(A_log)
            DeltaA = delta[..., None] * A_cont
            A_bar = jnp.clip(jnp.exp(DeltaA), 0.0, 1.0)
            injection = jnp.where(jnp.abs(A_cont) > 0.0001, jnp.expm1(DeltaA) / A_cont, delta[..., None])
            B_cont = jax.nn.silu(x_ssm @ B_W + B_b).reshape(Bsz, Tlen, d_h, n)
            B_cont = 0.5 * (B_cont - jnp.mean(B_cont, axis=(0, 1), keepdims=True))
            B_bar = jnp.nan_to_num(injection * B_cont, nan=0.0, posinf=1000.0, neginf=-1000.0)
            A_shift = jnp.concatenate([jnp.ones((Bsz, 1, d_h, n), x_seq.dtype), A_bar[:, :-1]], axis=1)
            pps = jnp.exp(jnp.cumsum(jnp.log(jnp.maximum(A_shift, 1e-06)), axis=1))
            h_seq = jnp.cumsum(B_bar * pps, axis=1) / pps
            C_coeff = jax.nn.silu(x_ssm @ C_W + C_b).reshape(Bsz, Tlen, d_h, n)
            h_out = jnp.einsum('btdn,btdn->btd', h_seq, C_coeff)
            y_ssm = h_out + D_scale * (x_seq @ D_W + D_b)
            k = y_ssm @ key_W + key_b
            v_hat = k @ M
            h_mem = v_hat @ recall_W + recall_b
            gate = jax.nn.sigmoid(y_ssm @ gate_W + gate_b)
            y = y_ssm + gate * h_mem
            return (y, h_seq)
        return _reference_tuple_inner(x_seq, A_log, ln_gamma, ln_beta, delta_W, delta_b, B_W, B_b, C_W, C_b, D_W, D_b, D_scale, key_W, key_b, recall_W, recall_b, gate_W, gate_b, M)[0]

    def _L0_ffn_ref(x, w_gating, gamma, w1, w2):
        import jax, jax.numpy as jnp
        import numpy as np
        EPS = 1e-09
        LN_EPS = 1e-05

        def _layernorm(x, gamma):
            x = x.astype(jnp.float32)
            mu = jnp.mean(x, axis=-1, keepdims=True)
            var = jnp.var(x, axis=-1, keepdims=True)
            return (x - mu) * jax.lax.rsqrt(var + LN_EPS) * gamma
        b, n, d = x.shape
        E = w_gating.shape[-1]
        C = max(min(n, int(n * 6.0 / E)), 4)
        raw = jnp.einsum('bnd,de->bne', x, w_gating)
        probs = jax.nn.softmax(raw, axis=-1)
        gate1 = jnp.max(probs, axis=-1)
        idx1 = jnp.argmax(probs, axis=-1)
        mask1 = jax.nn.one_hot(idx1, E, dtype=jnp.float32)
        gates_wo1 = probs * (1.0 - mask1)
        gate2 = jnp.max(gates_wo1, axis=-1)
        denom = gate1 + gate2 + EPS
        gate1 = gate1 / denom
        pos1 = (jnp.cumsum(mask1, axis=-2) - mask1) * mask1
        mask1 = mask1 * (pos1 < float(C)).astype(jnp.float32)
        mask1_flat = jnp.sum(mask1, axis=-1)
        pos1_flat = jnp.sum(pos1, axis=-1).astype(jnp.int32)
        gate1 = gate1 * mask1_flat
        combine = gate1[..., None, None] * mask1_flat[..., None, None] * jax.nn.one_hot(idx1, E, dtype=jnp.float32)[..., None] * jax.nn.one_hot(pos1_flat, C, dtype=jnp.float32)[..., None, :]
        dispatch = (combine != 0).astype(jnp.float32)
        expert_in = jnp.einsum('bnd,bnec->ebcd', x, dispatch)
        xn = _layernorm(expert_in, gamma)
        hidden = jax.nn.gelu(jnp.einsum('ebcd,edh->ebch', xn, w1), approximate=False)
        expert_out = jnp.einsum('ebch,ehd->ebcd', hidden, w2)
        out = jnp.einsum('ebcd,bnec->bnd', expert_out, combine)
        return out

    def _L1_attn_ref(x, qkv_w, qkv_b, rpb, proj_w, proj_b):
        import jax, jax.numpy as jnp
        import numpy as np
        K = 7
        H = 16
        DIM = 128
        D = DIM // H
        SCALE = D ** (-0.5)
        B, L, C = x.shape
        qkv = (x @ qkv_w.T + qkv_b).reshape(B, L, 3, H, D).transpose(2, 0, 3, 1, 4)
        q = qkv[0] * SCALE
        k = qkv[1]
        v = qkv[2]
        pos = jnp.arange(L)
        ni = jnp.clip(pos - K // 2, 0, L - K)
        idx = ni[:, None] + jnp.arange(K)
        kg = k[:, :, idx]
        vg = v[:, :, idx]
        bias = rpb[:, idx - pos[:, None] + (K - 1)]
        attn = jnp.einsum('bhld,bhlkd->bhlk', q, kg) + bias[None]
        attn = jax.nn.softmax(attn, axis=-1)
        out = jnp.einsum('bhlk,bhlkd->bhld', attn, vg)
        out = out.transpose(0, 2, 1, 3).reshape(B, L, C)
        return out @ proj_w.T + proj_b

    def _L1_ffn_ref(x, router_w, W1, b1, W2, b2):
        import jax, jax.numpy as jnp
        import numpy as np
        N_CONST = 6
        PARTITIONS_OF_6 = [(6,), (5, 1), (4, 2), (4, 1, 1), (3, 3), (3, 2, 1), (3, 1, 1, 1), (2, 2, 2), (2, 2, 1, 1), (2, 1, 1, 1, 1), (1, 1, 1, 1, 1, 1)]
        N_EXPERTS = 6
        TOP_K = 2

        def _partition_weights():
            w = np.zeros((len(PARTITIONS_OF_6), N_EXPERTS), dtype=np.float32)
            for i, partition in enumerate(PARTITIONS_OF_6):
                for j, part in enumerate(partition):
                    if j < N_EXPERTS:
                        w[i, j] = part / N_CONST
            return jnp.asarray(w)
        pw = _partition_weights()
        token_repr = x.mean(axis=1)
        logits = token_repr @ router_w.T
        probs = jax.nn.softmax(logits, axis=-1)
        topk_vals, topk_idx = jax.lax.top_k(probs, TOP_K)
        topk_vals = topk_vals / topk_vals.sum(axis=-1, keepdims=True)
        expert_weights = jnp.einsum('bk,bke->be', topk_vals, pw[topk_idx])
        expert_weights = jnp.where(expert_weights > 1e-06, expert_weights, 0.0)
        h = jax.nn.gelu(jnp.einsum('bsd,edf->ebsf', x, W1) + b1[:, None, None, :], approximate=False)
        out_e = jnp.einsum('ebsf,efd->ebsd', h, W2) + b2[:, None, None, :]
        return jnp.einsum('be,ebsd->bsd', expert_weights, out_e)
    h = _L0_tok_ref(x, L0_tok_W, L0_tok_b, L0_tok_gamma, L0_tok_beta)
    h = h + _L0_attn_ref(_layernorm(h, axis=-1), L0_attn_A_log, L0_attn_ln_gamma, L0_attn_ln_beta, L0_attn_delta_W, L0_attn_delta_b, L0_attn_B_W, L0_attn_B_b, L0_attn_C_W, L0_attn_C_b, L0_attn_D_W, L0_attn_D_b, L0_attn_D_scale, L0_attn_key_W, L0_attn_key_b, L0_attn_recall_W, L0_attn_recall_b, L0_attn_gate_W, L0_attn_gate_b, L0_attn_M)
    h = h + _L0_ffn_ref(_layernorm(h, axis=-1), L0_ffn_w_gating, L0_ffn_gamma, L0_ffn_w1, L0_ffn_w2)
    h = h + _L1_attn_ref(_layernorm(h, axis=-1), L1_attn_qkv_w, L1_attn_qkv_b, L1_attn_rpb, L1_attn_proj_w, L1_attn_proj_b)
    h = h + _L1_ffn_ref(_layernorm(h, axis=-1), L1_ffn_router_w, L1_ffn_W1, L1_ffn_b1, L1_ffn_W2, L1_ffn_b2)
    return h

_drawn_inputs = setup_inputs


def setup_inputs(seed=0):
    import zlib

    import numpy as np

    out = dict(_drawn_inputs(seed))
    spreads = {'L0_tok_gamma': (1.0, 0.2),
     'L0_tok_beta': (0.0, 0.1),
     'L0_attn_A_log': (-5.0, 0.2),
     'L0_attn_ln_gamma': (1.0, 0.2),
     'L0_attn_ln_beta': (0.0, 0.1),
     'L0_attn_D_scale': (1.0, 0.2),
     'L0_ffn_gamma': (1.0, 0.2),
     'L1_attn_qkv_b': (0.0, 0.38),
     'L1_attn_proj_b': (0.0, 0.1)}
    factors = {'L0_attn_key_W': 2.78,
     'L0_attn_key_b': 8.0,
     'L0_attn_gate_W': 5.597,
     'L1_attn_rpb': 64.0,
     'L1_ffn_b1': 8.0,
     'L1_ffn_b2': 8.0,
     'L1_attn_qkv_w': 2.721}
    for name, (base, spread) in spreads.items():
        noise = np.random.default_rng([zlib.crc32(name.encode()), seed]).standard_normal(out[name].shape)
        drawn = base * np.exp(spread * noise) if base else spread * noise
        out[name] = jnp.asarray(drawn.astype(out[name].dtype))
    for name, factor in factors.items():
        out[name] = (out[name] * factor).astype(out[name].dtype)
    return out
```

```python
from contextlib import ExitStack

import concourse.bass as bass
from concourse import mybir


def audio_tower(nc, t, out):
    f32 = mybir.dt.float32
    f32r = mybir.dt.float32r
    ALU = mybir.AluOpType
    ACT = mybir.ActivationFunctionType
    AX = mybir.AxisListType.X

    B, L, D = out.shape
    CB = 4
    NCH = B // CB
    NP = NCH // 2
    CT = CB * L
    TOK = B * L
    G = L + 1
    NS = 16
    NE = 6
    HID = 512
    HT = HID // D
    FF = 341
    FT = 3
    FR = FF - 2 * D
    K = 7
    HEADS = 16
    OH = K * HEADS
    NPART = 11
    SCALE = float(D // HEADS) ** -0.5
    EPS = 1e-5
    SEG = [(s, min(512, TOK - s)) for s in range(0, TOK, 512)]
    NSEG = len(SEG)

    names = [("tok_b", 1), ("ln_gamma", 1), ("ln_beta", 1), ("D_b", 1), ("D_scale", 1),
             ("recall_b", 1), ("ffn_gamma", 1), ("qkv_b", 3), ("A_log", NS), ("B_b", NS),
             ("C_b", NS), ("b1", 2 * NE), ("delta_b", 1), ("gate_b", 1)]
    at, NCOL = {}, 0
    for name, n in names:
        at[name] = NCOL
        NCOL += n

    ctx = ExitStack()
    with ctx:
        def sb(name, shape, dt=f32):
            return ctx.enter_context(nc.sbuf_tensor("s_" + name, shape, dt))

        def sem(name):
            return ctx.enter_context(nc.semaphore(name))

        xfm = sb("xfm", [128, TOK])
        xnfm = sb("xnfm", [128, TOK])
        H = sb("H", [L, B, D])
        cols = sb("cols", [128, NCOL])
        rows = sb("rows", [128, 4, D])
        ident = sb("ident", [128, 128])
        wprep = sb("wprep", [128, 6, 128])
        w_D = sb("w_D", [128, 128])
        w_mem = sb("w_mem", [128, 128])
        MR = sb("MR", [64, 128])
        keyb = sb("keyb", [64, 1])
        mem_b = sb("mem_b", [128, 1])
        stat = sb("stat", [L, 2, CB, 6])
        mv = sb("mv", [L, 2, CB, 2])
        rstd = sb("rstd", [L, 2, CB])
        rstd2 = sb("rstd2", [L, 2, CB])
        pa = sb("pa", [L, 2, CB])
        mhalf = sb("mhalf", [L, CB])
        xs = sb("xs", [L, 2, 2, CB, D])
        smallw = sb("smallw", [128, 32])
        A_pos = sb("A_pos", [128, NS])
        A_inj = sb("A_inj", [128, NS])
        A_half = sb("A_half", [128, NS])
        A_neg = sb("A_neg", [128, NS])
        A_c = sb("A_c", [128, NS])
        R_COLS = 10 * TOK + 1
        R = sb("R", [128, R_COLS])
        psum = ctx.enter_context(nc.psum_tensor("psum", [128, 8, 512], f32))

        taken = [0]

        def fresh():
            taken[0] = 0

        def take(*shape, parts=128):
            n = 1
            for s in shape:
                n *= s
            view = R[0:parts, taken[0]:taken[0] + n]
            taken[0] += n
            assert taken[0] <= R_COLS
            if len(shape) > 1:
                ax = "abcd"[:len(shape)]
                view = view.rearrange("p (" + " ".join(ax) + ") -> p " + " ".join(ax),
                                      **{x: s for x, s in zip(ax, shape)})
            return view

        def bank(b, parts=128, n=CT):
            return psum[0:parts, b, 0:n]

        def bank_tm(b):
            return psum[0:L, b, 0:CB * D].rearrange("p (j d) -> p j d", j=CB)

        wload = sem("wload")
        stage_done = sem("stage_done")
        apart = sem("apart")
        prep_mm, prep_cp = sem("prep_mm"), sem("prep_cp")
        prep_act = sem("prep_act")
        dve_step = sem("dve_step")
        pool_step = sem("pool_step")

        N_PREP = 11 * 16

        def wait_apart(eng, s, value):
            eng.wait_ge(s, value)
            eng.sem_inc(apart, 1)

        class Tally:

            def __init__(self, eng, s):
                self.eng, self.sem, self.base, self.n = eng, s, 0, 0

            def add(self, ins):
                self.n += 1
                return ins.then_inc(self.sem, 1)

            def wait(self, apart=False):
                (wait_apart(self.eng, self.sem, self.base + self.n) if apart
                 else self.eng.wait_ge(self.sem, self.base + self.n))

            def loop(self, trips, per):
                start = self.base + self.n
                with self.eng.Fori(0, trips) as i:
                    self.base, self.n = start + i * per, 0
                    yield i
                    assert self.n == per, (self.n, per)
                self.base, self.n = start + trips * per, 0

        def stage_end(eng, k):
            eng.drain().then_inc(stage_done, 1)
            eng.wait_ge(stage_done, 4 * k)

        def fm(tile, c):
            return tile[:, bass.ds(c * CT, CT)]

        def col(name, k=0):
            return cols[:, at[name] + k:at[name] + k + 1]

        class Norm:
            def __init__(self, tag, two):
                self.two = two
                self.n = 2 if two else 1
                self.var_ready = sem(tag + "_var_ready")
                self.rstd_ready = sem(tag + "_rstd_ready")
                self.xs_ready = sem(tag + "_xs_ready")
                self.xT_ready = sem(tag + "_xT_ready")
                self.xT_free = sem(tag + "_xT_free")

        def norm_stats(dve, nm, step, src, u):
            for j in range(CB):
                step.add(dve.bn_stats(stat[:, u, j, :], src[:, j, :]))
            step.wait(True)
            for j in range(CB):
                ins = dve.bn_aggr(mv[:, u, j, :], stat[:, u, j, :])
            ins.then_inc(nm.var_ready, 1)

        def norm_pool(pool, nm, step, u, ready, two):
            step.add(pool.tensor_scalar(pa[:, u, :], mv[:, u, :, 1], 1.0, EPS, ALU.mult, ALU.add))
            step.wait()
            last = pool.tensor_tensor(rstd[:, u, :], pa[:, u, :], mhalf[:, :], ALU.pow)
            if two:
                step.add(last)
                step.wait()
                step.add(pool.tensor_tensor(pa[:, u, :], rstd[:, u, :], rstd[:, u, :], ALU.mult))
                step.wait()
                step.add(pool.tensor_tensor(pa[:, u, :], pa[:, u, :], mv[:, u, :, 1], ALU.mult))
                step.wait(True)
                step.add(pool.tensor_scalar(pa[:, u, :], pa[:, u, :], 1.0, EPS, ALU.mult, ALU.add))
                step.wait()
                step.add(pool.tensor_tensor(pa[:, u, :], pa[:, u, :], mhalf[:, :], ALU.pow))
                step.wait()
                last = pool.tensor_tensor(rstd2[:, u, :], pa[:, u, :], rstd[:, u, :], ALU.mult)
            last.then_inc(ready, 1)

        def norm_apply(dve, nm, u, c):
            dve.wait_ge(nm.xT_ready, nm.n * (c + 1))
            for w, r in ((0, rstd), (1, rstd2))[:nm.n]:
                for j in range(CB):
                    ins = dve.tensor_scalar(xs[:, u, w, j, :], H[:, bass.ds(c * CB + j, 1), :].rearrange("p a d -> p (a d)"),
                                            mv[:, u, j, 0:1], r[:, u, j:j + 1], ALU.subtract, ALU.mult)
            ins.then_inc(nm.xs_ready, 1)

        def norm_transposes(pe, nm, u, c, banks):
            pe.wait_ge(nm.xs_ready, c + 1)
            for w in range(nm.n):
                pe.wait_ge(nm.xT_free, nm.n * c + w + 1)
                b = banks[w if nm.two else u]
                for j in range(CB):
                    ins = pe.transpose(psum[:, b, j * L:(j + 1) * L], xs[:, u, w, j, :], ident[0:L, 0:L])
                ins.then_inc(nm.xT_ready, 1)

        def norm_copies(act, nm, u, c, banks, scale=None, bias=None):
            for w in range(nm.n):
                wait_apart(act, nm.xT_ready, 2 * nm.n + nm.n * c + w + 1)
                b = banks[w if nm.two else u]
                if w == 0:
                    ins = act.activation(fm(xfm, c), bank(b), ACT.Copy)
                else:
                    ins = act.activation(fm(xnfm, c), bank(b), ACT.Identity, scale=scale,
                                         bias=0.0 if bias is None else bias)
                ins.then_inc(nm.xT_free, 1)

        fresh()
        w_emb = take(4, 2, D)
        xg = take(2, 4, CB * G)
        y_fm = take(2, CT)
        yn = take(2, CB, D, parts=L)
        nA = Norm("a", True)
        nA0 = sem("a_var0_ready"), sem("a_rstd0_ready")
        xg_ready = [sem("xg_ready0"), sem("xg_ready1")]
        y_mm = sem("y_mm")
        y_fm_ready = sem("y_fm_ready")
        yT_ready = sem("yT_ready")
        yT_free = sem("yT_free")

        fresh()
        dl = take(1 + TOK)
        bufB = take(2, TOK)
        bufC = take(2, TOK)
        th = take(2, TOK)
        ea = take(TOK)
        ra = take(2, TOK)
        wBC = sb("wBC", [128, 2, 2, D])
        w_hi = sb("w_hi", [128, 2, 2, D], f32r)
        w_lo = sb("w_lo", [128, 2, 2, D], f32r)
        xn_hi = sb("xn_hi", [128, TOK], f32r)
        xn_lo = sb("xn_lo", [128, TOK], f32r)
        w_hi_ready, w_split, x_split = sem("w_hi_ready"), sem("w_split"), sem("x_split")
        part = sb("part", [128, 2, NSEG])
        mean = sb("mean", [128, 2])
        skip_b = sb("skip_b", [128, 1])
        delta_mm, delta_act = sem("delta_mm"), sem("delta_act")
        wBC_ready = [sem("wBC_ready0"), sem("wBC_ready1")]
        bc_mm = sem("bc_mm")
        bc_free = sem("bc_free")
        C_ready = sem("C_ready")
        th_ready, ea_ready, ra_ready = sem("th_ready"), sem("ea_ready"), sem("ra_ready")
        th_free, ea_free, ra_free = sem("th_free"), sem("ea_free"), sem("ra_free")
        B_free = sem("B_free")
        prod_ready = sem("prod_ready")
        C_free = sem("C_free")
        acc_done = sem("acc_done")

        fresh()
        Y = take(TOK)
        sig = take(2, CT)
        cF = take(2, CT)
        lgF = take(2, CT, parts=NE)
        lg = take(B, NE, parts=L)
        nC = Norm("c", True)
        Y_ready = sem("Y_ready")
        hm_mm = sem("hm_mm")
        sig_ready = sem("sig_ready")
        hm_free = sem("hm_free")
        cF_ready = sem("cF_ready")
        cT_ready = sem("cT_ready")
        cT_free = sem("cT_free")
        lgF_mm, lgF_ready, lgT_ready, lg_free = sem("lgF_mm"), sem("lgF_ready"), sem("lgT_ready"), sem("lg_free")
        ex = take(B, NE, parts=L)
        oh = take(B, NE, parts=L)
        cand = take(B, NE, parts=L)
        gw = take(B, NE, parts=L)
        r1 = take(B, parts=L)
        r2 = take(B, parts=L)
        r3 = take(B, parts=L)
        r4 = take(B, parts=L)
        prio = sb("prio", [128, 16])
        rt_a, rt_b = sem("rt_a"), sem("rt_b")
        w1 = take(NE, HID)
        w2 = take(NE, HT, D)
        hid = take(2, HT, CT)
        w12_ready = sem("w12_ready")
        h_mm, h_free = sem("h_mm"), sem("h_free")
        hid_ready = sem("hid_ready")
        o_mm, o_free = sem("o_mm"), sem("o_free")
        fresh()
        w_qkv = take(3, D)
        w_proj = take(D)
        sel = take(K, OH)
        spread = take(K, D, parts=OH)
        rpb_w = take(OH, parts=K)
        posc = take(CT, parts=K)
        qkv = take(2, 3, CT)
        prod = take(2, K, CT)
        S_fm = take(2, CT, parts=OH)
        P_tm = take(2, CB, OH, parts=L)
        P_fm = take(2, CT, parts=OH)
        pv = take(2, CT)
        pv_t = take(2, CT)
        mx = take(2, CB, HEADS, parts=L)
        sm = take(2, CB, HEADS, parts=L)
        qb = take(1)
        at_tmp = take(CB, D, parts=L)
        nE = Norm("e", False)
        wE_ready = sem("wE_ready")
        qkv_mm, qkv_ready = sem("qkv_mm"), sem("qkv_ready")
        prod_r, S_mm, S_ready = sem("at_prod"), sem("S_mm"), sem("S_ready")
        ST_ready, sub_done, exp_done, P_ready = sem("ST_ready"), sem("sub_done"), sem("exp_done"), sem("P_ready")
        PT_ready, P_fm_ready = sem("PT_ready"), sem("P_fm_ready")
        pb_mm, pb_free, pv_ready = sem("pb_mm"), sem("pb_free"), sem("pv_ready")
        proj_mm, add_done = sem("proj_mm"), sem("add_done")
        fresh()
        v1 = take(NE, FF)
        v2 = take(NE, 2, D)
        v2b = take(NE, D, parts=FR)
        b1b = take(NE, parts=FR)
        b2 = take(D, parts=NE)
        pw = take(NE, parts=NPART)
        pwb = take(NE, D, parts=NPART)
        fh = take(2, FT, CT)
        facc = take(2, CT)
        fo = take(2, CB, D, parts=L)
        srep = take(B)
        z = take(8, 16, parts=B)
        zs = take(8, parts=B)
        wcT = take(B, parts=NPART)
        ew = take(NE, B)
        ewT = take(B, parts=NE)
        bb = take(B)
        nF = Norm("f", False)
        wF_ready = sem("wF_ready")
        rt_pe, rt_dve, rt_act = sem("rt_pe"), sem("rt_dve"), sem("rt_act")
        f_mm, f_free, fh_ready = sem("f_mm"), sem("f_free"), sem("fh_ready")
        fo_mm, fo_free = sem("fo_mm"), sem("fo_free")
        facc_ready, fT_ready, out_ready = sem("facc_ready"), sem("fT_ready"), sem("out_ready")
        out_done = [sem("out_done0"), sem("out_done1")]

        block = ctx.enter_context(nc.Block())

        @block.sync
        def _(sp):
            sp.dma_start(w_emb, t["w_emb"]).then_inc(wload, 16)
            sp.dma_start(cols[:, :], t["cols"]).then_inc(wload, 16)
            sp.dma_start(ident[:, :], t["ident"]).then_inc(wload, 16)
            sp.dma_start(rows[:, :, :], t["rows"]).then_inc(wload, 16)
            sp.dma_start(wprep[:, 0:3, :], t["w_full"]).then_inc(wload, 16)
            sp.dma_start(wprep[0:64, 3, :], t["key_WT"]).then_inc(wload, 16)
            sp.dma_start(wprep[0:64, 4, 0:64], t["M_T"]).then_inc(wload, 16)
            sp.dma_start(wprep[0:64, 5, :], t["recall_W"]).then_inc(wload, 16)
            sp.dma_start(keyb[:, :], t["key_b"]).then_inc(wload, 16)
            sp.dma_start(smallw[:, 0:NE + NPART], t["smallw"]).then_inc(wload, 16)
            sp.dma_start(prio[:, :], t["prio"]).then_inc(wload, 16)
            with sp.Fori(0, NP) as i:
                for u in range(2):
                    sp.wait_ge(y_mm, i * 2 + u + 1)
                    sp.dma_start(xg[:, u], t["xg"][bass.ds(i * 2 + u, 1)].rearrange("a p j n -> (a p) j n"))\
                        .then_inc(xg_ready[u], 16)
            with sp.Fori(0, NS // 2) as i:
                for u in range(2):
                    sp.wait_ge(w_split, i * 2 + u + 1)
                    sp.dma_start(wBC[:, u], t["wBC"][bass.ds(i * 2 + u, 1)].rearrange("a p w d -> (a p) w d"))\
                        .then_inc(wBC_ready[u], 16)
            sp.wait_ge(stage_done, 4 * 3)
            sp.dma_start(w1, t["w1"]).then_inc(w12_ready, 16)
            sp.dma_start(w2, t["w2"]).then_inc(w12_ready, 16)
            sp.wait_ge(stage_done, 4 * 5)
            for dst, name in ((w_qkv, "w_qkv"), (w_proj, "w_proj"), (sel, "sel"), (spread, "spread"),
                              (rpb_w, "rpb_w"), (posc, "posc")):
                sp.dma_start(dst, t[name]).then_inc(wE_ready, 16)
            sp.wait_ge(stage_done, 4 * 7)
            for dst, name in ((v1, "v1"), (v2, "v2"), (v2b, "v2b"), (b1b, "b1b"), (b2, "b2"), (pw, "pw"),
                              (pwb, "pwb")):
                sp.dma_start(dst, t[name]).then_inc(wF_ready, 16)
            with sp.Fori(0, NP) as i:
                for u in range(2):
                    sp.wait_ge(out_ready, i * 2 + u + 3)
                    sp.dma_start(out[bass.ds((i * 2 + u) * CB, CB)].rearrange("b l d -> l b d"), fo[:, u])\
                        .then_inc(out_done[u], 16)
            for u in range(2):
                sp.wait_ge(out_done[u], 16 * (NP + 1))

        @block.gpsimd
        def _(pool):
            step = Tally(pool, pool_step)
            step.add(pool.memset(mhalf[:, :], -0.5))
            pool.sem_inc(w_split, 2)
            step.wait()
            for i in step.loop(NP, 2 * 1 + 2 * 6):
                for u in range(2):
                    wait_apart(pool, nA0[0], i * 2 + u + 1)
                    norm_pool(pool, nA, step, u, nA0[1], False)
                for u in range(2):
                    wait_apart(pool, nA.var_ready, i * 2 + u + 1)
                    norm_pool(pool, nA, step, u, nA.rstd_ready, True)
            stage_end(pool, 1)
            with pool.Fori(0, NCH) as c:
                pool.tensor_copy(fm(xn_hi, c), fm(xnfm, c)).then_inc(x_split, 1)
                pool.wait_ge(x_split, 2 * c + 1)
                pool.tensor_tensor(fm(xn_lo, c), fm(xnfm, c), fm(xn_hi, c).bitcast(f32), ALU.subtract)\
                    .then_inc(x_split, 1)
            stage_end(pool, 2)
            with pool.Fori(0, NS // 2) as i:
                for u in range(2):
                    n = i * 2 + u
                    pool.wait_ge(wBC_ready[u], 16 * (i + 1))
                    wait_apart(pool, C_ready, n + 1)
                    pool.tensor_copy(w_hi[:, u], wBC[:, u]).then_inc(w_hi_ready, 1)
                    pool.wait_ge(w_hi_ready, n + 1)
                    pool.tensor_tensor(w_lo[:, u], wBC[:, u], w_hi[:, u].bitcast(f32), ALU.subtract)\
                        .then_inc(w_split, 1)
            stage_end(pool, 3)
            for i in step.loop(NP, 2 * 6):
                for u in range(2):
                    wait_apart(pool, nC.var_ready, i * 2 + u + 1)
                    norm_pool(pool, nC, step, u, nC.rstd_ready, True)
            stage_end(pool, 4)
            stage_end(pool, 5)
            for i in step.loop(NP, 2):
                for u in range(2):
                    wait_apart(pool, nE.var_ready, i * 2 + u + 1)
                    norm_pool(pool, nE, step, u, nE.rstd_ready, False)
            stage_end(pool, 6)
            stage_end(pool, 7)
            for i in step.loop(NP, 2):
                for u in range(2):
                    wait_apart(pool, nF.var_ready, i * 2 + u + 1)
                    norm_pool(pool, nF, step, u, nF.rstd_ready, False)
            stage_end(pool, 8)

        @block.scalar
        def _(act):
            act.wait_ge(wload, N_PREP)
            act.activation(A_pos[:, :], cols[:, at["A_log"]:at["A_log"] + NS], ACT.Exp).then_inc(prep_act, 1)
            act.sem_inc(y_fm_ready, 2)
            act.sem_inc(nA.xT_free, 2)
            act.sem_inc(C_ready, 2)

            def bias_copy(i):
                for u in range(2):
                    act.wait_ge(y_mm, i * 2 + u + 3)
                    act.wait_ge(yT_ready, i * 2 + u + 1)
                    act.activation(y_fm[:, u], bank(u), ACT.Identity, bias=col("tok_b"), scale=1.0)\
                        .then_inc(y_fm_ready, 1)

            bias_copy(0)
            with act.Fori(1, NP) as i:
                bias_copy(i)
                for u in range(2):
                    norm_copies(act, nA, u, (i - 1) * 2 + u, (4, 5), col("ln_gamma"), col("ln_beta"))
            for u in range(2):
                norm_copies(act, nA, u, (NP - 1) * 2 + u, (4, 5), col("ln_gamma"), col("ln_beta"))
            stage_end(act, 1)
            act.wait_ge(delta_act, NCH)
            act.activation(dl[:, 1:1 + TOK], dl[:, 1:1 + TOK], ACT.Exp).then_inc(delta_act, 1)
            act.wait_ge(delta_act, NCH + 1)
            act.activation(dl[:, 1:1 + TOK], dl[:, 1:1 + TOK], ACT.Ln, bias=1.0, scale=1.0).then_inc(delta_act, 1)
            stage_end(act, 2)

            act.sem_inc(bc_free, 2)

            def decays(i):
                for u in range(2):
                    n = i * 2 + u
                    wait_apart(act, th_free, n + 1)
                    act.activation(th[:, u], dl[:, 1:1 + TOK], ACT.Tanh, scale=A_half[:, bass.ds(n, 1)])\
                        .then_inc(th_ready, 1)
                    wait_apart(act, ea_free, n + 1)
                    act.activation(ea, dl[:, 1:1 + TOK], ACT.Exp, scale=A_neg[:, bass.ds(n, 1)])\
                        .then_inc(ea_ready, 1)
                    wait_apart(act, ra_free, n + 1)
                    act.activation(ra[:, u], dl[:, 0:TOK], ACT.Exp, scale=A_pos[:, bass.ds(n, 1)])\
                        .then_inc(ra_ready, 1)

            def silus(i):
                for u in range(2):
                    n = i * 2 + u
                    act.wait_ge(B_free, n + 1)
                    for s, (a, w) in enumerate(SEG):
                        wait_apart(act, bc_mm, (i * 2 + u) * 2 * NSEG + s + 1)
                        ins = act.activation(bufB[:, u, a:a + w], psum[:, 6 + s % 2, 0:w], ACT.Silu,
                                             bias=cols[:, bass.ds(n + at["B_b"], 1)], scale=1.0,
                                             accum_out=part[:, u, s:s + 1])
                        ins.then_inc(bc_free, 1)
                    act.wait_ge(C_free, n + 1)
                    for s, (a, w) in enumerate(SEG):
                        wait_apart(act, bc_mm, (i * 2 + u) * 2 * NSEG + NSEG + s + 1)
                        act.activation(bufC[:, u, a:a + w], psum[:, 6 + s % 2, 0:w], ACT.Silu,
                                       bias=cols[:, bass.ds(n + at["C_b"], 1)], scale=1.0).then_inc(bc_free, 1)
                    act.sem_inc(C_ready, 1)

            with act.Fori(0, NS // 2) as i:
                decays(i)
                silus(i)
            act.wait_ge(acc_done, 1)
            for s, (a, w) in enumerate(SEG):
                ins = act.activation(Y[:, a:a + w], psum[:, s, 0:w], ACT.Identity, bias=skip_b[:, 0:1], scale=1.0)
            stage_end(act, 3)

            act.sem_inc(nC.xT_free, 2)

            def gates(i):
                for u in range(2):
                    act.wait_ge(hm_mm, i * 2 + u + 1)
                    act.wait_ge(hm_free, i * 2 + u + 1)
                    act.activation(sig[:, u], bank(2 + u), ACT.Sigmoid, bias=col("gate_b"), scale=1.0)\
                        .then_inc(sig_ready, 1)

            with act.Fori(0, NP) as i:
                gates(i)
                for u in range(2):
                    norm_copies(act, nC, u, i * 2 + u, (6, 7), col("ffn_gamma"))
                for u in range(2):
                    act.wait_ge(lgF_mm, i * 2 + u + 1)
                    act.activation(lgF[:, u], bank(2 + u, NE), ACT.Copy).then_inc(lgF_ready, 1)
            stage_end(act, 4)
            act.wait_ge(rt_a, 1)
            act.activation(ex, lg, ACT.Exp).then_inc(rt_b, 1)

            act.sem_inc(h_free, HT)
            with act.Fori(0, NCH) as c:
                for e in range(NE):
                    for j in range(HT):
                        if j == 0:
                            act.wait_ge(o_mm, c * NE + e + 1)
                        act.wait_ge(h_mm, (c * NE + e) * HT + j + 1)
                        act.activation(hid[:, e % 2, j], bank(j), ACT.Gelu).then_inc(h_free, 1)
            stage_end(act, 5)

            act.sem_inc(nE.xT_free, 2)
            act.wait_ge(wE_ready, 6 * 16)
            with act.Fori(0, NP) as i:
                for u in range(2):
                    norm_copies(act, nE, u, i * 2 + u, (6, 7))
            act.mul(qb, col("qkv_b"), SCALE)
            stage_end(act, 6)
            with act.Fori(0, NP) as i:
                for u in range(2):
                    c = i * 2 + u
                    act.wait_ge(add_done, c + 1)
                    for k in range(3):
                        act.wait_ge(qkv_mm, c * 3 + k + 1)
                        act.activation(qkv[:, u, k], bank(k), ACT.Identity,
                                       bias=qb if k == 0 else col("qkv_b", k),
                                       scale=SCALE if k == 0 else 1.0).then_inc(qkv_ready, 1)
                for u in range(2):
                    c = i * 2 + u
                    act.wait_ge(S_mm, c + 1)
                    act.activation(S_fm[:, u], bank(3 + u, OH), ACT.Copy).then_inc(S_ready, 1)
                for u in range(2):
                    c = i * 2 + u
                    act.wait_ge(sub_done, c + 1)
                    act.activation(P_tm[:, u], P_tm[:, u], ACT.Exp).then_inc(exp_done, 1)
                for u in range(2):
                    c = i * 2 + u
                    act.wait_ge(PT_ready, c + 1)
                    act.activation(P_fm[:, u], bank(3 + u, OH), ACT.Copy).then_inc(P_fm_ready, 1)
            stage_end(act, 7)

            act.sem_inc(nF.xT_free, 2)
            act.wait_ge(wF_ready, 7 * 16)
            with act.Fori(0, NP) as i:
                for u in range(2):
                    norm_copies(act, nF, u, i * 2 + u, (6, 7))
            stage_end(act, 8)
            act.sem_inc(f_free, FT)
            act.wait_ge(rt_act, 1)
            act.activation(z[:, 1, 0:NPART], z[:, 0, 0:NPART], ACT.Exp).then_inc(rt_act, 1)
            with act.Fori(0, NCH) as c:
                for e in range(NE):
                    act.wait_ge(fo_mm, c * NE + e + 1)
                    for j in range(FT):
                        kk = D if j < 2 else FR
                        act.wait_ge(f_mm, (c * NE + e) * FT + j + 1)
                        act.activation(fh[0:kk, e % 2, j], bank(j, kk), ACT.Gelu,
                                       bias=col("b1", 2 * e + j) if j < 2 else b1b[:, e:e + 1], scale=1.0)\
                            .then_inc(f_free, 1)

        @block.vector
        def _(dve):
            step = Tally(dve, dve_step)
            dve.wait_ge(wload, N_PREP)
            step.add(dve.tensor_tensor(w_D[:, :], wprep[:, 0, :], rows[:, 3, :], ALU.mult))
            step.add(dve.tensor_tensor(skip_b[:, 0:1], col("D_b"), col("D_scale"), ALU.mult))
            dve.wait_ge(prep_act, 1)
            step.add(dve.tensor_scalar(A_c[:, :], A_pos[:, :], 1e-4, None, ALU.is_gt))
            step.wait()
            step.add(dve.scalar_tensor_tensor(A_inj[:, :], A_pos[:, :], -1e-12, A_c[:, :], ALU.add, ALU.mult))
            step.wait()
            step.add(dve.tensor_scalar(A_inj[:, :], A_inj[:, :], 1e-12, None, ALU.add))
            step.wait()
            step.add(dve.tensor_scalar(A_half[:, :], A_inj[:, :], 0.5, None, ALU.mult))
            step.add(dve.tensor_scalar(A_neg[:, :], A_inj[:, :], -1.0, None, ALU.mult))
            step.add(dve.reciprocal(A_c[:, :], A_inj[:, :]))
            step.wait()
            step.add(dve.tensor_scalar(A_c[:, :], A_c[:, :], 0.5, None, ALU.mult))
            dve.wait_ge(prep_mm, 1)
            dve.tensor_copy(MR[:, :], psum[0:64, 7, 0:D]).then_inc(prep_cp, 1)
            dve.wait_ge(prep_mm, 2)
            step.add(dve.tensor_copy(w_mem[:, :], psum[:, 7, 0:D]))
            step.add(dve.tensor_tensor(mem_b[:, :], psum[:, 7, D:D + 1], col("recall_b"), ALU.add))

            def seqs(tile, c):
                return tile[:, bass.ds(c * CB, CB), :]

            def row(k):
                return rows[0:L, k:k + 1, :].to_broadcast([L, CB, D])

            PER_A = 2 * (CB + 2 + CB)
            for i in step.loop(NP, PER_A):
                for u in range(2):
                    dve.wait_ge(yT_ready, i * 2 + u + 3)
                    src = bank_tm(2 + u)
                    for j in range(CB):
                        step.add(dve.bn_stats(stat[:, u, j, :], src[:, j, :]))
                    step.wait(True)
                    for j in range(CB):
                        ins = dve.bn_aggr(mv[:, u, j, :], stat[:, u, j, :])
                    ins.then_inc(nA0[0], 1)
                for u in range(2):
                    c = i * 2 + u
                    src = bank_tm(2 + u)
                    dve.wait_ge(nA0[1], c + 1)
                    for j in range(CB):
                        ins = dve.tensor_scalar(yn[:, u, j, :], src[:, j, :], mv[:, u, j, 0:1], rstd[:, u, j:j + 1],
                                                ALU.subtract, ALU.mult)
                    ins.then_inc(yT_free, 1)
                    dve.wait_ge(yT_free, 2 + c + 1)
                    step.add(dve.tensor_tensor(yn[:, u], yn[:, u], row(0), ALU.mult))
                    step.wait()
                    step.add(dve.tensor_tensor(seqs(H, c), yn[:, u], row(1), ALU.add))
                    step.wait(True)
                    norm_stats(dve, nA, step, seqs(H, c), u)
                for u in range(2):
                    dve.wait_ge(nA.rstd_ready, i * 2 + u + 1)
                    norm_apply(dve, nA, u, i * 2 + u)
            stage_end(dve, 1)

            dve.memset(dl[:, 0:1], 0.0)
            with dve.Fori(0, NP) as i:
                for u in range(2):
                    c = i * 2 + u
                    dve.wait_ge(delta_mm, c + 3)
                    dve.tensor_scalar(dl[:, bass.ds(c * CT + 1, CT)], bank(u), col("delta_b"), 0.0, ALU.add, ALU.min)\
                        .then_inc(delta_act, 1)
            dve.wait_ge(delta_act, NCH + 2)
            step.add(dve.tensor_scalar(dl[:, 1:1 + TOK], dl[:, 1:1 + TOK], 0.5, None, ALU.min))
            stage_end(dve, 2)

            dve.sem_inc(th_free, 2)
            dve.sem_inc(ea_free, 1)
            dve.sem_inc(ra_free, 2)
            dve.sem_inc(B_free, 2)
            for i in step.loop(NS // 2, 2 * 5):
                for u in range(2):
                    n = i * 2 + u
                    dve.wait_ge(th_ready, n + 1)
                    dve.wait_ge(ea_ready, n + 1)
                    dve.scalar_tensor_tensor(th[:, u], ea, 1.0, th[:, u], ALU.add, ALU.mult).then_inc(ea_free, 1)
                    dve.wait_ge(ra_ready, n + 1)
                    step.add(dve.tensor_scalar(ra[:, u], ra[:, u], 1e6, None, ALU.min))
                    step.wait()
                    step.add(dve.memset(ra[:, u, 0:TOK:L], 0.0))
                for u in range(2):
                    n = i * 2 + u
                    dve.wait_ge(bc_free, 2 + (n * 2 + 1) * NSEG)
                    step.add(dve.reduce_sum(mean[:, u:u + 1], part[:, u, :], axis=AX))
                    step.wait()
                    step.add(dve.tensor_scalar(mean[:, u:u + 1], mean[:, u:u + 1], 1.0 / TOK, None, ALU.mult))
                    step.wait()
                    dve.scalar_tensor_tensor(bufB[:, u], bufB[:, u], mean[:, u:u + 1], th[:, u],
                                             ALU.subtract, ALU.mult).then_inc(th_free, 1)
                    dve.wait_ge(th_free, 2 + n + 1)
                    dve.tensor_tensor_scan(bufB[:, u], ra[:, u], bufB[:, u], 0.0, ALU.mult, ALU.add).then_inc(ra_free, 1)
                    dve.wait_ge(ra_free, 2 + n + 1)
                    dve.wait_ge(bc_free, 2 + (n * 2 + 2) * NSEG)
                    step.add(dve.scalar_tensor_tensor(bufC[:, u], bufB[:, u], A_c[:, bass.ds(n, 1)], bufC[:, u],
                                                      ALU.mult, ALU.mult))
                    step.wait()
                    dve.sem_inc(B_free, 1)
                    dve.sem_inc(prod_ready, 1)
            stage_end(dve, 3)

            dve.sem_inc(hm_free, 2)
            dve.sem_inc(cT_free, 2)
            dve.sem_inc(lg_free, 2)
            PER_C = 2 * (1 + 1 + 4)
            for i in step.loop(NP, PER_C):
                for u in range(2):
                    c = i * 2 + u
                    dve.wait_ge(sig_ready, c + 1)
                    dve.wait_ge(cT_ready, c + 1)
                    step.add(dve.scalar_tensor_tensor(cF[:, u], bank(u), mem_b[:, 0:1], sig[:, u], ALU.add, ALU.mult))
                    step.wait()
                    dve.sem_inc(hm_free, 1)
                    dve.tensor_tensor(cF[:, u], cF[:, u], fm(Y, c), ALU.add).then_inc(cF_ready, 1)
                for u in range(2):
                    c = i * 2 + u
                    dve.wait_ge(cT_ready, c + 3)
                    step.add(dve.tensor_tensor(seqs(H, c), bank_tm(4 + u), seqs(H, c), ALU.add))
                    step.wait()
                    dve.sem_inc(cT_free, 1)
                    norm_stats(dve, nC, step, seqs(H, c), u)
                for u in range(2):
                    dve.wait_ge(nC.rstd_ready, i * 2 + u + 1)
                    norm_apply(dve, nC, u, i * 2 + u)
                for u in range(2):
                    c = i * 2 + u
                    dve.wait_ge(lgT_ready, c + 1)
                    dve.tensor_copy(lg[:, bass.ds(c * CB, CB), :],
                                    psum[0:L, 2 + u, 0:CB * NE].rearrange("p (j e) -> p j e", j=CB))\
                        .then_inc(lg_free, 1)
            stage_end(dve, 4)

            def per_e(x):
                return x.rearrange("p (b o) -> p b o", o=1).to_broadcast([L, B, NE])

            def tt(o, a, b, op):
                step.add(dve.tensor_tensor(o, a, b, op))
                step.wait()

            step.add(dve.tensor_reduce(r1, lg, AX, ALU.max))
            step.wait()
            dve.tensor_tensor(lg, lg, per_e(r1), ALU.subtract).then_inc(rt_a, 1)
            dve.wait_ge(rt_b, 1)
            step.add(dve.tensor_reduce(r2, ex, AX, ALU.add))
            step.add(dve.tensor_reduce(r1, ex, AX, ALU.max))
            step.wait()
            tt(oh, ex, per_e(r1), ALU.is_equal)
            tt(cand, oh, prio[0:L, 0:NE].rearrange("p (o e) -> p o e", o=1).to_broadcast([L, B, NE]), ALU.mult)
            step.add(dve.tensor_reduce(r3, cand, AX, ALU.max))
            step.wait()
            tt(oh, cand, per_e(r3), ALU.is_equal)
            tt(cand, ex, oh, ALU.mult)
            tt(cand, ex, cand, ALU.subtract)
            step.add(dve.tensor_reduce(r3, cand, AX, ALU.max))
            step.add(dve.reciprocal(r4, r2))
            step.wait()
            tt(r1, r1, r4, ALU.mult)
            tt(r3, r3, r4, ALU.mult)
            tt(r3, r3, r1, ALU.add)
            step.add(dve.tensor_scalar(r3, r3, 1e-9, None, ALU.add))
            step.wait()
            step.add(dve.reciprocal(r3, r3))
            step.wait()
            tt(r1, r1, r3, ALU.mult)
            tt(gw, oh, per_e(r1), ALU.mult)

            dve.sem_inc(o_free, 2)
            for c in step.loop(NCH, NE * CB):
                for e in range(NE):
                    dve.wait_ge(o_mm, c * NE + e + 3)
                    if e:
                        step.wait()
                    for j in range(CB):
                        s = H[:, bass.ds(c * CB + j, 1), :].rearrange("p a d -> p (a d)")
                        step.add(dve.scalar_tensor_tensor(s, bank_tm(4 + e % 2)[:, j, :],
                                                          gw[:, bass.ds(c * CB + j, 1), e],
                                                          s, ALU.mult, ALU.add))
                    step.wait()
                    dve.sem_inc(o_free, 1)
            stage_end(dve, 5)

            def norm_loop(nm):
                for i in step.loop(NP, 2 * 4):
                    for u in range(2):
                        norm_stats(dve, nm, step, seqs(H, i * 2 + u), u)
                    for u in range(2):
                        dve.wait_ge(nm.rstd_ready, i * 2 + u + 1)
                        norm_apply(dve, nm, u, i * 2 + u)

            norm_loop(nE)
            stage_end(dve, 6)
            dve.sem_inc(add_done, 2)
            dve.sem_inc(pb_free, 2)
            E0, E1 = K // 2, L - K // 2

            def per_head(x):
                return x.rearrange("p j (h o) -> p j h o", o=1).to_broadcast([L, CB, HEADS, K])

            def windowed(u, o, other, k, op_out):
                q3 = other.rearrange("p (j l) -> p j l", j=CB)
                k3 = qkv[:, u, k].rearrange("p (j l) -> p j l", j=CB)
                o3 = op_out.rearrange("p (j l) -> p j l", j=CB)
                yield o3[:, :, E0:E1], q3[:, :, E0:E1], k3[:, :, o:o + E1 - E0]
                for lo, at_k in ((0, o), (E1, L - K + o)):
                    yield (o3[:, :, lo:lo + E0], q3[:, :, lo:lo + E0],
                           k3[:, :, at_k:at_k + 1].to_broadcast([128, CB, E0]))

            PER_E = 2 * (1 + 2 + K - 1 + 1)
            for i in step.loop(NP, PER_E):
                for u in range(2):
                    c = i * 2 + u
                    dve.wait_ge(qkv_ready, c * 3 + 3)
                    for o in range(K):
                        for dst, a, b in windowed(u, o, qkv[:, u, 0], 1, prod[:, u, o]):
                            ins = dve.tensor_tensor(dst, a, b, ALU.mult)
                        ins.then_inc(prod_r, 1)
                for u in range(2):
                    c = i * 2 + u
                    dve.wait_ge(ST_ready, c + 1)
                    s4 = psum[0:L, 5, 0:CB * OH].rearrange("p (j o h) -> p j h o", j=CB, o=K)
                    p4 = P_tm[:, u].rearrange("p j (o h) -> p j h o", o=K)
                    step.add(dve.tensor_reduce(mx[:, u], s4, AX, ALU.max))
                    step.wait()
                    dve.tensor_tensor(p4, s4, per_head(mx[:, u]), ALU.subtract).then_inc(sub_done, 1)
                for u in range(2):
                    c = i * 2 + u
                    p4 = P_tm[:, u].rearrange("p j (o h) -> p j h o", o=K)
                    dve.wait_ge(exp_done, c + 1)
                    step.add(dve.tensor_reduce(sm[:, u], p4, AX, ALU.add))
                    step.wait()
                    step.add(dve.reciprocal(sm[:, u], sm[:, u]))
                    step.wait()
                    dve.tensor_tensor(p4, p4, per_head(sm[:, u]), ALU.mult).then_inc(P_ready, 1)
                for u in range(2):
                    c = i * 2 + u
                    for o in range(K):
                        dve.wait_ge(pb_mm, c * K + o + 1)
                        dst_t = pv[:, u] if o == 0 else pv_t[:, o % 2]
                        for dst, a, b in windowed(u, o, bank(6 + (u + o) % 2), 2, dst_t):
                            ins = dve.tensor_tensor(dst, a, b, ALU.mult)
                        ins.then_inc(pb_free, 1)
                        if o:
                            dve.wait_ge(pb_free, 2 + c * K + o + 1)
                            ins = step.add(dve.tensor_tensor(pv[:, u], pv[:, u], pv_t[:, o % 2], ALU.add))
                            step.wait()
                    dve.sem_inc(pv_ready, 1)
                for u in range(2):
                    c = i * 2 + u
                    dve.wait_ge(proj_mm, c + 1)
                    step.add(dve.tensor_tensor(at_tmp, bank_tm(3 + u), row(2), ALU.add))
                    step.wait()
                    dve.tensor_tensor(seqs(H, c), seqs(H, c), at_tmp, ALU.add).then_inc(add_done, 1)
                    dve.wait_ge(add_done, 2 + c + 1)
            stage_end(dve, 7)

            norm_loop(nF)
            stage_end(dve, 8)
            x3 = xfm[:, :].rearrange("p (b l) -> p b l", b=B)
            dve.tensor_reduce(srep, x3, AX, ALU.add).then_inc(rt_dve, 1)
            dve.wait_ge(rt_pe, 1)
            N = slice(0, NPART)
            zz = [z[:, k, N] for k in range(8)]
            s1 = [zs[:, k:k + 1] for k in range(8)]

            def ts(o, a, x, y, p, q=None):
                if q is None:
                    step.add(dve.tensor_scalar(o, a, x, None, p))
                else:
                    step.add(dve.tensor_scalar(o, a, x, y, p, q))
                step.wait()

            def red(o, a, op):
                step.add(dve.tensor_reduce(o, a, AX, op))
                step.wait()

            ts(zz[0], psum[0:B, 0, N], 1.0 / L, None, ALU.mult)
            red(s1[0], zz[0], ALU.max)
            dve.tensor_scalar(zz[0], zz[0], s1[0], None, ALU.subtract).then_inc(rt_act, 1)
            dve.wait_ge(rt_act, 2)
            red(s1[1], zz[1], ALU.add)
            step.add(dve.reciprocal(s1[1], s1[1]))
            step.wait()
            ts(zz[1], zz[1], s1[1], None, ALU.mult)

            def first_largest(p, m, one):
                red(m, p, ALU.max)
                ts(zz[7], p, m, None, ALU.is_equal)
                tt(zz[7], zz[7], prio[0:B, N], ALU.mult)
                red(s1[7], zz[7], ALU.max)
                ts(one, zz[7], s1[7], None, ALU.is_equal)

            first_largest(zz[1], s1[2], zz[2])
            step.add(dve.scalar_tensor_tensor(zz[3], zz[2], -2.0, zz[1], ALU.mult, ALU.add))
            step.wait()
            first_largest(zz[3], s1[3], zz[4])
            tt(s1[4], s1[2], s1[3], ALU.add)
            step.add(dve.reciprocal(s1[4], s1[4]))
            step.wait()
            ts(zz[2], zz[2], s1[2], s1[4], ALU.mult, ALU.mult)
            ts(zz[4], zz[4], s1[3], s1[4], ALU.mult, ALU.mult)
            dve.tensor_tensor(zz[5], zz[2], zz[4], ALU.add).then_inc(rt_dve, 1)
            dve.wait_ge(rt_pe, 2)
            dve.tensor_copy(wcT, psum[0:NPART, 1, 0:B]).then_inc(rt_dve, 1)
            dve.wait_ge(rt_pe, 3)
            step.add(dve.tensor_copy(ew, psum[:, 2, 0:NE * B].rearrange("p (e b) -> p e b", e=NE)))
            step.add(dve.tensor_copy(ewT, psum[0:NE, 3, 0:B]))
            step.wait()
            step.add(dve.scalar_tensor_tensor(ew, ew, 1e-6, ew, ALU.is_gt, ALU.mult))
            step.add(dve.scalar_tensor_tensor(ewT, ewT, 1e-6, ewT, ALU.is_gt, ALU.mult))
            step.wait()
            dve.sem_inc(rt_dve, 1)
            dve.wait_ge(rt_pe, 4)
            step.add(dve.tensor_copy(bb, psum[:, 4, 0:B]))
            step.wait()
            dve.sem_inc(fo_free, 2)
            dve.sem_inc(out_ready, 2)
            for u in range(2):
                dve.sem_inc(out_done[u], 16)
            for i in step.loop(NP, 2 * (NE * CB)):
                for u in range(2):
                    c = i * 2 + u
                    dve.wait_ge(fT_ready, c + 1)
                    for e in range(NE):
                        dve.wait_ge(fo_mm, c * NE + e + 3)
                        for j in range(CB):
                            a = facc[:, u, j * L:(j + 1) * L]
                            p = psum[:, 4 + e % 2, j * L:(j + 1) * L]
                            we = ew[:, e, bass.ds(c * CB + j, 1)]
                            if e == 0:
                                ins = dve.tensor_scalar(a, p, we, bb[:, bass.ds(c * CB + j, 1)], ALU.mult, ALU.add)
                            else:
                                ins = dve.scalar_tensor_tensor(a, p, we, a, ALU.mult, ALU.add)
                            step.add(ins)
                        step.wait()
                        dve.sem_inc(fo_free, 1)
                    dve.sem_inc(facc_ready, 1)
                for u in range(2):
                    c = i * 2 + u
                    dve.wait_ge(fT_ready, c + 3)
                    dve.wait_ge(out_done[u], 16 * (i + 1))
                    dve.tensor_tensor(fo[:, u], bank_tm(6 + u), seqs(H, c), ALU.add).then_inc(out_ready, 1)

        @block.tensor
        def _(pe):
            pe.wait_ge(wload, N_PREP)
            pe.matmul(psum[0:64, 7, 0:D], wprep[0:64, 4, 0:64], wprep[0:64, 5, :], start=True, stop=True)\
                .then_inc(prep_mm, 1)
            pe.wait_ge(prep_cp, 1)
            pe.matmul(psum[:, 7, 0:D], wprep[0:64, 3, :], MR[:, :], start=True, stop=True)
            pe.matmul(psum[:, 7, D:D + 1], MR[:, :], keyb[:, :], start=True, stop=True).then_inc(prep_mm, 1)

            pe.sem_inc(y_mm, 2)
            pe.sem_inc(yT_ready, 2)
            pe.sem_inc(nA.xT_ready, 4)
            pe.sem_inc(yT_free, 2)

            def embed(i):
                for u in range(2):
                    c = i * 2 + u
                    pe.wait_ge(xg_ready[u], 16 * (i + 1))
                    pe.wait_ge(y_fm_ready, c + 1)
                    x4 = xg[:, u].rearrange("p j (b g) -> p j b g", b=CB)
                    for n in range(8):
                        j, h = n // 2, n % 2
                        ins = pe.matmul(bank(u).rearrange("p (b l) -> p b l", b=CB), w_emb[:, j, h, :],
                                        x4[:, j, :, h:h + L], start=(n == 0), stop=(n == 7))
                    ins.then_inc(y_mm, 1)

            def to_tm(i):
                for u in range(2):
                    c = i * 2 + u
                    pe.wait_ge(y_fm_ready, c + 3)
                    pe.wait_ge(yT_free, c + 1)
                    for j in range(CB):
                        ins = pe.transpose(bank_tm(2 + u)[:, j, :], y_fm[:, u, j * L:(j + 1) * L], ident[:, :])
                    ins.then_inc(yT_ready, 1)

            def to_fm(nm, i, banks):
                for u in range(2):
                    norm_transposes(pe, nm, u, i * 2 + u, banks)

            embed(0)
            to_tm(0)
            with pe.Fori(1, NP) as i:
                embed(i)
                to_fm(nA, i - 1, (4, 5))
                to_tm(i)
            to_fm(nA, NP - 1, (4, 5))
            stage_end(pe, 1)

            pe.sem_inc(delta_mm, 2)
            with pe.Fori(0, NP) as i:
                for u in range(2):
                    c = i * 2 + u
                    pe.matmul(bank(u), wprep[:, 1, :], fm(xnfm, c), start=True, stop=True).then_inc(delta_mm, 1)
                    pe.wait_ge(delta_act, c + 1)
            stage_end(pe, 2)

            for s, (a, w) in enumerate(SEG):
                pe.matmul(psum[:, s, 0:w], w_D[:, :], xfm[:, a:a + w], start=True, stop=False, skip_group_check=True)
            pe.sem_inc(C_free, 2)

            def states(n, u, k):
                for s, (a, w) in enumerate(SEG):
                    pe.wait_ge(bc_free, n * 2 * NSEG + k * NSEG + s + 1)
                    o = psum[:, 6 + s % 2, 0:w]
                    pe.matmul(o, w_hi[:, u, k, :], xn_lo[:, a:a + w], start=True, stop=False)
                    pe.matmul(o, w_lo[:, u, k, :], xn_hi[:, a:a + w], start=False, stop=False)
                    pe.matmul(o, w_hi[:, u, k, :], xn_hi[:, a:a + w], start=False, stop=True).then_inc(bc_mm, 1)

            def add_state(n, u, last=False):
                pe.wait_ge(prod_ready, n + 1)
                for s, (a, w) in enumerate(SEG):
                    ins = pe.matmul(psum[:, s, 0:w], ident[:, :], bufC[:, u, a:a + w], start=False, stop=last,
                                    skip_group_check=True)
                ins.then_inc(C_free, 1)

            def state_pair(i, first=False):
                if not first:
                    add_state(i * 2 - 2, 0)
                    add_state(i * 2 - 1, 1)
                for u in range(2):
                    pe.wait_ge(w_split, 2 + i * 2 + u + 1)
                    states(i * 2 + u, u, 0)
                    states(i * 2 + u, u, 1)

            state_pair(0, True)
            with pe.Fori(1, NS // 2) as i:
                state_pair(i)
            add_state(NS - 2, 0)
            add_state(NS - 1, 1, True)
            pe.drain().then_inc(acc_done, 1)
            stage_end(pe, 3)

            pe.sem_inc(cT_ready, 2)
            pe.sem_inc(nC.xT_ready, 4)
            with pe.Fori(0, NP) as i:
                for u in range(2):
                    c = i * 2 + u
                    pe.wait_ge(hm_free, c + 1)
                    pe.wait_ge(lg_free, c + 1)
                    pe.matmul(bank(u), w_mem[:, :], fm(Y, c), start=True, stop=True)
                    pe.matmul(bank(2 + u), wprep[:, 2, :], fm(Y, c), start=True, stop=True).then_inc(hm_mm, 1)
                for u in range(2):
                    c = i * 2 + u
                    pe.wait_ge(cF_ready, c + 1)
                    pe.wait_ge(cT_free, c + 1)
                    for j in range(CB):
                        ins = pe.transpose(bank_tm(4 + u)[:, j, :], cF[:, u, j * L:(j + 1) * L], ident[:, :])
                    ins.then_inc(cT_ready, 1)
                to_fm(nC, i, (6, 7))
                for u in range(2):
                    c = i * 2 + u
                    pe.wait_ge(nC.xT_free, 2 + 2 * c + 2)
                    pe.wait_ge(sig_ready, c + 1)
                    pe.matmul(bank(2 + u, NE), smallw[:, 0:NE], fm(xfm, c), start=True, stop=True).then_inc(lgF_mm, 1)
                for u in range(2):
                    c = i * 2 + u
                    wait_apart(pe, lgF_ready, c + 1)
                    for j in range(CB):
                        ins = pe.transpose(psum[0:L, 2 + u, j * NE:(j + 1) * NE], lgF[:, u, j * L:(j + 1) * L],
                                           ident[0:NE, 0:NE])
                    ins.then_inc(lgT_ready, 1)
            stage_end(pe, 4)

            pe.wait_ge(w12_ready, 32)
            pe.sem_inc(o_mm, 2)
            with pe.Fori(0, NCH) as c:
                for e in range(NE):
                    for j in range(HT):
                        pe.wait_ge(h_free, (c * NE + e) * HT + j + 1)
                        pe.matmul(bank(j), w1[:, e, j * D:(j + 1) * D], fm(xnfm, c), start=True, stop=True)\
                            .then_inc(h_mm, 1)
                    pe.wait_ge(o_free, c * NE + e + 1)
                    pe.wait_ge(h_free, HT + (c * NE + e) * HT + HT)
                    for b in range(CB):
                        for j in range(HT):
                            ins = pe.matmul(bank_tm(4 + e % 2)[:, b, :], hid[:, e % 2, j, b * L:(b + 1) * L],
                                            w2[:, e, j, :], start=(j == 0), stop=(j == HT - 1))
                    ins.then_inc(o_mm, 1)
            stage_end(pe, 5)

            pe.sem_inc(nE.xT_ready, 2)
            with pe.Fori(0, NP) as i:
                to_fm(nE, i, (6, 7))
            stage_end(pe, 6)
            pe.wait_ge(wE_ready, 6 * 16)
            with pe.Fori(0, NP) as i:
                for u in range(2):
                    c = i * 2 + u
                    for k in range(3):
                        if u:
                            pe.wait_ge(qkv_ready, (c - 1) * 3 + k + 1)
                        pe.matmul(bank(k), w_qkv[:, k, :], fm(xfm, c), start=True, stop=True).then_inc(qkv_mm, 1)
                for u in range(2):
                    c = i * 2 + u
                    pe.wait_ge(add_done, c + 1)
                    for o in range(K):
                        pe.wait_ge(prod_r, c * K + o + 1)
                        pe.matmul(bank(3 + u, OH), sel[:, o, :], prod[:, u, o], start=(o == 0), stop=False)
                    pe.matmul(bank(3 + u, OH), rpb_w, posc, start=False, stop=True).then_inc(S_mm, 1)
                for u in range(2):
                    c = i * 2 + u
                    pe.wait_ge(S_ready, c + 1)
                    if u:
                        pe.wait_ge(sub_done, c)
                    for j in range(CB):
                        ins = pe.transpose(psum[0:L, 5, j * OH:(j + 1) * OH], S_fm[:, u, j * L:(j + 1) * L],
                                           ident[0:OH, 0:OH])
                    ins.then_inc(ST_ready, 1)
                for u in range(2):
                    c = i * 2 + u
                    pe.wait_ge(P_ready, c + 1)
                    for j in range(CB):
                        ins = pe.transpose(psum[0:OH, 3 + u, j * L:(j + 1) * L], P_tm[:, u, j], ident[0:L, 0:L])
                    ins.then_inc(PT_ready, 1)
                for u in range(2):
                    c = i * 2 + u
                    pe.wait_ge(P_fm_ready, c + 1)
                    for o in range(K):
                        pe.wait_ge(pb_free, c * K + o + 1)
                        pe.matmul(bank(6 + (u + o) % 2), spread[:, o, :], P_fm[:, u], start=True, stop=True)\
                            .then_inc(pb_mm, 1)
                for u in range(2):
                    c = i * 2 + u
                    pe.wait_ge(pv_ready, c + 1)
                    for j in range(CB):
                        ins = pe.matmul(bank_tm(3 + u)[:, j, :], pv[:, u, j * L:(j + 1) * L], w_proj,
                                        start=True, stop=True)
                    ins.then_inc(proj_mm, 1)
            stage_end(pe, 7)

            pe.sem_inc(nF.xT_ready, 2)
            with pe.Fori(0, NP) as i:
                to_fm(nF, i, (6, 7))
            stage_end(pe, 8)
            pe.wait_ge(wF_ready, 7 * 16)
            pe.wait_ge(rt_dve, 1)
            pe.matmul(psum[0:B, 0, 0:NPART], srep, smallw[:, NE:NE + NPART], start=True, stop=True).then_inc(rt_pe, 1)
            pe.wait_ge(rt_dve, 2)
            pe.transpose(psum[0:NPART, 1, 0:B], z[:, 5, 0:NPART], ident[0:B, 0:B]).then_inc(rt_pe, 1)
            pe.wait_ge(rt_dve, 3)
            for e in range(NE):
                pe.matmul(psum[:, 2, e * B:(e + 1) * B], pwb[:, e, :], wcT, start=True, stop=True)
            pe.matmul(psum[0:NE, 3, 0:B], pw, wcT, start=True, stop=True).then_inc(rt_pe, 1)
            pe.wait_ge(rt_dve, 4)
            pe.matmul(psum[:, 4, 0:B], b2, ewT, start=True, stop=True).then_inc(rt_pe, 1)
            pe.sem_inc(fo_mm, 2)
            pe.sem_inc(fT_ready, 2)
            with pe.Fori(0, NP) as i:
                for u in range(2):
                    c = i * 2 + u
                    for e in range(NE):
                        for j in range(FT):
                            kk = D if j < 2 else FR
                            pe.wait_ge(f_free, (c * NE + e) * FT + j + 1)
                            pe.matmul(bank(j, kk), v1[:, e, j * D:j * D + kk], fm(xfm, c), start=True, stop=True)\
                                .then_inc(f_mm, 1)
                        pe.wait_ge(fo_free, c * NE + e + 1)
                        pe.wait_ge(f_free, FT + (c * NE + e) * FT + FT)
                        for j in range(FT):
                            kk = D if j < 2 else FR
                            w = v2[:, e, j, :] if j < 2 else v2b[:, e, :]
                            ins = pe.matmul(bank(4 + e % 2), w, fh[0:kk, e % 2, j], start=(j == 0), stop=(j == FT - 1))
                        ins.then_inc(fo_mm, 1)
                for u in range(2):
                    c = i * 2 + u
                    pe.wait_ge(facc_ready, c + 1)
                    pe.wait_ge(out_ready, c + 1)
                    for j in range(CB):
                        ins = pe.transpose(bank_tm(6 + u)[:, j, :], facc[:, u, j * L:(j + 1) * L], ident[:, :])
                    ins.then_inc(fT_ready, 1)


def kernel(**inp):
    import numpy as np
    import concourse.bacc as bacc
    from concourse.bass_utils import run_bass_kernel_spmd

    a = {k: np.asarray(v) for k, v in inp.items()}
    B, S, C = a["x"].shape
    L = (S - 16) // 8 + 1
    G, D, CB, NS, NE, K, HEADS = L + 1, 128, 4, 16, 6, 7, 16
    f = np.float32

    def c_(x):
        return np.ascontiguousarray(x)

    t = {}
    x = a["x"][:, :G * 8].reshape(B // CB, CB, G, 512).transpose(0, 3, 1, 2)
    t["xg"] = c_(x.reshape(B // CB, 4, 128, CB * G).transpose(0, 2, 1, 3))
    w = a["L0_tok_W"].reshape(C, 2, 8, D).transpose(2, 0, 1, 3).reshape(4, 128, 2, D)
    t["w_emb"] = c_(w.transpose(1, 0, 2, 3))
    one = lambda k: a[k].reshape(D, 1)
    b1 = a["L1_ffn_b1"]
    t["cols"] = c_(np.concatenate([
        one("L0_tok_b"), one("L0_attn_ln_gamma"), one("L0_attn_ln_beta"), one("L0_attn_D_b"),
        one("L0_attn_D_scale"), one("L0_attn_recall_b"), one("L0_ffn_gamma"),
        a["L1_attn_qkv_b"].reshape(3, D).T, a["L0_attn_A_log"], a["L0_attn_B_b"].reshape(D, NS),
        a["L0_attn_C_b"].reshape(D, NS), b1[:, :2 * D].reshape(NE * 2, D).T,
        np.broadcast_to(a["L0_attn_delta_b"].reshape(1, 1), (D, 1)),
        np.broadcast_to(a["L0_attn_gate_b"].reshape(1, 1), (D, 1))], axis=1))
    t["rows"] = c_(np.broadcast_to(np.stack([a["L0_tok_gamma"], a["L0_tok_beta"], a["L1_attn_proj_b"],
                                             a["L0_attn_D_scale"]])[None], (128, 4, D)))
    t["ident"] = np.eye(128, dtype=f)
    t["w_full"] = c_(np.stack([a["L0_attn_D_W"], np.broadcast_to(a["L0_attn_delta_W"], (D, D)),
                               np.broadcast_to(a["L0_attn_gate_W"], (D, D))], axis=1))
    t["key_WT"] = c_(a["L0_attn_key_W"].T)
    t["M_T"] = c_(a["L0_attn_M"].T)
    t["recall_W"] = a["L0_attn_recall_W"]
    t["key_b"] = a["L0_attn_key_b"].reshape(64, 1)
    t["smallw"] = c_(np.concatenate([a["L0_ffn_w_gating"], a["L1_ffn_router_w"].T], axis=1))
    t["prio"] = c_(np.broadcast_to(np.arange(16, 0, -1).astype(f)[None], (128, 16)))
    bw = a["L0_attn_B_W"].reshape(D, D, NS).transpose(2, 0, 1)
    cw = a["L0_attn_C_W"].reshape(D, D, NS).transpose(2, 0, 1)
    t["wBC"] = c_(np.stack([bw, cw], axis=2))
    t["w1"] = c_(a["L0_ffn_w1"].transpose(1, 0, 2))
    t["w2"] = c_(a["L0_ffn_w2"].reshape(NE, 4, D, D).transpose(2, 0, 1, 3))
    t["w_qkv"] = c_(a["L1_attn_qkv_w"].reshape(3, D, D).transpose(2, 0, 1))
    t["w_proj"] = c_(a["L1_attn_proj_w"].T)
    head = np.arange(D) // (D // HEADS)
    sel = np.zeros((D, K, K * HEADS), f)
    for o in range(K):
        sel[np.arange(D), o, o * HEADS + head] = 1
    t["sel"] = sel
    t["spread"] = c_(sel.transpose(2, 1, 0))
    t["rpb_w"] = c_(np.stack([a["L1_attn_rpb"][:, c:c + K].T.reshape(-1) for c in range(K)]))
    pos = np.arange(L)
    first = np.clip(pos - K // 2, 0, L - K) - pos + K - 1
    t["posc"] = c_(np.tile((first[None] == np.arange(K)[:, None]).astype(f), (1, CB)))
    v = a["L1_ffn_W1"]
    t["v1"] = c_(v.transpose(1, 0, 2))
    t["v2"] = c_(a["L1_ffn_W2"][:, :2 * D].reshape(NE, 2, D, D).transpose(2, 0, 1, 3))
    t["v2b"] = c_(a["L1_ffn_W2"][:, 2 * D:].transpose(1, 0, 2))
    t["b1b"] = c_(b1[:, 2 * D:].T)
    t["b2"] = a["L1_ffn_b2"]
    parts = [(6,), (5, 1), (4, 2), (4, 1, 1), (3, 3), (3, 2, 1), (3, 1, 1, 1), (2, 2, 2), (2, 2, 1, 1),
             (2, 1, 1, 1, 1), (1, 1, 1, 1, 1, 1)]
    pw = np.zeros((11, NE), f)
    for i, p in enumerate(parts):
        for j, q in enumerate(p):
            pw[i, j] = q / 6
    t["pw"] = pw
    t["pwb"] = c_(np.broadcast_to(pw[:, :, None], (11, NE, D)))

    nc = bacc.Bacc("TRN2", target_bir_lowering=False, num_devices=1)
    f32 = mybir.dt.float32
    aps = {k: nc.dram_tensor("in_" + k, v.shape, f32, kind="ExternalInput").ap() for k, v in t.items()}
    out = nc.dram_tensor("out_0", (B, L, D), f32, kind="ExternalOutput").ap()
    audio_tower(nc, aps, out)
    r = run_bass_kernel_spmd(nc, [{"in_" + k: v for k, v in t.items()}], core_ids=[0])
    return r.results[0]["out_0"]
```

```python
from contextlib import ExitStack

import concourse.bass as bass
from concourse import mybir


def audio_tower(nc, t, out):
    f32 = mybir.dt.float32
    f32r = mybir.dt.float32r
    ALU = mybir.AluOpType
    ACT = mybir.ActivationFunctionType
    AX = mybir.AxisListType.X

    B, L, D = out.shape
    CB = 4
    NCH = B // CB
    NP = NCH // 2
    CT = CB * L
    TOK = B * L
    G = L + 1
    NS = 16
    NE = 6
    HID = 512
    HT = HID // D
    FF = 341
    FT = 3
    FR = FF - 2 * D
    K = 7
    HEADS = 16
    OH = K * HEADS
    NPART = 11
    TS = 128
    NTILE = (TOK + NE * (TS - 1)) // TS
    NTILE += NTILE % 2
    NTHR = -(-TOK // TS)
    SCALE = float(D // HEADS) ** -0.5
    EPS = 1e-5
    SEG = [(s, min(512, TOK - s)) for s in range(0, TOK, 512)]
    NSEG = len(SEG)

    names = [("tok_b", 1), ("ln_gamma", 1), ("ln_beta", 1), ("D_b", 1), ("D_scale", 1),
             ("recall_b", 1), ("ffn_gamma", 1), ("qkv_b", 3), ("A_log", NS), ("B_b", NS),
             ("C_b", NS), ("b1", 2 * NE), ("delta_b", 1), ("gate_b", 1)]
    at, NCOL = {}, 0
    for name, n in names:
        at[name] = NCOL
        NCOL += n

    ctx = ExitStack()
    with ctx:
        def sb(name, shape, dt=f32):
            return ctx.enter_context(nc.sbuf_tensor("s_" + name, shape, dt))

        def sem(name):
            return ctx.enter_context(nc.semaphore(name))

        xfm = sb("xfm", [128, TOK])
        xnfm = sb("xnfm", [128, TOK])
        H = sb("H", [L, B, D])
        cols = sb("cols", [128, NCOL])
        rows = sb("rows", [128, 4, D])
        ident = sb("ident", [128, 128])
        wprep = sb("wprep", [128, 6, 128])
        w_D = sb("w_D", [128, 128])
        w_mem = sb("w_mem", [128, 128])
        MR = sb("MR", [64, 128])
        keyb = sb("keyb", [64, 1])
        mem_b = sb("mem_b", [128, 1])
        stat = sb("stat", [L, 2, CB, 6])
        mv = sb("mv", [L, 2, CB, 2])
        rstd = sb("rstd", [L, 2, CB])
        rstd2 = sb("rstd2", [L, 2, CB])
        pa = sb("pa", [L, 2, CB])
        mhalf = sb("mhalf", [L, CB])
        xs = sb("xs", [L, 2, 2, CB, D])
        smallw = sb("smallw", [128, 32])
        A_pos = sb("A_pos", [128, NS])
        A_inj = sb("A_inj", [128, NS])
        A_half = sb("A_half", [128, NS])
        A_neg = sb("A_neg", [128, NS])
        A_c = sb("A_c", [128, NS])
        gate = sb("gate", [L, B])
        slot = sb("slot", [L, B], mybir.dt.uint32)
        R_COLS = 10 * TOK + 1
        R = sb("R", [128, R_COLS])
        psum = ctx.enter_context(nc.psum_tensor("psum", [128, 8, 512], f32))
        x_sorted = nc.dram_tensor("x_sorted", (NTILE * TS, D), f32, kind="Internal").ap()
        y_sorted = nc.dram_tensor("y_sorted", (NTILE * TS, D), f32, kind="Internal").ap()

        taken = [0]

        def fresh():
            taken[0] = 0

        def take(*shape, parts=128):
            n = 1
            for s in shape:
                n *= s
            view = R[0:parts, taken[0]:taken[0] + n]
            taken[0] += n
            assert taken[0] <= R_COLS
            if len(shape) > 1:
                ax = "abcd"[:len(shape)]
                view = view.rearrange("p (" + " ".join(ax) + ") -> p " + " ".join(ax),
                                      **{x: s for x, s in zip(ax, shape)})
            return view

        def bank(b, parts=128, n=CT):
            return psum[0:parts, b, 0:n]

        def bank_tm(b):
            return psum[0:L, b, 0:CB * D].rearrange("p (j d) -> p j d", j=CB)

        wload = sem("wload")
        stage_done = sem("stage_done")
        apart = sem("apart")
        prep_mm, prep_cp = sem("prep_mm"), sem("prep_cp")
        prep_act = sem("prep_act")
        dve_step = sem("dve_step")
        pool_step = sem("pool_step")

        N_PREP = 11 * 16

        def wait_apart(eng, s, value):
            eng.wait_ge(s, value)
            eng.sem_inc(apart, 1)

        class Tally:

            def __init__(self, eng, s):
                self.eng, self.sem, self.base, self.n = eng, s, 0, 0

            def add(self, ins):
                self.n += 1
                return ins.then_inc(self.sem, 1)

            def wait(self, apart=False):
                (wait_apart(self.eng, self.sem, self.base + self.n) if apart
                 else self.eng.wait_ge(self.sem, self.base + self.n))

            def loop(self, trips, per):
                start = self.base + self.n
                with self.eng.Fori(0, trips) as i:
                    self.base, self.n = start + i * per, 0
                    yield i
                    assert self.n == per, (self.n, per)
                self.base, self.n = start + trips * per, 0

        def stage_end(eng, k):
            eng.drain().then_inc(stage_done, 1)
            eng.wait_ge(stage_done, 4 * k)

        def fm(tile, c):
            return tile[:, bass.ds(c * CT, CT)]

        def col(name, k=0):
            return cols[:, at[name] + k:at[name] + k + 1]

        class Norm:
            def __init__(self, tag, n):
                self.n = n
                self.var_ready = sem(tag + "_var_ready")
                self.rstd_ready = sem(tag + "_rstd_ready")
                self.xs_ready = sem(tag + "_xs_ready")
                self.xT_ready = sem(tag + "_xT_ready")
                self.xT_free = sem(tag + "_xT_free")

        def norm_stats(dve, nm, step, src, u):
            for j in range(CB):
                step.add(dve.bn_stats(stat[:, u, j, :], src[:, j, :]))
            step.wait(True)
            for j in range(CB):
                ins = dve.bn_aggr(mv[:, u, j, :], stat[:, u, j, :])
            ins.then_inc(nm.var_ready, 1)

        def norm_pool(pool, nm, step, u, ready, two):
            step.add(pool.tensor_scalar(pa[:, u, :], mv[:, u, :, 1], 1.0, EPS, ALU.mult, ALU.add))
            step.wait()
            last = pool.tensor_tensor(rstd[:, u, :], pa[:, u, :], mhalf[:, :], ALU.pow)
            if two:
                step.add(last)
                step.wait()
                step.add(pool.tensor_tensor(pa[:, u, :], rstd[:, u, :], rstd[:, u, :], ALU.mult))
                step.wait()
                step.add(pool.tensor_tensor(pa[:, u, :], pa[:, u, :], mv[:, u, :, 1], ALU.mult))
                step.wait(True)
                step.add(pool.tensor_scalar(pa[:, u, :], pa[:, u, :], 1.0, EPS, ALU.mult, ALU.add))
                step.wait()
                step.add(pool.tensor_tensor(pa[:, u, :], pa[:, u, :], mhalf[:, :], ALU.pow))
                step.wait()
                last = pool.tensor_tensor(rstd2[:, u, :], pa[:, u, :], rstd[:, u, :], ALU.mult)
            last.then_inc(ready, 1)

        def norm_apply(dve, nm, u, c, keep=None):
            dve.wait_ge(nm.xT_ready, nm.n * (c + 1))
            for w, r in ((0, rstd), (1, rstd2))[:2 if keep is not None else nm.n]:
                for j in range(CB):
                    dst = xs[:, u, w, j, :]
                    if w and keep is not None:
                        dst = keep[:, bass.ds(c * CB + j, 1), :].rearrange("p a d -> p (a d)")
                    ins = dve.tensor_scalar(dst, H[:, bass.ds(c * CB + j, 1), :].rearrange("p a d -> p (a d)"),
                                            mv[:, u, j, 0:1], r[:, u, j:j + 1], ALU.subtract, ALU.mult)
            ins.then_inc(nm.xs_ready, 1)

        def norm_transposes(pe, nm, u, c, banks):
            pe.wait_ge(nm.xs_ready, c + 1)
            for w in range(nm.n):
                pe.wait_ge(nm.xT_free, nm.n * c + w + 1)
                b = banks[w if nm.n == 2 else u]
                for j in range(CB):
                    ins = pe.transpose(psum[:, b, j * L:(j + 1) * L], xs[:, u, w, j, :], ident[0:L, 0:L])
                ins.then_inc(nm.xT_ready, 1)

        def norm_copies(act, nm, u, c, banks, scale=None, bias=None):
            for w in range(nm.n):
                wait_apart(act, nm.xT_ready, 2 * nm.n + nm.n * c + w + 1)
                b = banks[w if nm.n == 2 else u]
                if w == 0:
                    ins = act.activation(fm(xfm, c), bank(b), ACT.Copy)
                else:
                    ins = act.activation(fm(xnfm, c), bank(b), ACT.Identity, scale=scale,
                                         bias=0.0 if bias is None else bias)
                ins.then_inc(nm.xT_free, 1)

        fresh()
        w_emb = take(4, 2, D)
        xg = take(2, 4, CB * G)
        y_fm = take(2, CT)
        yn = take(2, CB, D, parts=L)
        zeros = take(NTILE * D)
        zeros_ready, fill_done = sem("zeros_ready"), sem("fill_done")
        nA = Norm("a", 2)
        nA0 = sem("a_var0_ready"), sem("a_rstd0_ready")
        xg_ready = [sem("xg_ready0"), sem("xg_ready1")]
        y_mm = sem("y_mm")
        y_fm_ready = sem("y_fm_ready")
        yT_ready = sem("yT_ready")
        yT_free = sem("yT_free")

        fresh()
        dl = take(1 + TOK)
        bufB = take(2, TOK)
        bufC = take(2, TOK)
        th = take(2, TOK)
        ea = take(TOK)
        ra = take(2, TOK)
        wBC = sb("wBC", [128, 2, 2, D])
        w_hi = sb("w_hi", [128, 2, 2, D], f32r)
        w_lo = sb("w_lo", [128, 2, 2, D], f32r)
        xn_hi = sb("xn_hi", [128, TOK], f32r)
        xn_lo = sb("xn_lo", [128, TOK], f32r)
        w_hi_ready, w_split, x_split = sem("w_hi_ready"), sem("w_split"), sem("x_split")
        part = sb("part", [128, 2, NSEG])
        mean = sb("mean", [128, 2])
        skip_b = sb("skip_b", [128, 1])
        delta_mm, delta_act = sem("delta_mm"), sem("delta_act")
        wBC_ready = [sem("wBC_ready0"), sem("wBC_ready1")]
        bc_mm = sem("bc_mm")
        bc_free = sem("bc_free")
        C_ready = sem("C_ready")
        th_ready, ea_ready, ra_ready = sem("th_ready"), sem("ea_ready"), sem("ra_ready")
        th_free, ea_free, ra_free = sem("th_free"), sem("ea_free"), sem("ra_free")
        B_free = sem("B_free")
        prod_ready = sem("prod_ready")
        C_free = sem("C_free")
        acc_done = sem("acc_done")

        fresh()
        Y = take(TOK)
        sig = take(2, CT)
        cF = take(2, CT)
        lgF = take(2, CT, parts=NE)
        lg = take(B, NE, parts=L)
        nC = Norm("c", 1)
        Y_ready = sem("Y_ready")
        hm_mm = sem("hm_mm")
        sig_ready = sem("sig_ready")
        hm_free = sem("hm_free")
        cF_ready = sem("cF_ready")
        cT_ready = sem("cT_ready")
        cT_free = sem("cT_free")
        lgF_mm, lgF_ready, lgT_ready, lg_free = sem("lgF_mm"), sem("lgF_ready"), sem("lgT_ready"), sem("lg_free")
        ex = take(B, NE, parts=L)
        oh = take(B, NE, parts=L)
        cand = take(B, NE, parts=L)
        r1 = take(B, parts=L)
        r2 = take(B, parts=L)
        r3 = take(B, parts=L)
        r4 = take(B, parts=L)
        prio = sb("prio", [128, 16])
        rt_a, rt_b = sem("rt_a"), sem("rt_b")
        ohE = take(NE, B, parts=L)
        cum = take(NE, B, parts=L)
        rest = take(NE, B, parts=L)
        before = take(L, parts=L)
        ones = take(L, parts=L)
        thr = take(NTHR, parts=L)
        tile_no = take(NTILE, parts=L)
        row_n = take(NE, parts=L)
        over = take(NE, NTHR, parts=L)
        n_tiles = take(NE, parts=L)
        start = take(NE, parts=L)
        base = take(NE, parts=L)
        t_cmp = take(NTILE, NE - 1, parts=L)
        t_exp = take(NTILE, parts=L)
        tile_e = sb("tile_e", [L, NTILE], mybir.dt.int32)
        cnt_mm, cnt_dve, slot_ready = sem("cnt_mm"), sem("cnt_dve"), sem("slot_ready")
        w1 = take(NE, HID)
        w2 = take(NE, HT, D)
        XN = take(B, D, parts=L)
        xt = take(2, D)
        xeT = take(2, TS)
        hid = take(2, HID)
        hidT = take(2, HT, TS)
        ot = take(2, D)
        w12_ready = sem("w12_ready")
        scat_done = sem("scat_done")
        xt_ready = [sem("xt_ready0"), sem("xt_ready1")]
        xT_mm = sem("xT_mm")
        xeT_ready = sem("xeT_ready")
        h_mm = sem("h_mm")
        hid_ready = sem("hid_ready")
        hT_mm = sem("hT_mm")
        hidT_ready = sem("hidT_ready")
        o_mm = sem("o_mm")
        ot_ready = sem("ot_ready")
        ot_stored = [sem("ot_stored0"), sem("ot_stored1")]
        og_ready = [sem("og_ready0"), sem("og_ready1")]
        d_end = taken[0]
        taken[0] = R_COLS - B * D
        OG = take(B, D, parts=L)
        assert d_end <= R_COLS - B * D
        fresh()
        w_qkv = take(3, D)
        w_proj = take(D)
        sel = take(K, OH)
        spread = take(K, D, parts=OH)
        rpb_w = take(OH, parts=K)
        posc = take(CT, parts=K)
        qkv = take(2, 3, CT)
        prod = take(2, K, CT)
        S_fm = take(2, CT, parts=OH)
        P_tm = take(2, CB, OH, parts=L)
        P_fm = take(2, CT, parts=OH)
        pv = take(2, CT)
        pv_t = take(2, CT)
        mx = take(2, CB, HEADS, parts=L)
        sm = take(2, CB, HEADS, parts=L)
        qb = take(1)
        at_tmp = take(CB, D, parts=L)
        nE = Norm("e", 1)
        wE_ready = sem("wE_ready")
        qkv_mm, qkv_ready = sem("qkv_mm"), sem("qkv_ready")
        prod_r, S_mm, S_ready = sem("at_prod"), sem("S_mm"), sem("S_ready")
        ST_ready, sub_done, exp_done, P_ready = sem("ST_ready"), sem("sub_done"), sem("exp_done"), sem("P_ready")
        PT_ready, P_fm_ready = sem("PT_ready"), sem("P_fm_ready")
        pb_mm, pb_free, pv_ready = sem("pb_mm"), sem("pb_free"), sem("pv_ready")
        proj_mm, add_done = sem("proj_mm"), sem("add_done")
        assert taken[0] <= R_COLS - B * D
        fresh()
        v1 = take(NE, FF)
        v2 = take(NE, 2, D)
        v2b = take(NE, D, parts=FR)
        b1b = take(NE, parts=FR)
        b2 = take(D, parts=NE)
        pw = take(NE, parts=NPART)
        pwb = take(NE, D, parts=NPART)
        fh = take(2, FT, CT)
        facc = take(2, CT)
        fo = take(2, CB, D, parts=L)
        srep = take(B)
        z = take(8, 16, parts=B)
        zs = take(8, parts=B)
        wcT = take(B, parts=NPART)
        ew = take(NE, B)
        ewT = take(B, parts=NE)
        bb = take(B)
        nF = Norm("f", 1)
        wF_ready = sem("wF_ready")
        rt_pe, rt_dve, rt_act = sem("rt_pe"), sem("rt_dve"), sem("rt_act")
        f_mm, f_free, fh_ready = sem("f_mm"), sem("f_free"), sem("fh_ready")
        fo_mm, fo_free = sem("fo_mm"), sem("fo_free")
        facc_ready, fT_ready, out_ready = sem("facc_ready"), sem("fT_ready"), sem("out_ready")
        out_done = [sem("out_done0"), sem("out_done1")]

        block = ctx.enter_context(nc.Block())

        @block.sync
        def _(sp):
            sp.dma_start(w_emb, t["w_emb"]).then_inc(wload, 16)
            sp.dma_start(cols[:, :], t["cols"]).then_inc(wload, 16)
            sp.dma_start(ident[:, :], t["ident"]).then_inc(wload, 16)
            sp.dma_start(rows[:, :, :], t["rows"]).then_inc(wload, 16)
            sp.dma_start(wprep[:, 0:3, :], t["w_full"]).then_inc(wload, 16)
            sp.dma_start(wprep[0:64, 3, :], t["key_WT"]).then_inc(wload, 16)
            sp.dma_start(wprep[0:64, 4, 0:64], t["M_T"]).then_inc(wload, 16)
            sp.dma_start(wprep[0:64, 5, :], t["recall_W"]).then_inc(wload, 16)
            sp.dma_start(keyb[:, :], t["key_b"]).then_inc(wload, 16)
            sp.dma_start(smallw[:, 0:NE + NPART], t["smallw"]).then_inc(wload, 16)
            sp.dma_start(prio[:, :], t["prio"]).then_inc(wload, 16)
            with sp.Fori(0, NP) as i:
                for u in range(2):
                    sp.wait_ge(y_mm, i * 2 + u + 1)
                    sp.dma_start(xg[:, u], t["xg"][bass.ds(i * 2 + u, 1)].rearrange("a p j n -> (a p) j n"))\
                        .then_inc(xg_ready[u], 16)
            with sp.Fori(0, NS // 2) as i:
                for u in range(2):
                    sp.wait_ge(w_split, i * 2 + u + 1)
                    sp.dma_start(wBC[:, u], t["wBC"][bass.ds(i * 2 + u, 1)].rearrange("a p w d -> (a p) w d"))\
                        .then_inc(wBC_ready[u], 16)
            sp.wait_ge(stage_done, 4 * 3)
            sp.dma_start(w1, t["w1"]).then_inc(w12_ready, 16)
            sp.dma_start(w2, t["w2"]).then_inc(w12_ready, 16)
            for dst, name in ((before, "before"), (thr, "thr"), (tile_no, "tile_no"), (rest, "rest")):
                sp.dma_start(dst, t[name]).then_inc(w12_ready, 16)
            sp.wait_ge(scat_done, 16 * B)
            with sp.Fori(0, NTILE // 2) as i:
                for u in range(2):
                    sp.wait_ge(xT_mm, i * 2 + u + 1)
                    sp.dma_start(xt[:, u], x_sorted[bass.ds((i * 2 + u) * TS, TS)]).then_inc(xt_ready[u], 16)
            sp.wait_ge(stage_done, 4 * 5)
            for dst, name in ((w_qkv, "w_qkv"), (w_proj, "w_proj"), (sel, "sel"), (spread, "spread"),
                              (rpb_w, "rpb_w"), (posc, "posc")):
                sp.dma_start(dst, t[name]).then_inc(wE_ready, 16)
            sp.wait_ge(stage_done, 4 * 7)
            for dst, name in ((v1, "v1"), (v2, "v2"), (v2b, "v2b"), (b1b, "b1b"), (b2, "b2"), (pw, "pw"),
                              (pwb, "pwb")):
                sp.dma_start(dst, t[name]).then_inc(wF_ready, 16)
            with sp.Fori(0, NP) as i:
                for u in range(2):
                    sp.wait_ge(out_ready, i * 2 + u + 3)
                    sp.dma_start(out[bass.ds((i * 2 + u) * CB, CB)].rearrange("b l d -> l b d"), fo[:, u])\
                        .then_inc(out_done[u], 16)
            for u in range(2):
                sp.wait_ge(out_done[u], 16 * (NP + 1))

        @block.gpsimd
        def _(pool):
            step = Tally(pool, pool_step)
            step.add(pool.memset(mhalf[:, :], -0.5))
            pool.sem_inc(w_split, 2)
            step.wait()
            pool.memset(zeros, 0.0).then_inc(zeros_ready, 1)
            pool.wait_ge(zeros_ready, 1)
            pool.dma_start(x_sorted.rearrange("(p a) d -> p (a d)", p=128), zeros).then_inc(fill_done, 16)
            for i in step.loop(NP, 2 * 1 + 2 * 6):
                for u in range(2):
                    wait_apart(pool, nA0[0], i * 2 + u + 1)
                    norm_pool(pool, nA, step, u, nA0[1], False)
                for u in range(2):
                    wait_apart(pool, nA.var_ready, i * 2 + u + 1)
                    norm_pool(pool, nA, step, u, nA.rstd_ready, True)
            pool.wait_ge(fill_done, 16)
            stage_end(pool, 1)
            with pool.Fori(0, NCH) as c:
                pool.tensor_copy(fm(xn_hi, c), fm(xnfm, c)).then_inc(x_split, 1)
                pool.wait_ge(x_split, 2 * c + 1)
                pool.tensor_tensor(fm(xn_lo, c), fm(xnfm, c), fm(xn_hi, c).bitcast(f32), ALU.subtract)\
                    .then_inc(x_split, 1)
            stage_end(pool, 2)
            with pool.Fori(0, NS // 2) as i:
                for u in range(2):
                    n = i * 2 + u
                    pool.wait_ge(wBC_ready[u], 16 * (i + 1))
                    wait_apart(pool, C_ready, n + 1)
                    pool.tensor_copy(w_hi[:, u], wBC[:, u]).then_inc(w_hi_ready, 1)
                    pool.wait_ge(w_hi_ready, n + 1)
                    pool.tensor_tensor(w_lo[:, u], wBC[:, u], w_hi[:, u].bitcast(f32), ALU.subtract)\
                        .then_inc(w_split, 1)
            stage_end(pool, 3)
            for i in step.loop(NP, 2 * 6):
                for u in range(2):
                    wait_apart(pool, nC.var_ready, i * 2 + u + 1)
                    norm_pool(pool, nC, step, u, nC.rstd_ready, True)
            stage_end(pool, 4)
            pool.wait_ge(slot_ready, 1)
            for b in range(B):
                pool.indirect_dma_start(x_sorted, bass.IndirectOffsetOnAxis(ap=slot[:, b:b + 1], axis=0),
                                        XN[:, b, :], None).then_inc(scat_done, 16)
            with pool.Fori(0, NTILE // 2) as i:
                for u in range(2):
                    wait_apart(pool, ot_ready, i * 2 + u + 3)
                    pool.dma_start(y_sorted[bass.ds((i * 2 + u) * TS, TS)], ot[:, u]).then_inc(ot_stored[u], 16)
            for u in range(2):
                pool.wait_ge(ot_stored[u], 16 * (NTILE // 2))
            stage_end(pool, 5)
            for c in range(NCH + 1):
                if c < NCH:
                    if c >= 2:
                        pool.wait_ge(og_ready[c % 2], 16 * CB * (c // 2))
                    for b in range(c * CB, (c + 1) * CB):
                        pool.indirect_dma_start(OG[:, b, :], None, y_sorted,
                                                bass.IndirectOffsetOnAxis(ap=slot[:, b:b + 1], axis=0))\
                            .then_inc(og_ready[c % 2], 16)
                if c:
                    pool.wait_ge(nE.var_ready, c)
                    norm_pool(pool, nE, step, (c - 1) % 2, nE.rstd_ready, False)
            stage_end(pool, 6)
            stage_end(pool, 7)
            for i in step.loop(NP, 2):
                for u in range(2):
                    wait_apart(pool, nF.var_ready, i * 2 + u + 1)
                    norm_pool(pool, nF, step, u, nF.rstd_ready, False)
            stage_end(pool, 8)

        @block.scalar
        def _(act):
            act.wait_ge(wload, N_PREP)
            act.activation(A_pos[:, :], cols[:, at["A_log"]:at["A_log"] + NS], ACT.Exp).then_inc(prep_act, 1)
            act.sem_inc(y_fm_ready, 2)
            act.sem_inc(nA.xT_free, 2)
            act.sem_inc(C_ready, 2)

            def bias_copy(i):
                for u in range(2):
                    act.wait_ge(y_mm, i * 2 + u + 3)
                    act.wait_ge(yT_ready, i * 2 + u + 1)
                    act.activation(y_fm[:, u], bank(u), ACT.Identity, bias=col("tok_b"), scale=1.0)\
                        .then_inc(y_fm_ready, 1)

            bias_copy(0)
            with act.Fori(1, NP) as i:
                bias_copy(i)
                for u in range(2):
                    norm_copies(act, nA, u, (i - 1) * 2 + u, (4, 5), col("ln_gamma"), col("ln_beta"))
            for u in range(2):
                norm_copies(act, nA, u, (NP - 1) * 2 + u, (4, 5), col("ln_gamma"), col("ln_beta"))
            stage_end(act, 1)
            act.wait_ge(delta_act, NCH)
            act.activation(dl[:, 1:1 + TOK], dl[:, 1:1 + TOK], ACT.Exp).then_inc(delta_act, 1)
            act.wait_ge(delta_act, NCH + 1)
            act.activation(dl[:, 1:1 + TOK], dl[:, 1:1 + TOK], ACT.Ln, bias=1.0, scale=1.0).then_inc(delta_act, 1)
            stage_end(act, 2)

            act.sem_inc(bc_free, 2)

            def decays(i):
                for u in range(2):
                    n = i * 2 + u
                    wait_apart(act, th_free, n + 1)
                    act.activation(th[:, u], dl[:, 1:1 + TOK], ACT.Tanh, scale=A_half[:, bass.ds(n, 1)])\
                        .then_inc(th_ready, 1)
                    wait_apart(act, ea_free, n + 1)
                    act.activation(ea, dl[:, 1:1 + TOK], ACT.Exp, scale=A_neg[:, bass.ds(n, 1)])\
                        .then_inc(ea_ready, 1)
                    wait_apart(act, ra_free, n + 1)
                    act.activation(ra[:, u], dl[:, 0:TOK], ACT.Exp, scale=A_pos[:, bass.ds(n, 1)])\
                        .then_inc(ra_ready, 1)

            def silus(i):
                for u in range(2):
                    n = i * 2 + u
                    act.wait_ge(B_free, n + 1)
                    for s, (a, w) in enumerate(SEG):
                        wait_apart(act, bc_mm, (i * 2 + u) * 2 * NSEG + s + 1)
                        ins = act.activation(bufB[:, u, a:a + w], psum[:, 6 + s % 2, 0:w], ACT.Silu,
                                             bias=cols[:, bass.ds(n + at["B_b"], 1)], scale=1.0,
                                             accum_out=part[:, u, s:s + 1])
                        ins.then_inc(bc_free, 1)
                    act.wait_ge(C_free, n + 1)
                    for s, (a, w) in enumerate(SEG):
                        wait_apart(act, bc_mm, (i * 2 + u) * 2 * NSEG + NSEG + s + 1)
                        act.activation(bufC[:, u, a:a + w], psum[:, 6 + s % 2, 0:w], ACT.Silu,
                                       bias=cols[:, bass.ds(n + at["C_b"], 1)], scale=1.0).then_inc(bc_free, 1)
                    act.sem_inc(C_ready, 1)

            with act.Fori(0, NS // 2) as i:
                decays(i)
                silus(i)
            act.wait_ge(acc_done, 1)
            for s, (a, w) in enumerate(SEG):
                ins = act.activation(Y[:, a:a + w], psum[:, s, 0:w], ACT.Identity, bias=skip_b[:, 0:1], scale=1.0)
            stage_end(act, 3)

            act.sem_inc(nC.xT_free, 2)

            def gates(i):
                for u in range(2):
                    act.wait_ge(hm_mm, i * 2 + u + 1)
                    act.wait_ge(hm_free, i * 2 + u + 1)
                    act.activation(sig[:, u], bank(2 + u), ACT.Sigmoid, bias=col("gate_b"), scale=1.0)\
                        .then_inc(sig_ready, 1)

            with act.Fori(0, NP) as i:
                gates(i)
                for u in range(2):
                    norm_copies(act, nC, u, i * 2 + u, (6, 7), col("ffn_gamma"))
                for u in range(2):
                    act.wait_ge(lgF_mm, i * 2 + u + 1)
                    act.activation(lgF[:, u], bank(2 + u, NE), ACT.Copy).then_inc(lgF_ready, 1)
            stage_end(act, 4)
            act.wait_ge(rt_a, 1)
            act.activation(ex, lg, ACT.Exp).then_inc(rt_b, 1)

            act.sem_inc(hid_ready, 2)
            act.sem_inc(ot_ready, 2)

            def gelu(t, u):
                act.wait_ge(hT_mm, t + 1)
                act.wait_ge(h_mm, t + 3)
                act.activation(hid[:, u], psum[:, 2 + u, 0:HID], ACT.Gelu).then_inc(hid_ready, 1)

            def rows_out(t, u, stored=None):
                if stored is not None:
                    act.wait_ge(ot_stored[u], stored)
                act.wait_ge(o_mm, t + 3)
                act.activation(ot[:, u], psum[:, 6 + u, 0:D], ACT.Copy).then_inc(ot_ready, 1)

            gelu(0, 0)
            gelu(1, 1)
            for u in range(2):
                gelu(2 + u, u)
                rows_out(u, u)
            with act.Fori(2, NTILE // 2) as i:
                for u in range(2):
                    gelu(i * 2 + u, u)
                    rows_out(i * 2 + u - 2, u, i * 16 - 16)
            rows_out(NTILE - 2, 0, 8 * NTILE - 16)
            rows_out(NTILE - 1, 1, 8 * NTILE - 16)
            stage_end(act, 5)

            act.sem_inc(nE.xT_free, 2)
            act.wait_ge(wE_ready, 6 * 16)
            with act.Fori(0, NP) as i:
                for u in range(2):
                    norm_copies(act, nE, u, i * 2 + u, (6, 7))
            act.mul(qb, col("qkv_b"), SCALE)
            stage_end(act, 6)
            with act.Fori(0, NP) as i:
                for u in range(2):
                    c = i * 2 + u
                    act.wait_ge(add_done, c + 1)
                    for k in range(3):
                        act.wait_ge(qkv_mm, c * 3 + k + 1)
                        act.activation(qkv[:, u, k], bank(k), ACT.Identity,
                                       bias=qb if k == 0 else col("qkv_b", k),
                                       scale=SCALE if k == 0 else 1.0).then_inc(qkv_ready, 1)
                for u in range(2):
                    c = i * 2 + u
                    act.wait_ge(S_mm, c + 1)
                    act.activation(S_fm[:, u], bank(3 + u, OH), ACT.Copy).then_inc(S_ready, 1)
                for u in range(2):
                    c = i * 2 + u
                    act.wait_ge(sub_done, c + 1)
                    act.activation(P_tm[:, u], P_tm[:, u], ACT.Exp).then_inc(exp_done, 1)
                for u in range(2):
                    c = i * 2 + u
                    act.wait_ge(PT_ready, c + 1)
                    act.activation(P_fm[:, u], bank(3 + u, OH), ACT.Copy).then_inc(P_fm_ready, 1)
            stage_end(act, 7)

            act.sem_inc(nF.xT_free, 2)
            act.wait_ge(wF_ready, 7 * 16)
            with act.Fori(0, NP) as i:
                for u in range(2):
                    norm_copies(act, nF, u, i * 2 + u, (6, 7))
            stage_end(act, 8)
            act.sem_inc(f_free, FT)
            act.wait_ge(rt_act, 1)
            act.activation(z[:, 1, 0:NPART], z[:, 0, 0:NPART], ACT.Exp).then_inc(rt_act, 1)
            with act.Fori(0, NCH) as c:
                for e in range(NE):
                    act.wait_ge(fo_mm, c * NE + e + 1)
                    for j in range(FT):
                        kk = D if j < 2 else FR
                        act.wait_ge(f_mm, (c * NE + e) * FT + j + 1)
                        act.activation(fh[0:kk, e % 2, j], bank(j, kk), ACT.Gelu,
                                       bias=col("b1", 2 * e + j) if j < 2 else b1b[:, e:e + 1], scale=1.0)\
                            .then_inc(f_free, 1)

        @block.vector
        def _(dve):
            step = Tally(dve, dve_step)
            dve.wait_ge(wload, N_PREP)
            step.add(dve.tensor_tensor(w_D[:, :], wprep[:, 0, :], rows[:, 3, :], ALU.mult))
            step.add(dve.tensor_tensor(skip_b[:, 0:1], col("D_b"), col("D_scale"), ALU.mult))
            dve.wait_ge(prep_act, 1)
            step.add(dve.tensor_scalar(A_c[:, :], A_pos[:, :], 1e-4, None, ALU.is_gt))
            step.wait()
            step.add(dve.scalar_tensor_tensor(A_inj[:, :], A_pos[:, :], -1e-12, A_c[:, :], ALU.add, ALU.mult))
            step.wait()
            step.add(dve.tensor_scalar(A_inj[:, :], A_inj[:, :], 1e-12, None, ALU.add))
            step.wait()
            step.add(dve.tensor_scalar(A_half[:, :], A_inj[:, :], 0.5, None, ALU.mult))
            step.add(dve.tensor_scalar(A_neg[:, :], A_inj[:, :], -1.0, None, ALU.mult))
            step.add(dve.reciprocal(A_c[:, :], A_inj[:, :]))
            step.wait()
            step.add(dve.tensor_scalar(A_c[:, :], A_c[:, :], 0.5, None, ALU.mult))
            dve.wait_ge(prep_mm, 1)
            dve.tensor_copy(MR[:, :], psum[0:64, 7, 0:D]).then_inc(prep_cp, 1)
            dve.wait_ge(prep_mm, 2)
            step.add(dve.tensor_copy(w_mem[:, :], psum[:, 7, 0:D]))
            step.add(dve.tensor_tensor(mem_b[:, :], psum[:, 7, D:D + 1], col("recall_b"), ALU.add))

            def seqs(tile, c):
                return tile[:, bass.ds(c * CB, CB), :]

            def row(k):
                return rows[0:L, k:k + 1, :].to_broadcast([L, CB, D])

            PER_A = 2 * (CB + 2 + CB)
            for i in step.loop(NP, PER_A):
                for u in range(2):
                    dve.wait_ge(yT_ready, i * 2 + u + 3)
                    src = bank_tm(2 + u)
                    for j in range(CB):
                        step.add(dve.bn_stats(stat[:, u, j, :], src[:, j, :]))
                    step.wait(True)
                    for j in range(CB):
                        ins = dve.bn_aggr(mv[:, u, j, :], stat[:, u, j, :])
                    ins.then_inc(nA0[0], 1)
                for u in range(2):
                    c = i * 2 + u
                    src = bank_tm(2 + u)
                    dve.wait_ge(nA0[1], c + 1)
                    for j in range(CB):
                        ins = dve.tensor_scalar(yn[:, u, j, :], src[:, j, :], mv[:, u, j, 0:1], rstd[:, u, j:j + 1],
                                                ALU.subtract, ALU.mult)
                    ins.then_inc(yT_free, 1)
                    dve.wait_ge(yT_free, 2 + c + 1)
                    step.add(dve.tensor_tensor(yn[:, u], yn[:, u], row(0), ALU.mult))
                    step.wait()
                    step.add(dve.tensor_tensor(seqs(H, c), yn[:, u], row(1), ALU.add))
                    step.wait(True)
                    norm_stats(dve, nA, step, seqs(H, c), u)
                for u in range(2):
                    dve.wait_ge(nA.rstd_ready, i * 2 + u + 1)
                    norm_apply(dve, nA, u, i * 2 + u)
            stage_end(dve, 1)

            dve.memset(dl[:, 0:1], 0.0)
            with dve.Fori(0, NP) as i:
                for u in range(2):
                    c = i * 2 + u
                    dve.wait_ge(delta_mm, c + 3)
                    dve.tensor_scalar(dl[:, bass.ds(c * CT + 1, CT)], bank(u), col("delta_b"), 0.0, ALU.add, ALU.min)\
                        .then_inc(delta_act, 1)
            dve.wait_ge(delta_act, NCH + 2)
            step.add(dve.tensor_scalar(dl[:, 1:1 + TOK], dl[:, 1:1 + TOK], 0.5, None, ALU.min))
            stage_end(dve, 2)

            dve.sem_inc(th_free, 2)
            dve.sem_inc(ea_free, 1)
            dve.sem_inc(ra_free, 2)
            dve.sem_inc(B_free, 2)
            for i in step.loop(NS // 2, 2 * 5):
                for u in range(2):
                    n = i * 2 + u
                    dve.wait_ge(th_ready, n + 1)
                    dve.wait_ge(ea_ready, n + 1)
                    dve.scalar_tensor_tensor(th[:, u], ea, 1.0, th[:, u], ALU.add, ALU.mult).then_inc(ea_free, 1)
                    dve.wait_ge(ra_ready, n + 1)
                    step.add(dve.tensor_scalar(ra[:, u], ra[:, u], 1e6, None, ALU.min))
                    step.wait()
                    step.add(dve.memset(ra[:, u, 0:TOK:L], 0.0))
                for u in range(2):
                    n = i * 2 + u
                    dve.wait_ge(bc_free, 2 + (n * 2 + 1) * NSEG)
                    step.add(dve.reduce_sum(mean[:, u:u + 1], part[:, u, :], axis=AX))
                    step.wait()
                    step.add(dve.tensor_scalar(mean[:, u:u + 1], mean[:, u:u + 1], 1.0 / TOK, None, ALU.mult))
                    step.wait()
                    dve.scalar_tensor_tensor(bufB[:, u], bufB[:, u], mean[:, u:u + 1], th[:, u],
                                             ALU.subtract, ALU.mult).then_inc(th_free, 1)
                    dve.wait_ge(th_free, 2 + n + 1)
                    dve.tensor_tensor_scan(bufB[:, u], ra[:, u], bufB[:, u], 0.0, ALU.mult, ALU.add).then_inc(ra_free, 1)
                    dve.wait_ge(ra_free, 2 + n + 1)
                    dve.wait_ge(bc_free, 2 + (n * 2 + 2) * NSEG)
                    step.add(dve.scalar_tensor_tensor(bufC[:, u], bufB[:, u], A_c[:, bass.ds(n, 1)], bufC[:, u],
                                                      ALU.mult, ALU.mult))
                    step.wait()
                    dve.sem_inc(B_free, 1)
                    dve.sem_inc(prod_ready, 1)
            stage_end(dve, 3)

            dve.sem_inc(hm_free, 2)
            dve.sem_inc(cT_free, 2)
            dve.sem_inc(lg_free, 2)
            PER_C = 2 * (1 + 1 + 4)
            for i in step.loop(NP, PER_C):
                for u in range(2):
                    c = i * 2 + u
                    dve.wait_ge(sig_ready, c + 1)
                    dve.wait_ge(cT_ready, c + 1)
                    step.add(dve.scalar_tensor_tensor(cF[:, u], bank(u), mem_b[:, 0:1], sig[:, u], ALU.add, ALU.mult))
                    step.wait()
                    dve.sem_inc(hm_free, 1)
                    dve.tensor_tensor(cF[:, u], cF[:, u], fm(Y, c), ALU.add).then_inc(cF_ready, 1)
                for u in range(2):
                    c = i * 2 + u
                    dve.wait_ge(cT_ready, c + 3)
                    step.add(dve.tensor_tensor(seqs(H, c), bank_tm(4 + u), seqs(H, c), ALU.add))
                    step.wait()
                    dve.sem_inc(cT_free, 1)
                    norm_stats(dve, nC, step, seqs(H, c), u)
                for u in range(2):
                    dve.wait_ge(nC.rstd_ready, i * 2 + u + 1)
                    norm_apply(dve, nC, u, i * 2 + u, keep=XN)
                for u in range(2):
                    c = i * 2 + u
                    dve.wait_ge(lgT_ready, c + 1)
                    dve.tensor_copy(lg[:, bass.ds(c * CB, CB), :],
                                    psum[0:L, 2 + u, 0:CB * NE].rearrange("p (j e) -> p j e", j=CB))\
                        .then_inc(lg_free, 1)
            stage_end(dve, 4)

            def per_e(x):
                return x.rearrange("p (b o) -> p b o", o=1).to_broadcast([L, B, NE])

            def tt(o, a, b, op):
                step.add(dve.tensor_tensor(o, a, b, op))
                step.wait()

            step.add(dve.tensor_reduce(r1, lg, AX, ALU.max))
            step.wait()
            dve.tensor_tensor(lg, lg, per_e(r1), ALU.subtract).then_inc(rt_a, 1)
            dve.wait_ge(rt_b, 1)
            step.add(dve.tensor_reduce(r2, ex, AX, ALU.add))
            step.add(dve.tensor_reduce(r1, ex, AX, ALU.max))
            step.wait()
            tt(oh, ex, per_e(r1), ALU.is_equal)
            tt(cand, oh, prio[0:L, 0:NE].rearrange("p (o e) -> p o e", o=1).to_broadcast([L, B, NE]), ALU.mult)
            step.add(dve.tensor_reduce(r3, cand, AX, ALU.max))
            step.wait()
            tt(oh, cand, per_e(r3), ALU.is_equal)
            tt(cand, ex, oh, ALU.mult)
            tt(cand, ex, cand, ALU.subtract)
            step.add(dve.tensor_reduce(r3, cand, AX, ALU.max))
            step.add(dve.reciprocal(r4, r2))
            step.wait()
            tt(r1, r1, r4, ALU.mult)
            tt(r3, r3, r4, ALU.mult)
            tt(r3, r3, r1, ALU.add)
            step.add(dve.tensor_scalar(r3, r3, 1e-9, None, ALU.add))
            step.wait()
            step.add(dve.reciprocal(r3, r3))
            step.wait()
            tt(gate[:, :], r1, r3, ALU.mult)

            def per_b(x):
                return x.rearrange("p (e o) -> p e o", o=1).to_broadcast([L, NE, B])

            dve.wait_ge(w12_ready, 6 * 16)
            step.add(dve.memset(ones, 1.0))
            step.add(dve.tensor_copy(ohE, oh.rearrange("p b e -> p e b")))
            step.wait()
            step.add(dve.tensor_tensor_scan(cum.rearrange("p e b -> p (e b)"), rest.rearrange("p e b -> p (e b)"),
                                            ohE.rearrange("p e b -> p (e b)"), 0.0, ALU.mult, ALU.add))
            step.wait()
            dve.tensor_copy(row_n, cum[:, :, B - 1]).then_inc(cnt_dve, 1)
            dve.wait_ge(cnt_mm, 1)
            n_all = psum[0:L, 1, 0:NE]
            tt(over, n_all.rearrange("p (e o) -> p e o", o=1).to_broadcast([L, NE, NTHR]),
               thr.rearrange("p (o k) -> p o k", o=1).to_broadcast([L, NE, NTHR]), ALU.is_gt)
            step.add(dve.tensor_reduce(n_tiles, over, AX, ALU.add))
            step.wait()
            step.add(dve.tensor_tensor_scan(start, ones[:, 0:NE], n_tiles, 0.0, ALU.mult, ALU.add))
            step.wait()
            tt(start, start, n_tiles, ALU.subtract)
            step.add(dve.scalar_tensor_tensor(base, start, float(TS), psum[0:L, 0, 0:NE], ALU.mult, ALU.add))
            step.wait()
            tt(cum, cum, per_b(base), ALU.add)
            tt(cum, cum, ohE, ALU.mult)
            step.add(dve.tensor_reduce(r2, cum.rearrange("p e b -> p b e"), AX, ALU.add))
            step.wait()
            dve.tensor_scalar(slot[:, :], r2, -1.0, None, ALU.add).then_inc(slot_ready, 1)
            tt(t_cmp, tile_no.rearrange("p (t o) -> p t o", o=1).to_broadcast([L, NTILE, NE - 1]),
               start[:, 1:NE].rearrange("p (o e) -> p o e", o=1).to_broadcast([L, NTILE, NE - 1]), ALU.is_ge)
            step.add(dve.tensor_reduce(t_exp, t_cmp, AX, ALU.add))
            step.wait()
            dve.tensor_copy(tile_e[:, :], t_exp).then_inc(cnt_dve, 1)

            def tile_in(t, u):
                dve.wait_ge(h_mm, t + 1)
                dve.wait_ge(xT_mm, t + 3)
                dve.tensor_scalar(xeT[:, u], psum[:, u, 0:TS], col("ffn_gamma"), None, ALU.mult).then_inc(xeT_ready, 1)

            def hidden_copy(t, u):
                dve.wait_ge(o_mm, t + 1)
                dve.wait_ge(hT_mm, t + 3)
                dve.tensor_copy(hidT[:, u].rearrange("p j t -> p (j t)"), psum[:, 4 + u, 0:HID]).then_inc(hidT_ready, 1)

            tile_in(0, 0)
            tile_in(1, 1)
            with dve.Fori(1, NTILE // 2) as i:
                for u in range(2):
                    tile_in(i * 2 + u, u)
                    hidden_copy(i * 2 + u - 2, u)
            hidden_copy(NTILE - 2, 0)
            hidden_copy(NTILE - 1, 1)
            stage_end(dve, 5)

            def norm_loop(nm, add_experts=False):
                for i in step.loop(NP, 2 * (6 if add_experts else 4)):
                    for u in range(2):
                        if add_experts:
                            c = i * 2 + u
                            dve.wait_ge(og_ready[u], 16 * CB * (i + 1))
                            g = gate[:, bass.ds(c * CB, CB)].rearrange("p (j o) -> p j o", o=1).to_broadcast([L, CB, D])
                            step.add(dve.tensor_tensor(seqs(OG, c), seqs(OG, c), g, ALU.mult))
                            step.wait()
                            step.add(dve.tensor_tensor(seqs(H, c), seqs(H, c), seqs(OG, c), ALU.add))
                            step.wait(True)
                        norm_stats(dve, nm, step, seqs(H, i * 2 + u), u)
                    for u in range(2):
                        dve.wait_ge(nm.rstd_ready, i * 2 + u + 1)
                        norm_apply(dve, nm, u, i * 2 + u)

            norm_loop(nE, True)
            stage_end(dve, 6)
            dve.sem_inc(add_done, 2)
            dve.sem_inc(pb_free, 2)
            E0, E1 = K // 2, L - K // 2

            def per_head(x):
                return x.rearrange("p j (h o) -> p j h o", o=1).to_broadcast([L, CB, HEADS, K])

            def windowed(u, o, other, k, op_out):
                q3 = other.rearrange("p (j l) -> p j l", j=CB)
                k3 = qkv[:, u, k].rearrange("p (j l) -> p j l", j=CB)
                o3 = op_out.rearrange("p (j l) -> p j l", j=CB)
                yield o3[:, :, E0:E1], q3[:, :, E0:E1], k3[:, :, o:o + E1 - E0]
                for lo, at_k in ((0, o), (E1, L - K + o)):
                    yield (o3[:, :, lo:lo + E0], q3[:, :, lo:lo + E0],
                           k3[:, :, at_k:at_k + 1].to_broadcast([128, CB, E0]))

            PER_E = 2 * (1 + 2 + K - 1 + 1)
            for i in step.loop(NP, PER_E):
                for u in range(2):
                    c = i * 2 + u
                    dve.wait_ge(qkv_ready, c * 3 + 3)
                    for o in range(K):
                        for dst, a, b in windowed(u, o, qkv[:, u, 0], 1, prod[:, u, o]):
                            ins = dve.tensor_tensor(dst, a, b, ALU.mult)
                        ins.then_inc(prod_r, 1)
                for u in range(2):
                    c = i * 2 + u
                    dve.wait_ge(ST_ready, c + 1)
                    s4 = psum[0:L, 5, 0:CB * OH].rearrange("p (j o h) -> p j h o", j=CB, o=K)
                    p4 = P_tm[:, u].rearrange("p j (o h) -> p j h o", o=K)
                    step.add(dve.tensor_reduce(mx[:, u], s4, AX, ALU.max))
                    step.wait()
                    dve.tensor_tensor(p4, s4, per_head(mx[:, u]), ALU.subtract).then_inc(sub_done, 1)
                for u in range(2):
                    c = i * 2 + u
                    p4 = P_tm[:, u].rearrange("p j (o h) -> p j h o", o=K)
                    dve.wait_ge(exp_done, c + 1)
                    step.add(dve.tensor_reduce(sm[:, u], p4, AX, ALU.add))
                    step.wait()
                    step.add(dve.reciprocal(sm[:, u], sm[:, u]))
                    step.wait()
                    dve.tensor_tensor(p4, p4, per_head(sm[:, u]), ALU.mult).then_inc(P_ready, 1)
                for u in range(2):
                    c = i * 2 + u
                    for o in range(K):
                        dve.wait_ge(pb_mm, c * K + o + 1)
                        dst_t = pv[:, u] if o == 0 else pv_t[:, o % 2]
                        for dst, a, b in windowed(u, o, bank(6 + (u + o) % 2), 2, dst_t):
                            ins = dve.tensor_tensor(dst, a, b, ALU.mult)
                        ins.then_inc(pb_free, 1)
                        if o:
                            dve.wait_ge(pb_free, 2 + c * K + o + 1)
                            ins = step.add(dve.tensor_tensor(pv[:, u], pv[:, u], pv_t[:, o % 2], ALU.add))
                            step.wait()
                    dve.sem_inc(pv_ready, 1)
                for u in range(2):
                    c = i * 2 + u
                    dve.wait_ge(proj_mm, c + 1)
                    step.add(dve.tensor_tensor(at_tmp, bank_tm(3 + u), row(2), ALU.add))
                    step.wait()
                    dve.tensor_tensor(seqs(H, c), seqs(H, c), at_tmp, ALU.add).then_inc(add_done, 1)
                    dve.wait_ge(add_done, 2 + c + 1)
            stage_end(dve, 7)

            norm_loop(nF)
            stage_end(dve, 8)
            x3 = xfm[:, :].rearrange("p (b l) -> p b l", b=B)
            dve.tensor_reduce(srep, x3, AX, ALU.add).then_inc(rt_dve, 1)
            dve.wait_ge(rt_pe, 1)
            N = slice(0, NPART)
            zz = [z[:, k, N] for k in range(8)]
            s1 = [zs[:, k:k + 1] for k in range(8)]

            def ts(o, a, x, y, p, q=None):
                if q is None:
                    step.add(dve.tensor_scalar(o, a, x, None, p))
                else:
                    step.add(dve.tensor_scalar(o, a, x, y, p, q))
                step.wait()

            def red(o, a, op):
                step.add(dve.tensor_reduce(o, a, AX, op))
                step.wait()

            ts(zz[0], psum[0:B, 0, N], 1.0 / L, None, ALU.mult)
            red(s1[0], zz[0], ALU.max)
            dve.tensor_scalar(zz[0], zz[0], s1[0], None, ALU.subtract).then_inc(rt_act, 1)
            dve.wait_ge(rt_act, 2)
            red(s1[1], zz[1], ALU.add)
            step.add(dve.reciprocal(s1[1], s1[1]))
            step.wait()
            ts(zz[1], zz[1], s1[1], None, ALU.mult)

            def first_largest(p, m, one):
                red(m, p, ALU.max)
                ts(zz[7], p, m, None, ALU.is_equal)
                tt(zz[7], zz[7], prio[0:B, N], ALU.mult)
                red(s1[7], zz[7], ALU.max)
                ts(one, zz[7], s1[7], None, ALU.is_equal)

            first_largest(zz[1], s1[2], zz[2])
            step.add(dve.scalar_tensor_tensor(zz[3], zz[2], -2.0, zz[1], ALU.mult, ALU.add))
            step.wait()
            first_largest(zz[3], s1[3], zz[4])
            tt(s1[4], s1[2], s1[3], ALU.add)
            step.add(dve.reciprocal(s1[4], s1[4]))
            step.wait()
            ts(zz[2], zz[2], s1[2], s1[4], ALU.mult, ALU.mult)
            ts(zz[4], zz[4], s1[3], s1[4], ALU.mult, ALU.mult)
            dve.tensor_tensor(zz[5], zz[2], zz[4], ALU.add).then_inc(rt_dve, 1)
            dve.wait_ge(rt_pe, 2)
            dve.tensor_copy(wcT, psum[0:NPART, 1, 0:B]).then_inc(rt_dve, 1)
            dve.wait_ge(rt_pe, 3)
            step.add(dve.tensor_copy(ew, psum[:, 2, 0:NE * B].rearrange("p (e b) -> p e b", e=NE)))
            step.add(dve.tensor_copy(ewT, psum[0:NE, 3, 0:B]))
            step.wait()
            step.add(dve.scalar_tensor_tensor(ew, ew, 1e-6, ew, ALU.is_gt, ALU.mult))
            step.add(dve.scalar_tensor_tensor(ewT, ewT, 1e-6, ewT, ALU.is_gt, ALU.mult))
            step.wait()
            dve.sem_inc(rt_dve, 1)
            dve.wait_ge(rt_pe, 4)
            step.add(dve.tensor_copy(bb, psum[:, 4, 0:B]))
            step.wait()
            dve.sem_inc(fo_free, 2)
            dve.sem_inc(out_ready, 2)
            for u in range(2):
                dve.sem_inc(out_done[u], 16)
            for i in step.loop(NP, 2 * (NE * CB)):
                for u in range(2):
                    c = i * 2 + u
                    dve.wait_ge(fT_ready, c + 1)
                    for e in range(NE):
                        dve.wait_ge(fo_mm, c * NE + e + 3)
                        for j in range(CB):
                            a = facc[:, u, j * L:(j + 1) * L]
                            p = psum[:, 4 + e % 2, j * L:(j + 1) * L]
                            we = ew[:, e, bass.ds(c * CB + j, 1)]
                            if e == 0:
                                ins = dve.tensor_scalar(a, p, we, bb[:, bass.ds(c * CB + j, 1)], ALU.mult, ALU.add)
                            else:
                                ins = dve.scalar_tensor_tensor(a, p, we, a, ALU.mult, ALU.add)
                            step.add(ins)
                        step.wait()
                        dve.sem_inc(fo_free, 1)
                    dve.sem_inc(facc_ready, 1)
                for u in range(2):
                    c = i * 2 + u
                    dve.wait_ge(fT_ready, c + 3)
                    dve.wait_ge(out_done[u], 16 * (i + 1))
                    dve.tensor_tensor(fo[:, u], bank_tm(6 + u), seqs(H, c), ALU.add).then_inc(out_ready, 1)

        @block.tensor
        def _(pe):
            pe.wait_ge(wload, N_PREP)
            pe.matmul(psum[0:64, 7, 0:D], wprep[0:64, 4, 0:64], wprep[0:64, 5, :], start=True, stop=True)\
                .then_inc(prep_mm, 1)
            pe.wait_ge(prep_cp, 1)
            pe.matmul(psum[:, 7, 0:D], wprep[0:64, 3, :], MR[:, :], start=True, stop=True)
            pe.matmul(psum[:, 7, D:D + 1], MR[:, :], keyb[:, :], start=True, stop=True).then_inc(prep_mm, 1)

            pe.sem_inc(y_mm, 2)
            pe.sem_inc(yT_ready, 2)
            pe.sem_inc(nA.xT_ready, 4)
            pe.sem_inc(yT_free, 2)

            def embed(i):
                for u in range(2):
                    c = i * 2 + u
                    pe.wait_ge(xg_ready[u], 16 * (i + 1))
                    pe.wait_ge(y_fm_ready, c + 1)
                    x4 = xg[:, u].rearrange("p j (b g) -> p j b g", b=CB)
                    for n in range(8):
                        j, h = n // 2, n % 2
                        ins = pe.matmul(bank(u).rearrange("p (b l) -> p b l", b=CB), w_emb[:, j, h, :],
                                        x4[:, j, :, h:h + L], start=(n == 0), stop=(n == 7))
                    ins.then_inc(y_mm, 1)

            def to_tm(i):
                for u in range(2):
                    c = i * 2 + u
                    pe.wait_ge(y_fm_ready, c + 3)
                    pe.wait_ge(yT_free, c + 1)
                    for j in range(CB):
                        ins = pe.transpose(bank_tm(2 + u)[:, j, :], y_fm[:, u, j * L:(j + 1) * L], ident[:, :])
                    ins.then_inc(yT_ready, 1)

            def to_fm(nm, i, banks):
                for u in range(2):
                    norm_transposes(pe, nm, u, i * 2 + u, banks)

            embed(0)
            to_tm(0)
            with pe.Fori(1, NP) as i:
                embed(i)
                to_fm(nA, i - 1, (4, 5))
                to_tm(i)
            to_fm(nA, NP - 1, (4, 5))
            stage_end(pe, 1)

            pe.sem_inc(delta_mm, 2)
            with pe.Fori(0, NP) as i:
                for u in range(2):
                    c = i * 2 + u
                    pe.matmul(bank(u), wprep[:, 1, :], fm(xnfm, c), start=True, stop=True).then_inc(delta_mm, 1)
                    pe.wait_ge(delta_act, c + 1)
            stage_end(pe, 2)

            for s, (a, w) in enumerate(SEG):
                pe.matmul(psum[:, s, 0:w], w_D[:, :], xfm[:, a:a + w], start=True, stop=False, skip_group_check=True)
            pe.sem_inc(C_free, 2)

            def states(n, u, k):
                for s, (a, w) in enumerate(SEG):
                    pe.wait_ge(bc_free, n * 2 * NSEG + k * NSEG + s + 1)
                    o = psum[:, 6 + s % 2, 0:w]
                    pe.matmul(o, w_hi[:, u, k, :], xn_lo[:, a:a + w], start=True, stop=False)
                    pe.matmul(o, w_lo[:, u, k, :], xn_hi[:, a:a + w], start=False, stop=False)
                    pe.matmul(o, w_hi[:, u, k, :], xn_hi[:, a:a + w], start=False, stop=True).then_inc(bc_mm, 1)

            def add_state(n, u, last=False):
                pe.wait_ge(prod_ready, n + 1)
                for s, (a, w) in enumerate(SEG):
                    ins = pe.matmul(psum[:, s, 0:w], ident[:, :], bufC[:, u, a:a + w], start=False, stop=last,
                                    skip_group_check=True)
                ins.then_inc(C_free, 1)

            def state_pair(i, first=False):
                if not first:
                    add_state(i * 2 - 2, 0)
                    add_state(i * 2 - 1, 1)
                for u in range(2):
                    pe.wait_ge(w_split, 2 + i * 2 + u + 1)
                    states(i * 2 + u, u, 0)
                    states(i * 2 + u, u, 1)

            state_pair(0, True)
            with pe.Fori(1, NS // 2) as i:
                state_pair(i)
            add_state(NS - 2, 0)
            add_state(NS - 1, 1, True)
            pe.drain().then_inc(acc_done, 1)
            stage_end(pe, 3)

            pe.sem_inc(cT_ready, 2)
            pe.sem_inc(nC.xT_ready, 2)
            with pe.Fori(0, NP) as i:
                for u in range(2):
                    c = i * 2 + u
                    pe.wait_ge(hm_free, c + 1)
                    pe.wait_ge(lg_free, c + 1)
                    pe.matmul(bank(u), w_mem[:, :], fm(Y, c), start=True, stop=True)
                    pe.matmul(bank(2 + u), wprep[:, 2, :], fm(Y, c), start=True, stop=True).then_inc(hm_mm, 1)
                for u in range(2):
                    c = i * 2 + u
                    pe.wait_ge(cF_ready, c + 1)
                    pe.wait_ge(cT_free, c + 1)
                    for j in range(CB):
                        ins = pe.transpose(bank_tm(4 + u)[:, j, :], cF[:, u, j * L:(j + 1) * L], ident[:, :])
                    ins.then_inc(cT_ready, 1)
                to_fm(nC, i, (6, 7))
                for u in range(2):
                    c = i * 2 + u
                    pe.wait_ge(nC.xT_free, 2 + c + 1)
                    pe.wait_ge(sig_ready, c + 1)
                    pe.matmul(bank(2 + u, NE), smallw[:, 0:NE], fm(xfm, c), start=True, stop=True).then_inc(lgF_mm, 1)
                for u in range(2):
                    c = i * 2 + u
                    wait_apart(pe, lgF_ready, c + 1)
                    for j in range(CB):
                        ins = pe.transpose(psum[0:L, 2 + u, j * NE:(j + 1) * NE], lgF[:, u, j * L:(j + 1) * L],
                                           ident[0:NE, 0:NE])
                    ins.then_inc(lgT_ready, 1)
            stage_end(pe, 4)

            pe.wait_ge(cnt_dve, 1)
            pe.matmul(psum[0:L, 0, 0:NE], before, row_n, start=True, stop=True)
            pe.matmul(psum[0:L, 1, 0:NE], ones, row_n, start=True, stop=True).then_inc(cnt_mm, 1)

            def tile_in(t, u):
                pe.wait_ge(xt_ready[u], 8 * (t - u) + 16)
                pe.transpose(psum[:, u, 0:TS], xt[:, u], ident[:, :]).then_inc(xT_mm, 1)

            e_new = [pe.alloc_register("e_new0"), pe.alloc_register("e_new1")]
            e_old = [pe.alloc_register("e_old0"), pe.alloc_register("e_old1")]

            def next_expert(t, u, keep=True):
                if keep:
                    pe.reg_mov(e_old[u], e_new[u])
                pe.reg_load(e_new[u], tile_e[0:1, bass.ds(t, 1)])

            def expert(reg):
                return pe.snap(reg, min_val=0, max_val=NE - 1)

            def layer1(t, u, e):
                pe.wait_ge(xeT_ready, t + 1)
                pe.wait_ge(hid_ready, t + 1)
                pe.matmul(psum[:, 2 + u, 0:HID], xeT[:, u], w1[:, bass.ds(e, 1), :].rearrange("p a h -> p (a h)"),
                          start=True, stop=True).then_inc(h_mm, 1)

            def turn(t, u):
                pe.wait_ge(hid_ready, t + 3)
                for j in range(HT):
                    ins = pe.transpose(psum[:, 4 + u, j * TS:(j + 1) * TS], hid[:, u, j * D:(j + 1) * D], ident[:, :])
                ins.then_inc(hT_mm, 1)

            def layer2(t, u, e):
                pe.wait_ge(hidT_ready, t + 1)
                pe.wait_ge(ot_ready, t + 1)
                for j in range(HT):
                    ins = pe.matmul(psum[:, 6 + u, 0:D], hidT[:, u, j], w2[:, bass.ds(e, 1), j].rearrange("p a d -> p (a d)"),
                                    start=(j == 0), stop=(j == HT - 1))
                ins.then_inc(o_mm, 1)

            pe.wait_ge(cnt_dve, 2)
            for s in (xT_mm, h_mm, hT_mm, o_mm):
                pe.sem_inc(s, 2)
            def moe_step(t, u, more=True):
                layer1(t, u, expert(e_new[u]))
                if more:
                    next_expert(t + 1, 1 - u)
                    tile_in(t + 1, 1 - u)
                turn(t - 1, 1 - u)
                layer2(t - 2, u, expert(e_old[u]))

            tile_in(0, 0)
            next_expert(0, 0, False)
            next_expert(1, 1, False)
            layer1(0, 0, expert(e_new[0]))
            tile_in(1, 1)
            layer1(1, 1, expert(e_new[1]))
            next_expert(2, 0)
            tile_in(2, 0)
            turn(0, 0)
            with pe.Fori(1, NTILE // 2 - 1) as i:
                for u in range(2):
                    moe_step(i * 2 + u, u)
            moe_step(NTILE - 2, 0)
            moe_step(NTILE - 1, 1, False)
            turn(NTILE - 1, 1)
            layer2(NTILE - 2, 0, expert(e_new[0]))
            layer2(NTILE - 1, 1, expert(e_new[1]))
            stage_end(pe, 5)

            pe.sem_inc(nE.xT_ready, 2)
            with pe.Fori(0, NP) as i:
                to_fm(nE, i, (6, 7))
            stage_end(pe, 6)
            pe.wait_ge(wE_ready, 6 * 16)
            with pe.Fori(0, NP) as i:
                for u in range(2):
                    c = i * 2 + u
                    for k in range(3):
                        if u:
                            pe.wait_ge(qkv_ready, (c - 1) * 3 + k + 1)
                        pe.matmul(bank(k), w_qkv[:, k, :], fm(xfm, c), start=True, stop=True).then_inc(qkv_mm, 1)
                for u in range(2):
                    c = i * 2 + u
                    pe.wait_ge(add_done, c + 1)
                    for o in range(K):
                        pe.wait_ge(prod_r, c * K + o + 1)
                        pe.matmul(bank(3 + u, OH), sel[:, o, :], prod[:, u, o], start=(o == 0), stop=False)
                    pe.matmul(bank(3 + u, OH), rpb_w, posc, start=False, stop=True).then_inc(S_mm, 1)
                for u in range(2):
                    c = i * 2 + u
                    pe.wait_ge(S_ready, c + 1)
                    if u:
                        pe.wait_ge(sub_done, c)
                    for j in range(CB):
                        ins = pe.transpose(psum[0:L, 5, j * OH:(j + 1) * OH], S_fm[:, u, j * L:(j + 1) * L],
                                           ident[0:OH, 0:OH])
                    ins.then_inc(ST_ready, 1)
                for u in range(2):
                    c = i * 2 + u
                    pe.wait_ge(P_ready, c + 1)
                    for j in range(CB):
                        ins = pe.transpose(psum[0:OH, 3 + u, j * L:(j + 1) * L], P_tm[:, u, j], ident[0:L, 0:L])
                    ins.then_inc(PT_ready, 1)
                for u in range(2):
                    c = i * 2 + u
                    pe.wait_ge(P_fm_ready, c + 1)
                    for o in range(K):
                        pe.wait_ge(pb_free, c * K + o + 1)
                        pe.matmul(bank(6 + (u + o) % 2), spread[:, o, :], P_fm[:, u], start=True, stop=True)\
                            .then_inc(pb_mm, 1)
                for u in range(2):
                    c = i * 2 + u
                    pe.wait_ge(pv_ready, c + 1)
                    for j in range(CB):
                        ins = pe.matmul(bank_tm(3 + u)[:, j, :], pv[:, u, j * L:(j + 1) * L], w_proj,
                                        start=True, stop=True)
                    ins.then_inc(proj_mm, 1)
            stage_end(pe, 7)

            pe.sem_inc(nF.xT_ready, 2)
            with pe.Fori(0, NP) as i:
                to_fm(nF, i, (6, 7))
            stage_end(pe, 8)
            pe.wait_ge(wF_ready, 7 * 16)
            pe.wait_ge(rt_dve, 1)
            pe.matmul(psum[0:B, 0, 0:NPART], srep, smallw[:, NE:NE + NPART], start=True, stop=True).then_inc(rt_pe, 1)
            pe.wait_ge(rt_dve, 2)
            pe.transpose(psum[0:NPART, 1, 0:B], z[:, 5, 0:NPART], ident[0:B, 0:B]).then_inc(rt_pe, 1)
            pe.wait_ge(rt_dve, 3)
            for e in range(NE):
                pe.matmul(psum[:, 2, e * B:(e + 1) * B], pwb[:, e, :], wcT, start=True, stop=True)
            pe.matmul(psum[0:NE, 3, 0:B], pw, wcT, start=True, stop=True).then_inc(rt_pe, 1)
            pe.wait_ge(rt_dve, 4)
            pe.matmul(psum[:, 4, 0:B], b2, ewT, start=True, stop=True).then_inc(rt_pe, 1)
            pe.sem_inc(fo_mm, 2)
            pe.sem_inc(fT_ready, 2)
            with pe.Fori(0, NP) as i:
                for u in range(2):
                    c = i * 2 + u
                    for e in range(NE):
                        for j in range(FT):
                            kk = D if j < 2 else FR
                            pe.wait_ge(f_free, (c * NE + e) * FT + j + 1)
                            pe.matmul(bank(j, kk), v1[:, e, j * D:j * D + kk], fm(xfm, c), start=True, stop=True)\
                                .then_inc(f_mm, 1)
                        pe.wait_ge(fo_free, c * NE + e + 1)
                        pe.wait_ge(f_free, FT + (c * NE + e) * FT + FT)
                        for j in range(FT):
                            kk = D if j < 2 else FR
                            w = v2[:, e, j, :] if j < 2 else v2b[:, e, :]
                            ins = pe.matmul(bank(4 + e % 2), w, fh[0:kk, e % 2, j], start=(j == 0), stop=(j == FT - 1))
                        ins.then_inc(fo_mm, 1)
                for u in range(2):
                    c = i * 2 + u
                    pe.wait_ge(facc_ready, c + 1)
                    pe.wait_ge(out_ready, c + 1)
                    for j in range(CB):
                        ins = pe.transpose(bank_tm(6 + u)[:, j, :], facc[:, u, j * L:(j + 1) * L], ident[:, :])
                    ins.then_inc(fT_ready, 1)


def kernel(**inp):
    import numpy as np
    import concourse.bacc as bacc
    from concourse.bass_utils import run_bass_kernel_spmd

    a = {k: np.asarray(v) for k, v in inp.items()}
    B, S, C = a["x"].shape
    L = (S - 16) // 8 + 1
    G, D, CB, NS, NE, K, HEADS = L + 1, 128, 4, 16, 6, 7, 16
    f = np.float32

    def c_(x):
        return np.ascontiguousarray(x)

    t = {}
    x = a["x"][:, :G * 8].reshape(B // CB, CB, G, 512).transpose(0, 3, 1, 2)
    t["xg"] = c_(x.reshape(B // CB, 4, 128, CB * G).transpose(0, 2, 1, 3))
    w = a["L0_tok_W"].reshape(C, 2, 8, D).transpose(2, 0, 1, 3).reshape(4, 128, 2, D)
    t["w_emb"] = c_(w.transpose(1, 0, 2, 3))
    one = lambda k: a[k].reshape(D, 1)
    b1 = a["L1_ffn_b1"]
    t["cols"] = c_(np.concatenate([
        one("L0_tok_b"), one("L0_attn_ln_gamma"), one("L0_attn_ln_beta"), one("L0_attn_D_b"),
        one("L0_attn_D_scale"), one("L0_attn_recall_b"), one("L0_ffn_gamma"),
        a["L1_attn_qkv_b"].reshape(3, D).T, a["L0_attn_A_log"], a["L0_attn_B_b"].reshape(D, NS),
        a["L0_attn_C_b"].reshape(D, NS), b1[:, :2 * D].reshape(NE * 2, D).T,
        np.broadcast_to(a["L0_attn_delta_b"].reshape(1, 1), (D, 1)),
        np.broadcast_to(a["L0_attn_gate_b"].reshape(1, 1), (D, 1))], axis=1))
    t["rows"] = c_(np.broadcast_to(np.stack([a["L0_tok_gamma"], a["L0_tok_beta"], a["L1_attn_proj_b"],
                                             a["L0_attn_D_scale"]])[None], (128, 4, D)))
    t["ident"] = np.eye(128, dtype=f)
    t["w_full"] = c_(np.stack([a["L0_attn_D_W"], np.broadcast_to(a["L0_attn_delta_W"], (D, D)),
                               np.broadcast_to(a["L0_attn_gate_W"], (D, D))], axis=1))
    t["key_WT"] = c_(a["L0_attn_key_W"].T)
    t["M_T"] = c_(a["L0_attn_M"].T)
    t["recall_W"] = a["L0_attn_recall_W"]
    t["key_b"] = a["L0_attn_key_b"].reshape(64, 1)
    t["smallw"] = c_(np.concatenate([a["L0_ffn_w_gating"], a["L1_ffn_router_w"].T], axis=1))
    t["prio"] = c_(np.broadcast_to(np.arange(16, 0, -1).astype(f)[None], (128, 16)))
    TOK = B * L
    NTILE = (TOK + NE * 127) // 128
    NTILE += NTILE % 2
    t["before"] = np.triu(np.ones((L, L), f), 1)
    t["thr"] = c_(np.broadcast_to(128 * np.arange(-(-TOK // 128)).astype(f)[None], (L, -(-TOK // 128))))
    t["tile_no"] = c_(np.broadcast_to(np.arange(NTILE).astype(f)[None], (L, NTILE)))
    rest = np.ones((L, NE, B), f)
    rest[:, :, 0] = 0
    t["rest"] = rest
    bw = a["L0_attn_B_W"].reshape(D, D, NS).transpose(2, 0, 1)
    cw = a["L0_attn_C_W"].reshape(D, D, NS).transpose(2, 0, 1)
    t["wBC"] = c_(np.stack([bw, cw], axis=2))
    t["w1"] = c_(a["L0_ffn_w1"].transpose(1, 0, 2))
    t["w2"] = c_(a["L0_ffn_w2"].reshape(NE, 4, D, D).transpose(2, 0, 1, 3))
    t["w_qkv"] = c_(a["L1_attn_qkv_w"].reshape(3, D, D).transpose(2, 0, 1))
    t["w_proj"] = c_(a["L1_attn_proj_w"].T)
    head = np.arange(D) // (D // HEADS)
    sel = np.zeros((D, K, K * HEADS), f)
    for o in range(K):
        sel[np.arange(D), o, o * HEADS + head] = 1
    t["sel"] = sel
    t["spread"] = c_(sel.transpose(2, 1, 0))
    t["rpb_w"] = c_(np.stack([a["L1_attn_rpb"][:, c:c + K].T.reshape(-1) for c in range(K)]))
    pos = np.arange(L)
    first = np.clip(pos - K // 2, 0, L - K) - pos + K - 1
    t["posc"] = c_(np.tile((first[None] == np.arange(K)[:, None]).astype(f), (1, CB)))
    v = a["L1_ffn_W1"]
    t["v1"] = c_(v.transpose(1, 0, 2))
    t["v2"] = c_(a["L1_ffn_W2"][:, :2 * D].reshape(NE, 2, D, D).transpose(2, 0, 1, 3))
    t["v2b"] = c_(a["L1_ffn_W2"][:, 2 * D:].transpose(1, 0, 2))
    t["b1b"] = c_(b1[:, 2 * D:].T)
    t["b2"] = a["L1_ffn_b2"]
    parts = [(6,), (5, 1), (4, 2), (4, 1, 1), (3, 3), (3, 2, 1), (3, 1, 1, 1), (2, 2, 2), (2, 2, 1, 1),
             (2, 1, 1, 1, 1), (1, 1, 1, 1, 1, 1)]
    pw = np.zeros((11, NE), f)
    for i, p in enumerate(parts):
        for j, q in enumerate(p):
            pw[i, j] = q / 6
    t["pw"] = pw
    t["pwb"] = c_(np.broadcast_to(pw[:, :, None], (11, NE, D)))

    nc = bacc.Bacc("TRN2", target_bir_lowering=False, num_devices=1)
    f32 = mybir.dt.float32
    aps = {k: nc.dram_tensor("in_" + k, v.shape, f32, kind="ExternalInput").ap() for k, v in t.items()}
    out = nc.dram_tensor("out_0", (B, L, D), f32, kind="ExternalOutput").ap()
    audio_tower(nc, aps, out)
    r = run_bass_kernel_spmd(nc, [{"in_" + k: v for k, v in t.items()}], core_ids=[0])
    return r.results[0]["out_0"]
```

```python
import math
from contextlib import ExitStack

import concourse.bass as bass
from concourse import mybir


def audio_tower(nc, t, out):
    f32 = mybir.dt.float32
    f32r = mybir.dt.float32r
    ALU = mybir.AluOpType
    ACT = mybir.ActivationFunctionType
    AX = mybir.AxisListType.X

    B, L, D = out.shape
    CB = 4
    NCH = B // CB
    NP = NCH // 2
    CT = CB * L
    TOK = B * L
    G = L + 1
    NS = 16
    NE = 6
    HID = 512
    HT = HID // D
    FF = 341
    FT = 3
    FR = FF - 2 * D
    K = 7
    HEADS = 16
    OH = K * HEADS
    NPART = 11
    LG0 = 400
    TS = 128
    NTILE = (TOK + NE * (TS - 1)) // TS
    NTILE += NTILE % 2
    NTHR = -(-TOK // TS)
    SCALE = float(D // HEADS) ** -0.5
    EPS = 1e-5
    HB = 2
    NH = NCH // HB

    names = [("tok_b", 1), ("ln_gamma", 1), ("ln_beta", 1), ("D_b", 1), ("D_scale", 1),
             ("recall_b", 1), ("ffn_gamma", 1), ("qkv_b", 3), ("A_log", NS), ("B_b", NS),
             ("C_b", NS), ("b1", 2 * NE), ("delta_b", 1), ("gate_b", 1)]
    at, NCOL = {}, 0
    for name, n in names:
        at[name] = NCOL
        NCOL += n

    ctx = ExitStack()
    with ctx:
        def sb(name, shape, dt=f32):
            return ctx.enter_context(nc.sbuf_tensor("s_" + name, shape, dt))

        def sem(name):
            return ctx.enter_context(nc.semaphore(name))

        xfm = sb("xfm", [128, TOK])
        xnfm = sb("xnfm", [128, TOK])
        H = sb("H", [L, B, D])
        cols = sb("cols", [128, NCOL])
        rows = sb("rows", [128, 4, D])
        ident = sb("ident", [128, 128])
        wprep = sb("wprep", [128, 6, 128])
        w_D = sb("w_D", [128, 128])
        w_mem = sb("w_mem", [128, 128])
        MR = sb("MR", [64, 128])
        keyb = sb("keyb", [64, 1])
        unused = sb("unused", [128, 2])
        mem_b = sb("mem_b", [128, 1])
        stat = sb("stat", [L, 2, CB, 6])
        mv = sb("mv", [L, 2, CB, 2])
        rstd = sb("rstd", [L, 2, CB])
        rstd2 = sb("rstd2", [L, 2, CB])
        pa = sb("pa", [L, 2, CB])
        mhalf = sb("mhalf", [L, CB])
        xs = sb("xs", [L, 2, CB, D])
        smallw = sb("smallw", [128, 32])
        A_pos = sb("A_pos", [128, NS])
        A_inj = sb("A_inj", [128, NS])
        A_half = sb("A_half", [128, NS])
        A_neg = sb("A_neg", [128, NS])
        A_c = sb("A_c", [128, NS])
        gate = sb("gate", [L, B])
        slot = sb("slot", [L, B], mybir.dt.uint32)
        R_COLS = 10 * TOK + 1
        R = sb("R", [128, R_COLS])
        psum = ctx.enter_context(nc.psum_tensor("psum", [128, 8, 512], f32))
        x_sorted = nc.dram_tensor("x_sorted", (NTILE * TS, D), f32, kind="Internal").ap()
        y_sorted = nc.dram_tensor("y_sorted", (NTILE * TS, D), f32, kind="Internal").ap()

        taken = [0]

        def fresh():
            taken[0] = 0

        def take(*shape, parts=128):
            n = 1
            for s in shape:
                n *= s
            view = R[0:parts, taken[0]:taken[0] + n]
            taken[0] += n
            assert taken[0] <= R_COLS
            if len(shape) > 1:
                ax = "abcd"[:len(shape)]
                view = view.rearrange("p (" + " ".join(ax) + ") -> p " + " ".join(ax),
                                      **{x: s for x, s in zip(ax, shape)})
            return view

        def bank(b, parts=128, n=CT):
            return psum[0:parts, b, 0:n]

        def bank_tm(b):
            return psum[0:L, b, 0:CB * D].rearrange("p (j d) -> p j d", j=CB)

        wload = sem("wload")
        stage_done = sem("stage_done")
        apart = sem("apart")
        prep_mm, prep_cp = sem("prep_mm"), sem("prep_cp")
        prep_act, prep_read = sem("prep_act"), sem("prep_read")
        dve_step = sem("dve_step")
        pool_step = sem("pool_step")

        w_emb_ready, cols_ready = sem("w_emb_ready"), sem("cols_ready")
        N_PREP = 9 * 16

        def wait_apart(eng, s, value):
            eng.wait_ge(s, value)
            eng.sem_inc(apart, 1)

        class Tally:

            def __init__(self, eng, s):
                self.eng, self.sem, self.base, self.n = eng, s, 0, 0

            def add(self, ins):
                self.n += 1
                return ins.then_inc(self.sem, 1)

            def wait(self, apart=False):
                (wait_apart(self.eng, self.sem, self.base + self.n) if apart
                 else self.eng.wait_ge(self.sem, self.base + self.n))

            def loop(self, trips, per):
                start = self.base + self.n
                with self.eng.Fori(0, trips) as i:
                    self.base, self.n = start + i * per, 0
                    yield i
                    assert self.n == per, (self.n, per)
                self.base, self.n = start + trips * per, 0

        def stage_end(eng, k):
            eng.drain().then_inc(stage_done, 1)
            eng.wait_ge(stage_done, 4 * k)

        def fm(tile, c):
            return tile[:, bass.ds(c * CT, CT)]

        def seqs(tile, c):
            return tile[:, bass.ds(c * CB, CB), :]

        def col(name, k=0):
            return cols[:, at[name] + k:at[name] + k + 1]

        class Norm:
            def __init__(self, tag, n):
                self.n = n
                self.var_ready = sem(tag + "_var_ready")
                self.rstd_ready = sem(tag + "_rstd_ready")
                self.xs_ready = sem(tag + "_xs_ready")
                self.xs1_ready = sem(tag + "_xs1_ready")
                self.xT_ready = sem(tag + "_xT_ready")
                self.xT_free = sem(tag + "_xT_free")

        def norm_stats(dve, nm, step, src, u):
            for j in range(CB):
                step.add(dve.bn_stats(stat[:, u, j, :], src[:, j, :]))
            step.wait(True)
            for j in range(CB):
                ins = dve.bn_aggr(mv[:, u, j, :], stat[:, u, j, :])
            ins.then_inc(nm.var_ready, 1)

        def norm_pool(pool, nm, step, u, c, ready, two):
            step.add(pool.tensor_scalar(pa[:, u, :], mv[:, u, :, 1], 1.0, EPS, ALU.mult, ALU.add))
            step.wait()
            last = pool.tensor_tensor(rstd[:, u, :], pa[:, u, :], mhalf[:, :], ALU.pow)
            if two:
                step.add(last)
                step.wait()
                step.add(pool.tensor_tensor(pa[:, u, :], rstd[:, u, :], rstd[:, u, :], ALU.mult))
                step.wait()
                step.add(pool.tensor_tensor(pa[:, u, :], pa[:, u, :], mv[:, u, :, 1], ALU.mult))
                step.wait(True)
                step.add(pool.tensor_scalar(pa[:, u, :], pa[:, u, :], 1.0, EPS, ALU.mult, ALU.add))
                step.wait()
                wait_apart(pool, nm.xs1_ready, c + 1)
                last = pool.tensor_tensor(rstd2[:, u, :], pa[:, u, :], mhalf[:, :], ALU.pow)
            last.then_inc(ready, 1)

        def norm_apply(dve, nm, u, c, two=False):
            dve.wait_ge(nm.xT_ready, nm.n * (c + 1))
            if two:
                dve.wait_ge(nm.xs1_ready, c + 1)
            for j in range(CB):
                ins = dve.tensor_scalar(xs[:, u, j, :], H[:, bass.ds(c * CB + j, 1), :].rearrange("p a d -> p (a d)"),
                                        mv[:, u, j, 0:1], rstd[:, u, j:j + 1], ALU.subtract, ALU.mult)
            ins.then_inc(nm.xs_ready, 1)

        def norm_second(act, nm, u, c, keep=None):
            wait_apart(act, nm.xs_ready, c + 1)
            if keep is None:
                wait_apart(act, nm.xT_ready, nm.n * (c + 1))
            for j in range(CB):
                dst = xs1[:, u, j, :]
                if keep is not None:
                    dst = keep[:, bass.ds(c * CB + j, 1), :].rearrange("p a d -> p (a d)")
                ins = act.activation(dst, xs[:, u, j, :], ACT.Identity, scale=rstd2[:, u, j:j + 1], bias=0.0)
            ins.then_inc(nm.xs1_ready, 1)

        def norm_transposes(pe, nm, u, c, banks):
            for w in range(nm.n):
                if w:
                    pe.wait_ge(nm.xs1_ready, c + 3)
                else:
                    pe.wait_ge(nm.xs_ready, c + 1)
                pe.wait_ge(nm.xT_free, nm.n * c + w + 1)
                b = banks[w if nm.n == 2 else u]
                for j in range(CB):
                    ins = pe.transpose(psum[:, b, j * L:(j + 1) * L], (xs1 if w else xs)[:, u, j, :], ident[0:L, 0:L])
                ins.then_inc(nm.xT_ready, 1)

        def norm_copies(act, nm, u, c, banks, scale=None, bias=None, dst=xfm, hi=None):
            for w in range(nm.n):
                wait_apart(act, nm.xT_ready, 2 * nm.n + nm.n * c + w + 1)
                b = banks[w if nm.n == 2 else u]
                if w == 0:
                    if nm.n == 1 and hi is not None:
                        act.activation(fm(hi, c), bank(b), ACT.Copy)
                    ins = act.activation(dst[:, u] if dst is lgx else fm(dst, c), bank(b), ACT.Copy)
                else:
                    act.activation(fm(hi, c), bank(b), ACT.Identity, scale=scale, bias=bias)
                    ins = act.activation(fm(xnfm, c), bank(b), ACT.Identity, scale=scale, bias=bias)
                ins.then_inc(nm.xT_free, 1)

        fresh()
        w_emb = take(4, 2, D)
        xg = take(2, 4, CB * G)
        y_fm = take(2, CT)
        yn = take(2, CB, D, parts=L)
        xs1 = take(2, CB, D, parts=L)
        zeros = take(NTILE * D)
        zeros_ready, fill_done = sem("zeros_ready"), sem("fill_done")
        nA = Norm("a", 2)
        nA0 = sem("a_var0_ready"), sem("a_rstd0_ready")
        stat0 = take(2, CB, 6, parts=L)
        mv0 = take(2, CB, 2, parts=L)
        rstd0 = take(2, CB, parts=L)
        xg_ready = [sem("xg_ready0"), sem("xg_ready1")]
        y_mm = sem("y_mm")
        y_fm_ready = sem("y_fm_ready")
        yT_ready = sem("yT_ready")
        yT_free = sem("yT_free")

        fresh()
        bufB = take(2, TOK)
        bufC = take(2, TOK)
        th = take(2, TOK)
        ea = take(TOK)
        ra = take(2, TOK)
        dl = take(1 + TOK)
        wBC = sb("wBC", [128, 2, 2, D])
        split_hi = sb("split_hi", [128, NE * FF], f32r)
        split_lo = sb("split_lo", [128, NE * FF], f32r)
        w_hi, w_lo = (x[:, 0:4 * D].rearrange("p (u k d) -> p u k d", u=2, k=2) for x in (split_hi, split_lo))
        v1_hi, v1_lo = (x[:, :].rearrange("p (e f) -> p e f", e=NE) for x in (split_hi, split_lo))
        xn_hi = sb("xn_hi", [128, TOK], f32r)
        xn_lo = sb("xn_lo", [128, TOK], f32r)
        w_hi_ready, w_split, x_split = sem("w_hi_ready"), sem("w_split"), sem("x_split")
        part = sb("part", [128, 2, NH])
        mean = sb("mean", [128, 2])
        skip_b = sb("skip_b", [128, 1])
        delta_mm, delta_act, delta_read = sem("delta_mm"), sem("delta_act"), sem("delta_read")
        wBC_ready = [sem("wBC_ready0"), sem("wBC_ready1")]
        bc_mm = sem("bc_mm")
        bc_free = sem("bc_free")
        C_ready = sem("C_ready")
        th_ready, ea_ready, ra_ready = sem("th_ready"), sem("ea_ready"), sem("ra_ready")
        th_free, ea_free, ra_free = sem("th_free"), sem("ea_free"), sem("ra_free")
        B_free = sem("B_free")
        prod_ready = sem("prod_ready")
        C_free = sem("C_free")
        skip_mm = sem("skip_mm")

        fresh()
        Y = xnfm
        sig = take(2, CT)
        cF = take(2, CT)
        lgx = take(2, CT)
        lg = take(B, NE, parts=L)
        nC = Norm("c", 1)
        hm_mm = sem("hm_mm")
        sig_ready = sem("sig_ready")
        hm_free = sem("hm_free")
        cF_ready = sem("cF_ready")
        cT_ready = sem("cT_ready")
        cT_free = sem("cT_free")
        lg_mm, lg_free = sem("lg_mm"), sem("lg_free")
        ex = take(B, NE, parts=L)
        oh = take(B, NE, parts=L)
        cand = take(B, NE, parts=L)
        r1 = take(B, parts=L)
        r2 = take(B, parts=L)
        r3 = take(B, parts=L)
        r4 = take(B, parts=L)
        prio = sb("prio", [128, 16])
        rt_a, rt_b = sem("rt_a"), sem("rt_b")
        ohE = take(NE, B, parts=L)
        cum = take(NE, B, parts=L)
        rest = take(NE, B, parts=L)
        before = take(L, parts=L)
        ones = take(L, parts=L)
        thr = take(NTHR, parts=L)
        tile_no = take(NTILE, parts=L)
        row_n = take(NE, parts=L)
        over = take(NE, NTHR, parts=L)
        n_tiles = take(NE, parts=L)
        start = take(NE, parts=L)
        base = take(NE, parts=L)
        t_cmp = take(NTILE, NE - 1, parts=L)
        t_exp = take(NTILE, parts=L)
        tile_e = sb("tile_e", [L, NTILE], mybir.dt.int32)
        cnt_mm, cnt_dve, slot_ready = sem("cnt_mm"), sem("cnt_dve"), sem("slot_ready")
        w1 = take(NE, HID)
        w2 = take(NE, HT, D)
        XN = take(B, D, parts=L)
        xt = take(2, D)
        xeT = take(2, TS)
        hid = take(2, HID)
        hidT = take(2, HT, TS)
        ot = take(2, D)
        w12_ready = sem("w12_ready")
        scat_done = sem("scat_done")
        xt_ready = [sem("xt_ready0"), sem("xt_ready1")]
        xT_mm = sem("xT_mm")
        xeT_ready = sem("xeT_ready")
        h_mm = sem("h_mm")
        hid_ready = sem("hid_ready")
        hT_mm = sem("hT_mm")
        hidT_ready = sem("hidT_ready")
        o_mm = sem("o_mm")
        ot_ready = sem("ot_ready")
        ot_stored = [sem("ot_stored0"), sem("ot_stored1")]
        og_ready = [sem("og_ready0"), sem("og_ready1")]
        d_end = taken[0]
        taken[0] = R_COLS - B * D
        OG = take(B, D, parts=L)
        W_COLS = 3 * D + D + K * OH + K * D + OH + CT + NE * FF + 3 * NE * D + NE + D + NE + NE * D
        W_AT = R_COLS - B * D - W_COLS
        taken[0] = W_AT
        w_qkv = take(3, D)
        w_proj = take(D)
        sel = take(K, OH)
        spread = take(K, D, parts=OH)
        rpb_w = take(OH, parts=K)
        posc = take(CT, parts=K)
        v1 = take(NE, FF)
        v2 = take(NE, 2, D)
        v2b = take(NE, D, parts=FR)
        b1b = take(NE, parts=FR)
        b2 = take(D, parts=NE)
        pw = take(NE, parts=NPART)
        pwb = take(NE, D, parts=NPART)
        assert d_end <= W_AT and taken[0] == W_AT + W_COLS
        fresh()
        qkv = take(2, 3, CT)
        prod = take(K, CT)
        S_fm = take(CT, parts=OH)
        P_tm = take(2, CB, OH, parts=L)
        P_fm = take(2, CT, parts=OH)
        pv = take(2, CT)
        pv_t = take(2, CT)
        mx = take(2, CB, HEADS, parts=L)
        sm = take(2, CB, HEADS, parts=L)
        qb = take(1)
        nE = Norm("e", 1)
        wE_ready, qb_ready = sem("wE_ready"), sem("qb_ready")
        qkv_mm, qkv_ready = sem("qkv_mm"), sem("qkv_ready")
        prod_r, S_mm, S_ready = sem("at_prod"), sem("S_mm"), sem("S_ready")
        ST_ready, sub_done, exp_done, P_ready = sem("ST_ready"), sem("sub_done"), sem("exp_done"), sem("P_ready")
        PT_ready, P_fm_ready = sem("PT_ready"), sem("P_fm_ready")
        pb_mm, pb_free = sem("pb_mm"), sem("pb_free")
        proj_mm = sem("proj_mm")
        fh = take(3, FT, CT)
        facc = take(CT)
        ftmp = take(2, CT)
        fo = take(2, CB, D, parts=L)
        srep = take(CB)
        z = take(8, 16, parts=CB)
        zs = take(8, parts=CB)
        euler = take(NPART, parts=CB)
        bias_added = sem("bias_added")
        wcT = take(CB, parts=NPART)
        ew = take(NE, CB)
        ewT = take(CB, parts=NE)
        bb = take(CB)
        assert taken[0] <= W_AT
        nF = Norm("f", 1)
        wF_ready = sem("wF_ready")
        v1_hi_ready, v1_split, xf_split = sem("v1_hi_ready"), sem("v1_split"), sem("xf_split")
        srep_ready, lgt_mm, rt_max, rt_exp = sem("srep_ready"), sem("lgt_mm"), sem("rt_max"), sem("rt_exp")
        wc_ready, wcT_mm, wcT_ready = sem("wc_ready"), sem("wcT_mm"), sem("wcT_ready")
        ew_mm, ewT_ready, bb_mm, ew_ready = sem("ew_mm"), sem("ewT_ready"), sem("bb_mm"), sem("ew_ready")
        pv_add = sem("pv_add")
        facc_add = sem("facc_add")
        f_mm, f_free = sem("f_mm"), sem("f_free")
        fo_mm, fo_free = sem("fo_mm"), sem("fo_free")
        fT_ready, out_ready = sem("fT_ready"), sem("out_ready")
        out_done = [sem("out_done0"), sem("out_done1")]
        FFN = ([(1, e, j) for e in (0, 1, 2) for j in range(FT)]
               + [(2, e, j) for e in (0, 1) for j in range(FT)]
               + [(1, 3, j) for j in range(FT)] + [(2, 2, j) for j in range(FT)]
               + [(1, 4, j) for j in range(FT)] + [(2, 3, j) for j in range(FT)]
               + [(1, 5, j) for j in range(FT)] + [(2, e, j) for e in (4, 5) for j in range(FT)])
        NF = len(FFN)

        block = ctx.enter_context(nc.Block())

        @block.sync
        def _(sp):
            sp.dma_start(w_emb, t["w_emb"]).then_inc(w_emb_ready, 16)
            for u in range(2):
                sp.dma_start(xg[:, u], t["xg"][u]).then_inc(xg_ready[u], 16)
            sp.dma_start(cols[:, :], t["cols"]).then_inc(cols_ready, 16)
            sp.dma_start(ident[:, :], t["ident"]).then_inc(wload, 16)
            sp.dma_start(rows[:, :, :], t["rows"]).then_inc(wload, 16)
            sp.dma_start(wprep[:, 0:3, :], t["w_full"]).then_inc(wload, 16)
            sp.dma_start(wprep[0:64, 3, :], t["key_WT"]).then_inc(wload, 16)
            sp.dma_start(wprep[0:64, 4, 0:64], t["M_T"]).then_inc(wload, 16)
            sp.dma_start(wprep[0:64, 5, :], t["recall_W"]).then_inc(wload, 16)
            sp.dma_start(keyb[:, :], t["key_b"]).then_inc(wload, 16)
            sp.dma_start(smallw[:, 0:NE + NPART], t["smallw"]).then_inc(wload, 16)
            sp.dma_start(prio[:, :], t["prio"]).then_inc(wload, 16)
            with sp.Fori(1, NP) as i:
                for u in range(2):
                    sp.wait_ge(y_mm, i * 2 + u + 1)
                    sp.dma_start(xg[:, u], t["xg"][bass.ds(i * 2 + u, 1)].rearrange("a p j n -> (a p) j n"))\
                        .then_inc(xg_ready[u], 16)
            with sp.Fori(0, NS // 2) as i:
                for u in range(2):
                    sp.wait_ge(w_split, i * 2 + u + 1)
                    sp.dma_start(wBC[:, u], t["wBC"][bass.ds(i * 2 + u, 1)].rearrange("a p w d -> (a p) w d"))\
                        .then_inc(wBC_ready[u], 16)
            sp.wait_ge(stage_done, 4 * 2)
            sp.dma_start(w1, t["w1"]).then_inc(w12_ready, 16)
            sp.dma_start(w2, t["w2"]).then_inc(w12_ready, 16)
            for dst, name in ((before, "before"), (thr, "thr"), (tile_no, "tile_no"), (rest, "rest")):
                sp.dma_start(dst, t[name]).then_inc(w12_ready, 16)
            for dst, name in ((w_qkv, "w_qkv"), (w_proj, "w_proj"), (sel, "sel"), (spread, "spread"),
                              (rpb_w, "rpb_w"), (posc, "posc")):
                sp.dma_start(dst, t[name]).then_inc(wE_ready, 16)
            for dst, name in ((v1, "v1"), (v2, "v2"), (v2b, "v2b"), (b1b, "b1b"), (b2, "b2"), (pw, "pw"),
                              (pwb, "pwb")):
                sp.dma_start(dst, t[name]).then_inc(wF_ready, 16)
            sp.wait_ge(scat_done, 16 * B)
            with sp.Fori(0, NTILE // 2) as i:
                for u in range(2):
                    sp.wait_ge(xT_mm, i * 2 + u + 1)
                    sp.dma_start(xt[:, u], x_sorted[bass.ds((i * 2 + u) * TS, TS)]).then_inc(xt_ready[u], 16)
            with sp.Fori(0, NP) as i:
                for u in range(2):
                    sp.wait_ge(out_ready, i * 2 + u + 1)
                    sp.dma_start(out[bass.ds((i * 2 + u) * CB, CB)].rearrange("b l d -> l b d"), fo[:, u])\
                        .then_inc(out_done[u], 16)
            for u in range(2):
                sp.wait_ge(out_done[u], 16 * (NP + 1))

        @block.gpsimd
        def _(pool):
            step = Tally(pool, pool_step)
            step.add(pool.memset(mhalf[:, :], -0.5))
            pool.sem_inc(w_split, 2)
            step.wait()
            pool.memset(zeros, 0.0).then_inc(zeros_ready, 1)
            pool.wait_ge(zeros_ready, 1)
            pool.dma_start(x_sorted.rearrange("(p a) d -> p (a d)", p=128), zeros).then_inc(fill_done, 16)
            step.wait(True)

            def rstd_embed(i):
                for u in range(2):
                    wait_apart(pool, nA0[0], i * 2 + u + 1)
                    step.add(pool.tensor_scalar(pa[:, u, :], mv0[:, u, :, 1], 1.0, EPS, ALU.mult, ALU.add))
                    step.wait()
                    pool.tensor_tensor(rstd0[:, u, :], pa[:, u, :], mhalf[:, :], ALU.pow).then_inc(nA0[1], 1)

            def rstd_stream(i):
                for u in range(2):
                    wait_apart(pool, nA.var_ready, i * 2 + u + 1)
                    norm_pool(pool, nA, step, u, i * 2 + u, nA.rstd_ready, True)

            def split_x(i):
                for u in range(2):
                    c = i * 2 + u
                    wait_apart(pool, nA.xT_free, 2 + 2 * c + 2)
                    pool.tensor_tensor(fm(xn_lo, c), fm(xnfm, c), fm(xn_hi, c).bitcast(f32), ALU.subtract)\
                        .then_inc(x_split, 1)

            before_0 = step.n
            rstd_embed(0)
            rstd_stream(0)
            for i in step.loop(NP - 1, step.n - before_0):
                rstd_embed(i + 1)
                rstd_stream(i + 1)
                split_x(i)
            split_x(NP - 1)
            pool.wait_ge(fill_done, 16)
            stage_end(pool, 1)
            pool.memset(Y[:, :], 0.0).then_inc(C_free, 1)

            def add_states(i):
                for u in range(2):
                    n = i * 2 + u
                    pool.wait_ge(prod_ready, n + 1)
                    wait_apart(pool, C_free, n + 1)
                    pool.tensor_tensor(Y[:, :], Y[:, :], bufC[:, u], ALU.add).then_inc(C_free, 1)

            def split_weights(i):
                for u in range(2):
                    n = i * 2 + u
                    pool.wait_ge(wBC_ready[u], 16 * (i + 1))
                    wait_apart(pool, C_ready, n + 1)
                    pool.tensor_copy(w_hi[:, u], wBC[:, u]).then_inc(w_hi_ready, 1)
                    pool.wait_ge(w_hi_ready, n + 1)
                    pool.tensor_tensor(w_lo[:, u], wBC[:, u], w_hi[:, u].bitcast(f32), ALU.subtract)\
                        .then_inc(w_split, 1)

            split_weights(0)
            with pool.Fori(1, NS // 2) as i:
                split_weights(i)
                add_states(i - 1)
            stage_end(pool, 2)
            for i in step.loop(NP, 2 * 5):
                for u in range(2):
                    wait_apart(pool, nC.var_ready, i * 2 + u + 1)
                    norm_pool(pool, nC, step, u, i * 2 + u, nC.rstd_ready, True)
            stage_end(pool, 3)
            pool.wait_ge(slot_ready, 1)
            for b in range(B):
                pool.indirect_dma_start(x_sorted, bass.IndirectOffsetOnAxis(ap=slot[:, b:b + 1], axis=0),
                                        XN[:, b, :], None).then_inc(scat_done, 16)
            with pool.Fori(0, NTILE // 2) as i:
                for u in range(2):
                    wait_apart(pool, ot_ready, i * 2 + u + 3)
                    pool.dma_start(y_sorted[bass.ds((i * 2 + u) * TS, TS)], ot[:, u]).then_inc(ot_stored[u], 16)
            for u in range(2):
                pool.wait_ge(ot_stored[u], 16 * (NTILE // 2))
            stage_end(pool, 4)

            def gather(c):
                if c >= 2:
                    pool.wait_ge(og_ready[c % 2], 16 * CB * (c // 2))
                for b in range(c * CB, (c + 1) * CB):
                    pool.indirect_dma_start(OG[:, b, :], None, y_sorted,
                                            bass.IndirectOffsetOnAxis(ap=slot[:, b:b + 1], axis=0))\
                        .then_inc(og_ready[c % 2], 16)

            def rstd_e(c, u):
                wait_apart(pool, nE.var_ready, c + 1)
                norm_pool(pool, nE, step, u, c, nE.rstd_ready, False)

            def add_experts(f, lo, hi, first_wait=None):
                for layer, e, j in FFN[lo:hi]:
                    if (layer, j) == (2, FT - 1):
                        if e == 0 and first_wait is not None:
                            wait_apart(pool, fT_ready, first_wait)
                        wait_apart(pool, fo_free, f * NE + e + 3)
                        if e:
                            wait_apart(pool, facc_add, f * NE + e + 2)
                        a3, t3 = (x.rearrange("p (j l) -> p j l", j=CB) for x in (facc, ftmp[:, e % 2]))
                        other = bb.rearrange("p (j o) -> p j o", o=1).to_broadcast([D, CB, L]) if e == 0 else a3
                        pool.tensor_tensor(a3, t3, other, ALU.add).then_inc(facc_add, 1)

            step.add(pool.memset(euler, math.e))
            step.wait(True)

            def pool_chunk(c, u, att=True, ffn=True, out=True, nxt=True, gathers=()):
                f = c - 1
                if ffn:
                    pool.wait_ge(rt_max, f + 1)
                    pool.tensor_tensor(z[:, 1, 0:NPART], euler, z[:, 0, 0:NPART], ALU.pow).then_inc(rt_exp, 1)
                if att:
                    wait_apart(pool, nE.xs_ready, c + 1)
                    h = seqs(H, c)
                    pool.tensor_tensor(h, h, rows[0:L, 2:3, :].to_broadcast([L, CB, D]), ALU.add).then_inc(bias_added, 1)
                for g in gathers:
                    gather(g)
                if att and nxt:
                    rstd_e(c + 1, 1 - u)
                if ffn:
                    add_experts(f, 0, 17, c - 1 if out else None)
                if att:
                    for o in range(1, K):
                        wait_apart(pool, pb_free, c * K + o + 1)
                        pool.tensor_tensor(pv[:, u], pv[:, u], pv_t[:, o % 2], ALU.add).then_inc(pv_add, 1)
                        if o < K - 1:
                            wait_apart(pool, pv_add, c * (K - 1) + o)
                    if ffn:
                        add_experts(f, 17, 27)
                    wait_apart(pool, nF.var_ready, c + 1)
                    norm_pool(pool, nF, step, u, c, nF.rstd_ready, False)
                if ffn:
                    add_experts(f, 27 if att else 17, NF)

            gather(0)
            gather(1)
            rstd_e(0, 0)
            gather(2)
            gather(3)
            pool_chunk(0, 0, ffn=False, out=False, gathers=(4, 5))
            before_1 = step.n
            pool_chunk(1, 1, out=False, gathers=(6, 7))
            for i in step.loop(NP - 2, 2 * (step.n - before_1)):
                for u in range(2):
                    pool_chunk(i * 2 + 2 + u, u)
            pool_chunk(NCH - 2, 0)
            pool_chunk(NCH - 1, 1, nxt=False)
            pool_chunk(NCH, 0, att=False)
            stage_end(pool, 5)

        @block.scalar
        def _(act):
            act.wait_ge(cols_ready, 16)
            act.activation(A_pos[:, :], cols[:, at["A_log"]:at["A_log"] + NS], ACT.Exp).then_inc(prep_act, 1)
            act.sem_inc(y_fm_ready, 2)
            act.sem_inc(nA.xT_free, 2)
            act.sem_inc(C_ready, 2)

            def load_table(func, k):
                act.activation(unused[:, k:k + 1], ident[:, 0:1], func)

            def bias_copy(i):
                for u in range(2):
                    act.wait_ge(y_mm, i * 2 + u + 3)
                    act.wait_ge(yT_ready, i * 2 + u + 1)
                    act.activation(y_fm[:, u], bank(u), ACT.Identity, bias=col("tok_b"), scale=1.0)\
                        .then_inc(y_fm_ready, 1)

            def norms_fm(i):
                for u in range(2):
                    norm_second(act, nA, u, i * 2 + u)
                for u in range(2):
                    norm_copies(act, nA, u, i * 2 + u, (4, 5), col("ln_gamma"), col("ln_beta"), hi=xn_hi)

            act.sem_inc(nA.xs1_ready, 2)
            bias_copy(0)
            with act.Fori(1, NP) as i:
                bias_copy(i)
                norms_fm(i - 1)
            norms_fm(NP - 1)
            act.wait_ge(delta_read, 2 + NCH)
            act.activation(dl[:, 1:1 + TOK], dl[:, 1:1 + TOK], ACT.Exp).then_inc(delta_act, 1)
            act.wait_ge(delta_act, 1)
            act.activation(dl[:, 1:1 + TOK], dl[:, 1:1 + TOK], ACT.Ln, bias=1.0, scale=1.0).then_inc(delta_act, 1)
            stage_end(act, 1)

            act.sem_inc(bc_free, NH)

            def decays(i):
                def tanh(n, u):
                    wait_apart(act, th_free, n + 1)
                    act.activation(th[:, u], dl[:, 1:1 + TOK], ACT.Tanh, scale=A_half[:, bass.ds(n, 1)])\
                        .then_inc(th_ready, 1)

                def exp_minus(n):
                    wait_apart(act, ea_free, n + 1)
                    act.activation(ea, dl[:, 1:1 + TOK], ACT.Exp, scale=A_neg[:, bass.ds(n, 1)])\
                        .then_inc(ea_ready, 1)

                def exp_plus(n, u):
                    wait_apart(act, ra_free, n + 1)
                    act.activation(ra[:, u], dl[:, 0:TOK], ACT.Exp, scale=A_pos[:, bass.ds(n, 1)])\
                        .then_inc(ra_ready, 1)

                tanh(i * 2, 0)
                exp_minus(i * 2)
                exp_plus(i * 2, 0)
                tanh(i * 2 + 1, 1)
                exp_plus(i * 2 + 1, 1)
                exp_minus(i * 2 + 1)

            def group(tile, u, h):
                return tile[:, u, h * HB * CT:(h + 1) * HB * CT].rearrange("p (s n) -> p s n", s=HB)

            def silus(i):
                for u in range(2):
                    n = i * 2 + u
                    act.wait_ge(B_free, n + 1)
                    for h in range(NH):
                        wait_apart(act, bc_mm, n * 2 * NH + h + 1)
                        act.activation(group(bufB, u, h), psum[:, h * HB:(h + 1) * HB, 0:CT], ACT.Silu,
                                       bias=cols[:, bass.ds(n + at["B_b"], 1)], scale=1.0,
                                       accum_out=part[:, u, h:h + 1]).then_inc(bc_free, 1)
                    if not isinstance(i, int):
                        act.wait_ge(C_free, n)
                    for h in range(NH):
                        wait_apart(act, bc_mm, n * 2 * NH + NH + h + 1)
                        act.activation(group(bufC, u, h), psum[:, h * HB:(h + 1) * HB, 0:CT], ACT.Silu,
                                       bias=cols[:, bass.ds(n + at["C_b"], 1)], scale=1.0).then_inc(bc_free, 1)
                    act.sem_inc(C_ready, 1)

            decays(0)
            silus(0)
            with act.Fori(1, NS // 2) as i:
                decays(i)
                silus(i)
            stage_end(act, 2)

            act.sem_inc(nC.xT_free, 2)

            def gates(i):
                for u in range(2):
                    act.wait_ge(hm_mm, i * 2 + u + 1)
                    act.wait_ge(hm_free, i * 2 + u + 1)
                    act.activation(sig[:, u], bank(2 + u), ACT.Sigmoid, bias=col("gate_b"), scale=1.0)\
                        .then_inc(sig_ready, 1)

            def logits_in(i):
                for u in range(2):
                    norm_second(act, nC, u, i * 2 + u, XN)
                for u in range(2):
                    act.wait_ge(lg_mm, i * 2 + u + 1)
                    norm_copies(act, nC, u, i * 2 + u, (6, 7), dst=lgx)

            act.sem_inc(nC.xs1_ready, 2)
            gates(0)
            gates(1)
            with act.Fori(1, NP - 1) as i:
                gates(i + 1)
                logits_in(i - 1)
            logits_in(NP - 2)
            logits_in(NP - 1)
            stage_end(act, 3)
            act.wait_ge(rt_a, 1)
            act.activation(ex, lg, ACT.Exp).then_inc(rt_b, 1)

            act.sem_inc(hid_ready, 2)
            act.sem_inc(ot_ready, 2)

            def gelu(t, u):
                act.wait_ge(hT_mm, t + 1)
                act.wait_ge(h_mm, t + 3)
                act.activation(hid[:, u], psum[:, 2 + u, 0:HID], ACT.Gelu).then_inc(hid_ready, 1)

            def rows_out(t, u, stored=None):
                if stored is not None:
                    act.wait_ge(ot_stored[u], stored)
                act.wait_ge(o_mm, t + 3)
                act.activation(ot[:, u], psum[:, 6 + u, 0:D], ACT.Copy).then_inc(ot_ready, 1)

            gelu(0, 0)
            gelu(1, 1)
            for u in range(2):
                gelu(2 + u, u)
                rows_out(u, u)
            with act.Fori(2, NTILE // 2) as i:
                for u in range(2):
                    gelu(i * 2 + u, u)
                    rows_out(i * 2 + u - 2, u, i * 16 - 16)
            rows_out(NTILE - 2, 0, 8 * NTILE - 16)
            rows_out(NTILE - 1, 1, 8 * NTILE - 16)
            stage_end(act, 4)

            act.sem_inc(nE.xT_free, 2)
            act.mul(qb, col("qkv_b"), SCALE).then_inc(qb_ready, 1)
            act.wait_ge(qb_ready, 1)
            norm_copies(act, nE, 0, 0, (7, 7))
            act.sem_inc(nF.xT_free, 2)
            act.sem_inc(f_free, 2)

            def gelus(f, lo, hi):
                for layer, e, j in FFN[lo:hi]:
                    if layer == 1:
                        kk = D if j < 2 else FR
                        if j == 0:
                            act.wait_ge(fo_mm, f * NE + e + 1)
                        wait_apart(act, f_mm, (f * NE + e) * FT + j + 1)
                        act.activation(fh[0:kk, e % 3, j], bank(j % 2 if e % 2 == 0 else (j + 1) % 2, kk), ACT.Gelu,
                                       bias=col("b1", 2 * e + j) if j < 2 else b1b[:, e:e + 1], scale=1.0)\
                            .then_inc(f_free, 1)

            def act_chunk(c, u, att=True, ffn=True, nxt=True):
                f = c - 1
                if att:
                    for k, b in enumerate((6, 7, 3)):
                        act.wait_ge(qkv_mm, c * 3 + k + 1)
                        act.activation(qkv[:, u, k], bank(b), ACT.Identity,
                                       bias=qb if k == 0 else col("qkv_b", k),
                                       scale=SCALE if k == 0 else 1.0).then_inc(qkv_ready, 1)
                if ffn:
                    gelus(f, 0, 9)
                else:
                    act.wait_ge(wF_ready, 7 * 16)
                    act.activation(v1_hi[:, :, :], v1, ACT.Copy).then_inc(v1_hi_ready, 1)
                if att:
                    act.wait_ge(S_mm, c + 1)
                    act.activation(S_fm, bank(3, OH), ACT.Copy).then_inc(S_ready, 1)
                    load_table(ACT.Exp, 0)
                    act.wait_ge(sub_done, c + 1)
                    act.activation(P_tm[:, u], P_tm[:, u], ACT.Exp).then_inc(exp_done, 1)
                    if ffn:
                        load_table(ACT.Gelu, 1)
                if ffn:
                    gelus(f, 9, 17)
                if att:
                    act.wait_ge(PT_ready, c + 1)
                    act.activation(P_fm[:, u], bank(3, OH), ACT.Copy).then_inc(P_fm_ready, 1)
                if ffn:
                    gelus(f, 17, NF)
                if att and nxt:
                    norm_copies(act, nE, 1 - u, c + 1, (7, 7))
                if att:
                    norm_copies(act, nF, u, c, (5, 5), dst=xnfm, hi=xn_hi)

            act_chunk(0, 0, ffn=False)
            act_chunk(1, 1)
            with act.Fori(1, NP - 1) as i:
                for u in range(2):
                    act_chunk(i * 2 + u, u)
            act_chunk(NCH - 2, 0)
            act_chunk(NCH - 1, 1, nxt=False)
            act_chunk(NCH, 0, att=False)
            stage_end(act, 5)

        @block.vector
        def _(dve):
            step = Tally(dve, dve_step)
            dve.wait_ge(wload, N_PREP)
            dve.wait_ge(cols_ready, 16)
            step.add(dve.tensor_tensor(w_D[:, :], wprep[:, 0, :], rows[:, 3, :], ALU.mult))
            step.add(dve.tensor_tensor(skip_b[:, 0:1], col("D_b"), col("D_scale"), ALU.mult))
            dve.wait_ge(prep_act, 1)
            step.add(dve.tensor_scalar(A_c[:, :], A_pos[:, :], 1e-4, None, ALU.is_gt))
            step.wait()
            step.add(dve.scalar_tensor_tensor(A_inj[:, :], A_pos[:, :], -1e-12, A_c[:, :], ALU.add, ALU.mult))
            step.wait()
            step.add(dve.tensor_scalar(A_inj[:, :], A_inj[:, :], 1e-12, None, ALU.add))
            step.wait()
            step.add(dve.tensor_scalar(A_half[:, :], A_inj[:, :], 0.5, None, ALU.mult))
            step.add(dve.tensor_scalar(A_neg[:, :], A_inj[:, :], -1.0, None, ALU.mult))
            step.add(dve.reciprocal(A_c[:, :], A_inj[:, :]))
            step.wait()
            step.add(dve.tensor_scalar(A_c[:, :], A_c[:, :], 0.5, None, ALU.mult))
            dve.wait_ge(prep_mm, 1)
            dve.tensor_copy(MR[:, :], psum[0:64, 7, 0:D]).then_inc(prep_cp, 1)
            dve.wait_ge(prep_mm, 2)
            step.add(dve.tensor_copy(w_mem[:, :], psum[:, 7, 0:D]))
            dve.tensor_tensor(mem_b[:, :], psum[:, 7, D:D + 1], col("recall_b"), ALU.add).then_inc(prep_read, 1)

            def row(k):
                return rows[0:L, k:k + 1, :].to_broadcast([L, CB, D])

            def embed_stats(i):
                for u in range(2):
                    dve.wait_ge(yT_ready, i * 2 + u + 3)
                    src = bank_tm(2 + u)
                    for j in range(CB):
                        step.add(dve.bn_stats(stat0[:, u, j, :], src[:, j, :]))
                    step.wait(True)
                    for j in range(CB):
                        ins = dve.bn_aggr(mv0[:, u, j, :], stat0[:, u, j, :])
                    ins.then_inc(nA0[0], 1)

            def embed_norm(i):
                for u in range(2):
                    c = i * 2 + u
                    src = bank_tm(2 + u)
                    dve.wait_ge(nA0[1], c + 1)
                    for j in range(CB):
                        ins = dve.tensor_scalar(yn[:, u, j, :], src[:, j, :], mv0[:, u, j, 0:1], rstd0[:, u, j:j + 1],
                                                ALU.subtract, ALU.mult)
                    ins.then_inc(yT_free, 1)
                    dve.wait_ge(yT_free, 2 + c + 1)
                    step.add(dve.tensor_tensor(yn[:, u], yn[:, u], row(0), ALU.mult))
                    step.wait()
                    step.add(dve.tensor_tensor(seqs(H, c), yn[:, u], row(1), ALU.add))
                    step.wait(True)
                    norm_stats(dve, nA, step, seqs(H, c), u)

            def stream_norm(i):
                for u in range(2):
                    dve.wait_ge(nA.rstd_ready, i * 2 + u + 1)
                    norm_apply(dve, nA, u, i * 2 + u, True)

            def delta_arg(i):
                for u in range(2):
                    c = i * 2 + u
                    dve.wait_ge(delta_mm, c + 1)
                    dve.tensor_scalar(dl[:, bass.ds(c * CT + 1, CT)], bank(6 + u), col("delta_b"), 0.0, ALU.add, ALU.min)\
                        .then_inc(delta_read, 1)

            dve.memset(dl[:, 0:1], 0.0)
            before_0 = step.n
            embed_stats(0)
            embed_norm(0)
            before_1 = step.n
            embed_stats(1)
            stream_norm(0)
            embed_norm(1)
            for i in step.loop(NP - 2, before_1 - before_0):
                embed_stats(i + 2)
                stream_norm(i + 1)
                delta_arg(i)
                embed_norm(i + 2)
            delta_arg(NP - 2)
            stream_norm(NP - 1)
            delta_arg(NP - 1)
            dve.wait_ge(delta_act, 2)
            step.add(dve.tensor_scalar(dl[:, 1:1 + TOK], dl[:, 1:1 + TOK], 0.5, None, ALU.min))
            stage_end(dve, 1)

            dve.sem_inc(th_free, 2)
            dve.sem_inc(ea_free, 1)
            dve.sem_inc(ra_free, 2)
            dve.sem_inc(B_free, 2)
            def injection(n, u):
                dve.wait_ge(th_ready, n + 1)
                dve.wait_ge(ea_ready, n + 1)
                dve.scalar_tensor_tensor(th[:, u], ea, 1.0, th[:, u], ALU.add, ALU.mult).then_inc(ea_free, 1)

            def decay(n, u):
                dve.wait_ge(ra_ready, n + 1)
                step.add(dve.tensor_scalar(ra[:, u], ra[:, u], 1e6, None, ALU.min))
                step.wait()
                step.add(dve.memset(ra[:, u, 0:TOK:L], 0.0))

            for i in step.loop(NS // 2, 2 * 5):
                injection(i * 2, 0)
                decay(i * 2, 0)
                decay(i * 2 + 1, 1)
                injection(i * 2 + 1, 1)
                for u in range(2):
                    n = i * 2 + u
                    dve.wait_ge(bc_free, NH + (n * 2 + 1) * NH)
                    step.add(dve.reduce_sum(mean[:, u:u + 1], part[:, u, :], axis=AX))
                    step.wait()
                    step.add(dve.tensor_scalar(mean[:, u:u + 1], mean[:, u:u + 1], 1.0 / TOK, None, ALU.mult))
                    step.wait()
                    dve.scalar_tensor_tensor(bufB[:, u], bufB[:, u], mean[:, u:u + 1], th[:, u],
                                             ALU.subtract, ALU.mult).then_inc(th_free, 1)
                    dve.wait_ge(th_free, 2 + n + 1)
                    dve.tensor_tensor_scan(bufB[:, u], ra[:, u], bufB[:, u], 0.0, ALU.mult, ALU.add).then_inc(ra_free, 1)
                    dve.wait_ge(ra_free, 2 + n + 1)
                    dve.wait_ge(bc_free, NH + (n * 2 + 2) * NH)
                    step.add(dve.scalar_tensor_tensor(bufC[:, u], bufB[:, u], A_c[:, bass.ds(n, 1)], bufC[:, u],
                                                      ALU.mult, ALU.mult))
                    step.wait()
                    dve.sem_inc(B_free, 1)
                    dve.sem_inc(prod_ready, 1)
            dve.wait_ge(C_free, NS - 2 + 1)
            for h in range(NH):
                dve.wait_ge(skip_mm, h + 1)
                y3 = Y[:, h * HB * CT:(h + 1) * HB * CT].rearrange("p (s n) -> p s n", s=HB)
                dve.scalar_tensor_tensor(y3, psum[:, h * HB:(h + 1) * HB, 0:CT], skip_b[:, 0:1], y3, ALU.add, ALU.add)
            stage_end(dve, 2)

            dve.sem_inc(hm_free, 2)
            dve.sem_inc(cT_free, 2)
            dve.sem_inc(lg_free, 2)

            def memory_read(i):
                for u in range(2):
                    c = i * 2 + u
                    dve.wait_ge(sig_ready, c + 1)
                    dve.wait_ge(cT_ready, c + 1)
                    step.add(dve.scalar_tensor_tensor(cF[:, u], bank(u), mem_b[:, 0:1], sig[:, u], ALU.add, ALU.mult))
                    step.wait()
                    dve.sem_inc(hm_free, 1)
                    dve.tensor_tensor(cF[:, u], cF[:, u], fm(Y, c), ALU.add).then_inc(cF_ready, 1)

            def onto_stream(i):
                for u in range(2):
                    c = i * 2 + u
                    dve.wait_ge(cT_ready, c + 3)
                    step.add(dve.tensor_tensor(seqs(H, c), bank_tm(4 + u), seqs(H, c), ALU.add))
                    step.wait()
                    dve.sem_inc(cT_free, 1)
                    norm_stats(dve, nC, step, seqs(H, c), u)

            def normed(i):
                for u in range(2):
                    dve.wait_ge(nC.rstd_ready, i * 2 + u + 1)
                    norm_apply(dve, nC, u, i * 2 + u, True)

            def logits_tm(i):
                for u in range(2):
                    c = i * 2 + u
                    dve.wait_ge(lg_mm, c + 3)
                    dve.tensor_copy(lg[:, bass.ds(c * CB, CB), :],
                                    psum[0:L, 6 + u, LG0:LG0 + CB * NE].rearrange("p (j e) -> p j e", j=CB))\
                        .then_inc(lg_free, 1)

            memory_read(0)
            onto_stream(0)
            before_1 = step.n
            memory_read(1)
            normed(0)
            onto_stream(1)
            for i in step.loop(NP - 2, step.n - before_1):
                memory_read(i + 2)
                logits_tm(i)
                normed(i + 1)
                onto_stream(i + 2)
            logits_tm(NP - 2)
            normed(NP - 1)
            logits_tm(NP - 1)
            stage_end(dve, 3)

            def per_e(x):
                return x.rearrange("p (b o) -> p b o", o=1).to_broadcast([L, B, NE])

            def tt(o, a, b, op):
                step.add(dve.tensor_tensor(o, a, b, op))
                step.wait()

            step.add(dve.tensor_reduce(r1, lg, AX, ALU.max))
            step.wait()
            dve.tensor_tensor(lg, lg, per_e(r1), ALU.subtract).then_inc(rt_a, 1)
            dve.wait_ge(rt_b, 1)
            step.add(dve.tensor_reduce(r2, ex, AX, ALU.add))
            step.add(dve.tensor_reduce(r1, ex, AX, ALU.max))
            step.wait()
            tt(oh, ex, per_e(r1), ALU.is_equal)
            tt(cand, oh, prio[0:L, 0:NE].rearrange("p (o e) -> p o e", o=1).to_broadcast([L, B, NE]), ALU.mult)
            step.add(dve.tensor_reduce(r3, cand, AX, ALU.max))
            step.wait()
            tt(oh, cand, per_e(r3), ALU.is_equal)
            tt(cand, ex, oh, ALU.mult)
            tt(cand, ex, cand, ALU.subtract)
            step.add(dve.tensor_reduce(r3, cand, AX, ALU.max))
            step.add(dve.reciprocal(r4, r2))
            step.wait()
            tt(r1, r1, r4, ALU.mult)
            tt(r3, r3, r4, ALU.mult)
            tt(r3, r3, r1, ALU.add)
            step.add(dve.tensor_scalar(r3, r3, 1e-9, None, ALU.add))
            step.wait()
            step.add(dve.reciprocal(r3, r3))
            step.wait()
            tt(gate[:, :], r1, r3, ALU.mult)

            def per_b(x):
                return x.rearrange("p (e o) -> p e o", o=1).to_broadcast([L, NE, B])

            dve.wait_ge(w12_ready, 6 * 16)
            step.add(dve.memset(ones, 1.0))
            step.add(dve.tensor_copy(ohE, oh.rearrange("p b e -> p e b")))
            step.wait()
            step.add(dve.tensor_tensor_scan(cum.rearrange("p e b -> p (e b)"), rest.rearrange("p e b -> p (e b)"),
                                            ohE.rearrange("p e b -> p (e b)"), 0.0, ALU.mult, ALU.add))
            step.wait()
            dve.tensor_copy(row_n, cum[:, :, B - 1]).then_inc(cnt_dve, 1)
            dve.wait_ge(cnt_mm, 1)
            n_all = psum[0:L, 1, 0:NE]
            tt(over, n_all.rearrange("p (e o) -> p e o", o=1).to_broadcast([L, NE, NTHR]),
               thr.rearrange("p (o k) -> p o k", o=1).to_broadcast([L, NE, NTHR]), ALU.is_gt)
            step.add(dve.tensor_reduce(n_tiles, over, AX, ALU.add))
            step.wait()
            step.add(dve.tensor_tensor_scan(start, ones[:, 0:NE], n_tiles, 0.0, ALU.mult, ALU.add))
            step.wait()
            tt(start, start, n_tiles, ALU.subtract)
            step.add(dve.scalar_tensor_tensor(base, start, float(TS), psum[0:L, 0, 0:NE], ALU.mult, ALU.add))
            step.wait()
            tt(cum, cum, per_b(base), ALU.add)
            tt(cum, cum, ohE, ALU.mult)
            step.add(dve.tensor_reduce(r2, cum.rearrange("p e b -> p b e"), AX, ALU.add))
            step.wait()
            dve.tensor_scalar(slot[:, :], r2, -1.0, None, ALU.add).then_inc(slot_ready, 1)
            tt(t_cmp, tile_no.rearrange("p (t o) -> p t o", o=1).to_broadcast([L, NTILE, NE - 1]),
               start[:, 1:NE].rearrange("p (o e) -> p o e", o=1).to_broadcast([L, NTILE, NE - 1]), ALU.is_ge)
            step.add(dve.tensor_reduce(t_exp, t_cmp, AX, ALU.add))
            step.wait()
            dve.tensor_copy(tile_e[:, :], t_exp).then_inc(cnt_dve, 1)

            def tile_in(t, u):
                dve.wait_ge(h_mm, t + 1)
                dve.wait_ge(xT_mm, t + 3)
                dve.tensor_scalar(xeT[:, u], psum[:, u, 0:TS], col("ffn_gamma"), None, ALU.mult).then_inc(xeT_ready, 1)

            def hidden_copy(t, u):
                dve.wait_ge(o_mm, t + 1)
                dve.wait_ge(hT_mm, t + 3)
                dve.tensor_copy(hidT[:, u].rearrange("p j t -> p (j t)"), psum[:, 4 + u, 0:HID]).then_inc(hidT_ready, 1)

            tile_in(0, 0)
            tile_in(1, 1)
            with dve.Fori(1, NTILE // 2) as i:
                for u in range(2):
                    tile_in(i * 2 + u, u)
                    hidden_copy(i * 2 + u - 2, u)
            hidden_copy(NTILE - 2, 0)
            hidden_copy(NTILE - 1, 1)
            stage_end(dve, 4)

            def first_experts(c, u):
                dve.wait_ge(og_ready[u], 8 * CB * (c - u) + 16 * CB)
                g = gate[:, bass.ds(c * CB, CB)].rearrange("p (j o) -> p j o", o=1).to_broadcast([L, CB, D])
                step.add(dve.tensor_tensor(seqs(OG, c), seqs(OG, c), g, ALU.mult))
                step.wait()
                step.add(dve.tensor_tensor(seqs(H, c), seqs(H, c), seqs(OG, c), ALU.add))
                step.wait(True)
                norm_stats(dve, nE, step, seqs(H, c), u)

            def normed_e(c, u):
                dve.wait_ge(nE.rstd_ready, c + 1)
                norm_apply(dve, nE, u, c)

            dve.sem_inc(fo_free, 2)
            dve.sem_inc(facc_add, 2)
            for u in range(2):
                dve.sem_inc(out_done[u], 16)
            E0, E1 = K // 2, L - K // 2

            def per_head(x):
                return x.rearrange("p j (h o) -> p j h o", o=1).to_broadcast([L, CB, HEADS, K])

            def windowed(u, o, other, k, op_out):
                q3 = other.rearrange("p (j l) -> p j l", j=CB)
                k3 = qkv[:, u, k].rearrange("p (j l) -> p j l", j=CB)
                o3 = op_out.rearrange("p (j l) -> p j l", j=CB)
                yield o3[:, :, E0:E1], q3[:, :, E0:E1], k3[:, :, o:o + E1 - E0]
                for lo, at_k in ((0, o), (E1, L - K + o)):
                    yield (o3[:, :, lo:lo + E0], q3[:, :, lo:lo + E0],
                           k3[:, :, at_k:at_k + 1].to_broadcast([128, CB, E0]))

            N = slice(0, NPART)
            zz = [z[:, k, N] for k in range(8)]
            s1 = [zs[:, k:k + 1] for k in range(8)]

            def ts(o, a, x, y, p, q=None):
                if q is None:
                    step.add(dve.tensor_scalar(o, a, x, None, p))
                else:
                    step.add(dve.tensor_scalar(o, a, x, y, p, q))
                step.wait()

            def red(o, a, op):
                step.add(dve.tensor_reduce(o, a, AX, op))
                step.wait()

            def first_largest(p, m, one):
                red(m, p, ALU.max)
                step.add(dve.scalar_tensor_tensor(zz[7], p, m, prio[0:CB, N], ALU.is_equal, ALU.mult))
                step.wait()
                red(s1[7], zz[7], ALU.max)
                ts(one, zz[7], s1[7], None, ALU.is_equal)

            def weigh_experts(f, lo, hi):
                for layer, e, j in FFN[lo:hi]:
                    if (layer, j) == (2, FT - 1):
                        dve.wait_ge(facc_add, f * NE + e + 1)
                        dve.wait_ge(fo_mm, f * NE + e + 4)
                        w = ew[:, e].rearrange("p (j o) -> p j o", o=1).to_broadcast([D, CB, L])
                        dve.tensor_tensor(ftmp[:, e % 2].rearrange("p (j l) -> p j l", j=CB),
                                          bank((2, 4)[e % 2]).rearrange("p (j l) -> p j l", j=CB), w, ALU.mult)\
                            .then_inc(fo_free, 1)

            def store_chunk(g, u, turn):
                dve.wait_ge(fT_ready, g + 1)
                dve.wait_ge(out_done[u], 16 * (turn + 1))
                dve.tensor_tensor(fo[:, u], bank_tm(6), seqs(H, g), ALU.add).then_inc(out_ready, 1)

            def dve_chunk(c, u, turn, att=True, ffn=True, out=True, nxt=True):
                f = c - 1
                if ffn:
                    dve.wait_ge(lgt_mm, f + 1)
                    ts(zz[0], psum[0:CB, 5, 448:448 + NPART], 1.0 / L, None, ALU.mult)
                    red(s1[0], zz[0], ALU.max)
                    dve.tensor_scalar(zz[0], zz[0], s1[0], None, ALU.subtract).then_inc(rt_max, 1)
                if att:
                    dve.wait_ge(qkv_ready, c * 3 + 3)
                    q3, k3 = (qkv[:, u, k].rearrange("p (j l) -> p j l", j=CB) for k in (0, 1))
                    p4 = prod.rearrange("p o (j l) -> p o j l", j=CB)
                    for lo, w0 in ((0, 0), (E1, L - K)):
                        dve.tensor_tensor(
                            p4[:, :, :, lo:lo + E0],
                            q3[:, :, lo:lo + E0].rearrange("p (o j) l -> p o j l", o=1).to_broadcast([D, K, CB, E0]),
                            k3[:, :, w0:w0 + K].rearrange("p j (o l) -> p o j l", l=1).to_broadcast([D, K, CB, E0]),
                            ALU.mult)
                    for o in range(K):
                        dve.tensor_tensor(p4[:, o, :, E0:E1], q3[:, :, E0:E1], k3[:, :, o:o + E1 - E0], ALU.mult)\
                            .then_inc(prod_r, 1)
                if not ffn:
                    dve.wait_ge(v1_hi_ready, 1)
                    dve.tensor_tensor(v1_lo[:, :, :], v1, v1_hi[:, :, :].bitcast(f32), ALU.subtract).then_inc(v1_split, 1)
                if ffn:
                    dve.wait_ge(rt_exp, f + 1)
                    red(s1[1], zz[1], ALU.add)
                    step.add(dve.reciprocal(s1[1], s1[1]))
                    step.wait()
                    ts(zz[1], zz[1], s1[1], None, ALU.mult)
                    first_largest(zz[1], s1[2], zz[2])
                    step.add(dve.scalar_tensor_tensor(zz[3], zz[2], -2.0, zz[1], ALU.mult, ALU.add))
                    step.wait()
                    first_largest(zz[3], s1[3], zz[4])
                    step.add(dve.tensor_tensor(zz[2], zz[2], zz[4], ALU.add))
                    tt(s1[4], s1[2], s1[3], ALU.add)
                    step.add(dve.reciprocal(s1[4], s1[4]))
                    step.wait()
                    dve.scalar_tensor_tensor(zz[5], zz[2], s1[4], zz[1], ALU.mult, ALU.mult).then_inc(wc_ready, 1)
                if att and nxt:
                    first_experts(c + 1, 1 - u)
                if out:
                    store_chunk(c - 2, u, turn - 1)
                if att:
                    s4 = psum[0:L, 5, 0:CB * OH].rearrange("p (j o h) -> p j h o", j=CB, o=K)
                    p4 = P_tm[:, u].rearrange("p j (o h) -> p j h o", o=K)
                    dve.wait_ge(ST_ready, c + 1)
                    step.add(dve.tensor_reduce(mx[:, u], s4, AX, ALU.max))
                    step.wait()
                    dve.tensor_tensor(p4, s4, per_head(mx[:, u]), ALU.subtract).then_inc(sub_done, 1)
                if ffn:
                    dve.wait_ge(wcT_mm, f + 1)
                    dve.tensor_copy(wcT, psum[0:NPART, 5, 460:460 + CB]).then_inc(wcT_ready, 1)
                if att:
                    dve.wait_ge(exp_done, c + 1)
                    step.add(dve.tensor_reduce(sm[:, u], p4, AX, ALU.add))
                    step.wait()
                    step.add(dve.reciprocal(sm[:, u], sm[:, u]))
                    step.wait()
                    dve.tensor_tensor(p4, p4, per_head(sm[:, u]), ALU.mult).then_inc(P_ready, 1)
                if ffn:
                    dve.wait_ge(ew_mm, f + 1)
                    step.add(dve.tensor_copy(ewT, psum[0:NE, 5, 488:488 + CB]))
                    step.add(dve.tensor_copy(ew, psum[:, 5, 464:464 + NE * CB].rearrange("p (e b) -> p e b", e=NE)))
                    step.wait()
                    dve.scalar_tensor_tensor(ewT, ewT, 1e-6, ewT, ALU.is_gt, ALU.mult).then_inc(ewT_ready, 1)
                    step.add(dve.scalar_tensor_tensor(ew, ew, 1e-6, ew, ALU.is_gt, ALU.mult))
                    step.wait()
                    dve.wait_ge(bb_mm, f + 1)
                    dve.tensor_copy(bb, psum[:, 5, 492:492 + CB]).then_inc(ew_ready, 1)
                    dve.wait_ge(ew_ready, f + 1)
                    weigh_experts(f, 0, 17)
                if att:
                    for o in range(K):
                        dve.wait_ge(pb_mm, c * K + o + 1)
                        if o >= 3:
                            dve.wait_ge(pv_add, c * (K - 1) + o - 2)
                        dst_t = pv[:, u] if o == 0 else pv_t[:, o % 2]
                        for dst, a, b in windowed(u, o, bank(6 + o % 2), 2, dst_t):
                            ins = dve.tensor_tensor(dst, a, b, ALU.mult)
                        ins.then_inc(pb_free, 1)
                        if ffn:
                            weigh_experts(f, 17 + o, 18 + o)
                    if ffn:
                        weigh_experts(f, 24, 27)
                    dve.wait_ge(proj_mm, c + 1)
                    dve.wait_ge(bias_added, c + 1)
                    step.add(dve.tensor_tensor(seqs(H, c), bank_tm(3), seqs(H, c), ALU.add))
                    step.wait(True)
                    norm_stats(dve, nF, step, seqs(H, c), u)
                    if nxt:
                        normed_e(c + 1, 1 - u)
                    dve.wait_ge(nF.rstd_ready, c + 1)
                    norm_apply(dve, nF, u, c)
                if ffn:
                    weigh_experts(f, 27 if att else 17, NF)
                if att:
                    dve.wait_ge(nF.xT_free, c + 3)
                    dve.tensor_tensor(fm(xn_lo, c), fm(xnfm, c), fm(xn_hi, c).bitcast(f32), ALU.subtract)\
                        .then_inc(xf_split, 1)
                    dve.tensor_reduce(srep, fm(xnfm, c).rearrange("p (b l) -> p b l", b=CB), AX, ALU.add)\
                        .then_inc(srep_ready, 1)

            first_experts(0, 0)
            normed_e(0, 0)
            dve_chunk(0, 0, 0, ffn=False, out=False)
            before_1 = step.n
            dve_chunk(1, 1, 0, out=False)
            for i in step.loop(NP - 2, 2 * (step.n - before_1)):
                for u in range(2):
                    dve_chunk(i * 2 + 2 + u, u, i + 1)
            dve_chunk(NCH - 2, 0, NP - 1)
            dve_chunk(NCH - 1, 1, NP - 1, nxt=False)
            dve_chunk(NCH, 0, NP, att=False)
            store_chunk(NCH - 1, 1, NP - 1)
            stage_end(dve, 5)

        @block.tensor
        def _(pe):
            pe.sem_inc(y_mm, 2)
            pe.sem_inc(yT_ready, 2)
            pe.sem_inc(nA.xT_ready, 4)
            pe.sem_inc(yT_free, 2)

            def embed(i):
                for u in range(2):
                    c = i * 2 + u
                    pe.wait_ge(xg_ready[u], 16 * (i + 1))
                    pe.wait_ge(y_fm_ready, c + 1)
                    x4 = xg[:, u].rearrange("p j (b g) -> p j b g", b=CB)
                    for n in range(8):
                        j, h = n // 2, n % 2
                        ins = pe.matmul(bank(u).rearrange("p (b l) -> p b l", b=CB), w_emb[:, j, h, :],
                                        x4[:, j, :, h:h + L], start=(n == 0), stop=(n == 7))
                    ins.then_inc(y_mm, 1)

            def to_tm(i):
                for u in range(2):
                    c = i * 2 + u
                    pe.wait_ge(y_fm_ready, c + 3)
                    pe.wait_ge(yT_free, c + 1)
                    for j in range(CB):
                        ins = pe.transpose(bank_tm(2 + u)[:, j, :], y_fm[:, u, j * L:(j + 1) * L], ident[:, :])
                    ins.then_inc(yT_ready, 1)

            def to_fm(nm, i, banks):
                for u in range(2):
                    norm_transposes(pe, nm, u, i * 2 + u, banks)

            def delta(i):
                for u in range(2):
                    c = i * 2 + u
                    pe.wait_ge(nA.xT_free, 2 + 2 * c + 2)
                    pe.wait_ge(delta_read, c + 1)
                    pe.matmul(bank(6 + u), wprep[:, 1, :], fm(xnfm, c), start=True, stop=True).then_inc(delta_mm, 1)

            pe.sem_inc(delta_read, 2)
            pe.wait_ge(w_emb_ready, 16)
            embed(0)
            pe.wait_ge(wload, N_PREP)
            to_tm(0)
            pe.matmul(psum[0:64, 7, 0:D], wprep[0:64, 4, 0:64], wprep[0:64, 5, :], start=True, stop=True)\
                .then_inc(prep_mm, 1)
            pe.wait_ge(prep_cp, 1)
            pe.matmul(psum[:, 7, 0:D], wprep[0:64, 3, :], MR[:, :], start=True, stop=True)
            pe.matmul(psum[:, 7, D:D + 1], MR[:, :], keyb[:, :], start=True, stop=True).then_inc(prep_mm, 1)
            pe.wait_ge(prep_read, 1)
            embed(1)
            with pe.Fori(1, NP - 1) as i:
                to_tm(i)
                embed(i + 1)
                to_fm(nA, i - 1, (4, 5))
                delta(i - 1)
            to_tm(NP - 1)
            to_fm(nA, NP - 2, (4, 5))
            delta(NP - 2)
            to_fm(nA, NP - 1, (4, 5))
            delta(NP - 1)
            stage_end(pe, 1)

            def states(i):
                for u in range(2):
                    n = i * 2 + u
                    pe.wait_ge(w_split, 2 + n + 1)
                    for k in range(2):
                        for h in range(NH):
                            pe.wait_ge(bc_free, n * 2 * NH + k * NH + h + 1)
                            for c in range(h * HB, (h + 1) * HB):
                                a, b = c * CT, (c + 1) * CT
                                pe.matmul(bank(c), w_hi[:, u, k, :], xn_lo[:, a:b], start=True, stop=False)
                                pe.matmul(bank(c), w_lo[:, u, k, :], xn_hi[:, a:b], start=False, stop=False)
                                ins = pe.matmul(bank(c), w_hi[:, u, k, :], xn_hi[:, a:b], start=False, stop=True)
                            ins.then_inc(bc_mm, 1)

            with pe.Fori(0, NS // 2) as i:
                states(i)
            pe.wait_ge(bc_free, NH + 2 * NH * NS)
            for c in range(NCH):
                pe.matmul(bank(c), w_D[:, :], xfm[:, c * CT:(c + 1) * CT], start=True, stop=False)
            for u in range(2):
                pe.wait_ge(prod_ready, NS - 1 + u)
                for c in range(NCH):
                    ins = pe.matmul(bank(c), ident[:, :], bufC[:, u, c * CT:(c + 1) * CT], start=False, stop=(u == 1))
                    if u == 1 and c % HB == HB - 1:
                        ins.then_inc(skip_mm, 1)
            stage_end(pe, 2)

            pe.sem_inc(cT_ready, 2)
            pe.sem_inc(nC.xT_ready, 2)
            def read_memory(i):
                for u in range(2):
                    c = i * 2 + u
                    pe.wait_ge(hm_free, c + 1)
                    pe.matmul(bank(u), w_mem[:, :], fm(Y, c), start=True, stop=True)
                    pe.matmul(bank(2 + u), wprep[:, 2, :], fm(Y, c), start=True, stop=True).then_inc(hm_mm, 1)

            def memory_tm(i):
                for u in range(2):
                    c = i * 2 + u
                    pe.wait_ge(cF_ready, c + 1)
                    pe.wait_ge(cT_free, c + 1)
                    for j in range(CB):
                        ins = pe.transpose(bank_tm(4 + u)[:, j, :], cF[:, u, j * L:(j + 1) * L], ident[:, :])
                    ins.then_inc(cT_ready, 1)

            def logits(i):
                for u in range(2):
                    c = i * 2 + u
                    pe.wait_ge(nC.xT_free, 2 + c + 1)
                    pe.wait_ge(lg_free, c + 1)
                    for j in range(CB):
                        ins = pe.matmul(psum[0:L, 6 + u, LG0 + j * NE:LG0 + (j + 1) * NE],
                                        lgx[:, u, j * L:(j + 1) * L], smallw[:, 0:NE], start=True, stop=True)
                    ins.then_inc(lg_mm, 1)

            pe.sem_inc(lg_mm, 2)
            read_memory(0)
            memory_tm(0)
            read_memory(1)
            with pe.Fori(1, NP - 1) as i:
                memory_tm(i)
                read_memory(i + 1)
                to_fm(nC, i - 1, (6, 7))
                logits(i - 1)
            memory_tm(NP - 1)
            to_fm(nC, NP - 2, (6, 7))
            logits(NP - 2)
            to_fm(nC, NP - 1, (6, 7))
            logits(NP - 1)
            stage_end(pe, 3)

            pe.wait_ge(cnt_dve, 1)
            pe.matmul(psum[0:L, 0, 0:NE], before, row_n, start=True, stop=True)
            pe.matmul(psum[0:L, 1, 0:NE], ones, row_n, start=True, stop=True).then_inc(cnt_mm, 1)

            def tile_in(t, u):
                pe.wait_ge(xt_ready[u], 8 * (t - u) + 16)
                pe.transpose(psum[:, u, 0:TS], xt[:, u], ident[:, :]).then_inc(xT_mm, 1)

            e_new = [pe.alloc_register("e_new0"), pe.alloc_register("e_new1")]
            e_old = [pe.alloc_register("e_old0"), pe.alloc_register("e_old1")]

            def next_expert(t, u, keep=True):
                if keep:
                    pe.reg_mov(e_old[u], e_new[u])
                pe.reg_load(e_new[u], tile_e[0:1, bass.ds(t, 1)])

            def expert(reg):
                return pe.snap(reg, min_val=0, max_val=NE - 1)

            def layer1(t, u, e):
                pe.wait_ge(xeT_ready, t + 1)
                pe.wait_ge(hid_ready, t + 1)
                pe.matmul(psum[:, 2 + u, 0:HID], xeT[:, u], w1[:, bass.ds(e, 1), :].rearrange("p a h -> p (a h)"),
                          start=True, stop=True).then_inc(h_mm, 1)

            def turn(t, u):
                pe.wait_ge(hid_ready, t + 3)
                for j in range(HT):
                    ins = pe.transpose(psum[:, 4 + u, j * TS:(j + 1) * TS], hid[:, u, j * D:(j + 1) * D], ident[:, :])
                ins.then_inc(hT_mm, 1)

            def layer2(t, u, e):
                pe.wait_ge(hidT_ready, t + 1)
                pe.wait_ge(ot_ready, t + 1)
                for j in range(HT):
                    ins = pe.matmul(psum[:, 6 + u, 0:D], hidT[:, u, j], w2[:, bass.ds(e, 1), j].rearrange("p a d -> p (a d)"),
                                    start=(j == 0), stop=(j == HT - 1))
                ins.then_inc(o_mm, 1)

            pe.wait_ge(cnt_dve, 2)
            for s in (xT_mm, h_mm, hT_mm, o_mm):
                pe.sem_inc(s, 2)
            def moe_step(t, u, more=True):
                layer1(t, u, expert(e_new[u]))
                if more:
                    next_expert(t + 1, 1 - u)
                    tile_in(t + 1, 1 - u)
                turn(t - 1, 1 - u)
                layer2(t - 2, u, expert(e_old[u]))

            tile_in(0, 0)
            next_expert(0, 0, False)
            next_expert(1, 1, False)
            layer1(0, 0, expert(e_new[0]))
            tile_in(1, 1)
            layer1(1, 1, expert(e_new[1]))
            next_expert(2, 0)
            tile_in(2, 0)
            turn(0, 0)
            with pe.Fori(1, NTILE // 2 - 1) as i:
                for u in range(2):
                    moe_step(i * 2 + u, u)
            moe_step(NTILE - 2, 0)
            moe_step(NTILE - 1, 1, False)
            turn(NTILE - 1, 1)
            layer2(NTILE - 2, 0, expert(e_new[0]))
            layer2(NTILE - 1, 1, expert(e_new[1]))
            stage_end(pe, 4)

            pe.sem_inc(nE.xT_ready, 2)
            norm_transposes(pe, nE, 0, 0, (7, 7))
            pe.wait_ge(wE_ready, 6 * 16)
            pe.sem_inc(nF.xT_ready, 2)
            pe.sem_inc(fo_mm, 3)

            def ffn(f, lo, hi):
                for layer, e, j in FFN[lo:hi]:
                    kk = D if j < 2 else FR
                    if layer == 1:
                        if (e, j) == (0, 0):
                            pe.wait_ge(xf_split, f + 1)
                        pe.wait_ge(f_free, (f * NE + e) * FT + j + 1)
                        o = bank(j % 2 if e % 2 == 0 else (j + 1) % 2, kk)
                        w_hi_, w_lo_ = v1_hi[:, e, j * D:j * D + kk], v1_lo[:, e, j * D:j * D + kk]
                        pe.matmul(o, w_hi_, fm(xn_lo, f), start=True, stop=False)
                        pe.matmul(o, w_lo_, fm(xn_hi, f), start=False, stop=False)
                        pe.matmul(o, w_hi_, fm(xn_hi, f), start=False, stop=True).then_inc(f_mm, 1)
                    else:
                        if j == 0:
                            pe.wait_ge(fo_free, f * NE + e + 1)
                            pe.wait_ge(f_free, 2 + (f * NE + e) * FT + FT)
                        w = v2[:, e, j, :] if j < 2 else v2b[:, e, :]
                        ins = pe.matmul(bank((2, 4)[e % 2]), w, fh[0:kk, e % 3, j], start=(j == 0), stop=(j == FT - 1))
                        if j == FT - 1:
                            ins.then_inc(fo_mm, 1)

            def result_tm(g):
                pe.wait_ge(facc_add, g * NE + NE + 2)
                for j in range(CB):
                    ins = pe.transpose(bank_tm(6)[:, j, :], facc[:, j * L:(j + 1) * L], ident[:, :])
                ins.then_inc(fT_ready, 1)

            def pe_chunk(c, u, att=True, ffn_=True, out=True, nxt=True):
                f = c - 1
                if att:
                    pe.wait_ge(nE.xT_free, c + 3)
                    for k, b in enumerate((6, 7, 3)):
                        pe.matmul(bank(b), w_qkv[:, k, :], fm(xfm, c), start=True, stop=True).then_inc(qkv_mm, 1)
                if ffn_:
                    pe.wait_ge(srep_ready, f + 1)
                    pe.matmul(psum[0:CB, 5, 448:448 + NPART], srep, smallw[:, NE:NE + NPART], start=True, stop=True)\
                        .then_inc(lgt_mm, 1)
                    ffn(f, 0, 2)
                for o in range(K):
                    if att:
                        pe.wait_ge(prod_r, c * K + o + 1)
                        pe.matmul(bank(3, OH), sel[:, o, :], prod[:, o], start=(o == 0), stop=False)
                    if ffn_:
                        ffn(f, 2 + o, 3 + o)
                if att:
                    pe.matmul(bank(3, OH), rpb_w, posc, start=False, stop=True).then_inc(S_mm, 1)
                if out:
                    result_tm(c - 2)
                if ffn_:
                    wait_apart(pe, wc_ready, f + 1)
                    pe.transpose(psum[0:NPART, 5, 460:460 + CB], z[:, 5, 0:NPART], ident[0:CB, 0:CB]).then_inc(wcT_mm, 1)
                    ffn(f, 9, 11)
                if att:
                    pe.wait_ge(S_ready, c + 1)
                    for j in range(CB):
                        ins = pe.transpose(psum[0:L, 5, j * OH:(j + 1) * OH], S_fm[:, j * L:(j + 1) * L],
                                           ident[0:OH, 0:OH])
                    ins.then_inc(ST_ready, 1)
                if ffn_:
                    ffn(f, 11, 14)
                    pe.wait_ge(wcT_ready, f + 1)
                    for e in range(NE):
                        pe.matmul(psum[:, 5, 464 + e * CB:464 + (e + 1) * CB], pwb[:, e, :], wcT, start=True, stop=True)
                    pe.matmul(psum[0:NE, 5, 488:488 + CB], pw, wcT, start=True, stop=True).then_inc(ew_mm, 1)
                    ffn(f, 14, 16)
                    pe.wait_ge(ewT_ready, f + 1)
                    pe.matmul(psum[:, 5, 492:492 + CB], b2, ewT, start=True, stop=True).then_inc(bb_mm, 1)
                    ffn(f, 16, 17)
                if att:
                    pe.wait_ge(P_ready, c + 1)
                    for j in range(CB):
                        ins = pe.transpose(psum[0:OH, 3, j * L:(j + 1) * L], P_tm[:, u, j], ident[0:L, 0:L])
                    ins.then_inc(PT_ready, 1)
                if ffn_:
                    ffn(f, 17, 19)
                if att:
                    pe.wait_ge(P_fm_ready, c + 1)
                    for o in range(K):
                        if o >= 2:
                            pe.wait_ge(pb_free, c * K + o - 1)
                        elif o == 0 and out:
                            pe.wait_ge(out_ready, c - 1)
                        pe.matmul(bank(6 + o % 2), spread[:, o, :], P_fm[:, u], start=True, stop=True).then_inc(pb_mm, 1)
                        if ffn_:
                            ffn(f, 19 + o, 20 + o)
                    if ffn_:
                        ffn(f, 26, 28)
                    pe.wait_ge(pv_add, c * (K - 1) + K - 1)
                    for j in range(CB):
                        ins = pe.matmul(bank_tm(3)[:, j, :], pv[:, u, j * L:(j + 1) * L], w_proj,
                                        start=True, stop=True)
                    ins.then_inc(proj_mm, 1)
                    if ffn_:
                        ffn(f, 28, 34)
                    if nxt:
                        norm_transposes(pe, nE, 1 - u, c + 1, (7, 7))
                    if ffn_:
                        ffn(f, 34, NF)
                    norm_transposes(pe, nF, u, c, (5, 5))
                elif ffn_:
                    ffn(f, 19, NF)

            pe_chunk(0, 0, ffn_=False, out=False)
            pe.wait_ge(wF_ready, 7 * 16)
            pe.wait_ge(v1_split, 1)
            pe_chunk(1, 1, out=False)
            with pe.Fori(1, NP - 1) as i:
                for u in range(2):
                    pe_chunk(i * 2 + u, u)
            pe_chunk(NCH - 2, 0)
            pe_chunk(NCH - 1, 1, nxt=False)
            pe_chunk(NCH, 0, att=False)
            pe.wait_ge(out_ready, NCH - 1)
            result_tm(NCH - 1)
            stage_end(pe, 5)


def kernel(**inp):
    import numpy as np
    import concourse.bacc as bacc
    from concourse.bass_utils import run_bass_kernel_spmd

    a = {k: np.asarray(v) for k, v in inp.items()}
    B, S, C = a["x"].shape
    L = (S - 16) // 8 + 1
    G, D, CB, NS, NE, K, HEADS = L + 1, 128, 4, 16, 6, 7, 16
    f = np.float32

    def c_(x):
        return np.ascontiguousarray(x)

    t = {}
    x = a["x"][:, :G * 8].reshape(B // CB, CB, G, 512).transpose(0, 3, 1, 2)
    t["xg"] = c_(x.reshape(B // CB, 4, 128, CB * G).transpose(0, 2, 1, 3))
    w = a["L0_tok_W"].reshape(C, 2, 8, D).transpose(2, 0, 1, 3).reshape(4, 128, 2, D)
    t["w_emb"] = c_(w.transpose(1, 0, 2, 3))
    one = lambda k: a[k].reshape(D, 1)
    b1 = a["L1_ffn_b1"]
    t["cols"] = c_(np.concatenate([
        one("L0_tok_b"), one("L0_attn_ln_gamma"), one("L0_attn_ln_beta"), one("L0_attn_D_b"),
        one("L0_attn_D_scale"), one("L0_attn_recall_b"), one("L0_ffn_gamma"),
        a["L1_attn_qkv_b"].reshape(3, D).T, a["L0_attn_A_log"], a["L0_attn_B_b"].reshape(D, NS),
        a["L0_attn_C_b"].reshape(D, NS), b1[:, :2 * D].reshape(NE * 2, D).T,
        np.broadcast_to(a["L0_attn_delta_b"].reshape(1, 1), (D, 1)),
        np.broadcast_to(a["L0_attn_gate_b"].reshape(1, 1), (D, 1))], axis=1))
    t["rows"] = c_(np.broadcast_to(np.stack([a["L0_tok_gamma"], a["L0_tok_beta"], a["L1_attn_proj_b"],
                                             a["L0_attn_D_scale"]])[None], (128, 4, D)))
    t["ident"] = np.eye(128, dtype=f)
    t["w_full"] = c_(np.stack([a["L0_attn_D_W"], np.broadcast_to(a["L0_attn_delta_W"], (D, D)),
                               np.broadcast_to(a["L0_attn_gate_W"], (D, D))], axis=1))
    t["key_WT"] = c_(a["L0_attn_key_W"].T)
    t["M_T"] = c_(a["L0_attn_M"].T)
    t["recall_W"] = a["L0_attn_recall_W"]
    t["key_b"] = a["L0_attn_key_b"].reshape(64, 1)
    t["smallw"] = c_(np.concatenate([a["L0_ffn_w_gating"], a["L1_ffn_router_w"].T], axis=1))
    t["prio"] = c_(np.broadcast_to(np.arange(16, 0, -1).astype(f)[None], (128, 16)))
    TOK = B * L
    NTILE = (TOK + NE * 127) // 128
    NTILE += NTILE % 2
    t["before"] = np.triu(np.ones((L, L), f), 1)
    t["thr"] = c_(np.broadcast_to(128 * np.arange(-(-TOK // 128)).astype(f)[None], (L, -(-TOK // 128))))
    t["tile_no"] = c_(np.broadcast_to(np.arange(NTILE).astype(f)[None], (L, NTILE)))
    rest = np.ones((L, NE, B), f)
    rest[:, :, 0] = 0
    t["rest"] = rest
    bw = a["L0_attn_B_W"].reshape(D, D, NS).transpose(2, 0, 1)
    cw = a["L0_attn_C_W"].reshape(D, D, NS).transpose(2, 0, 1)
    t["wBC"] = c_(np.stack([bw, cw], axis=2))
    t["w1"] = c_(a["L0_ffn_w1"].transpose(1, 0, 2))
    t["w2"] = c_(a["L0_ffn_w2"].reshape(NE, 4, D, D).transpose(2, 0, 1, 3))
    t["w_qkv"] = c_(a["L1_attn_qkv_w"].reshape(3, D, D).transpose(2, 0, 1))
    t["w_proj"] = c_(a["L1_attn_proj_w"].T)
    head = np.arange(D) // (D // HEADS)
    sel = np.zeros((D, K, K * HEADS), f)
    for o in range(K):
        sel[np.arange(D), o, o * HEADS + head] = 1
    t["sel"] = sel
    t["spread"] = c_(sel.transpose(2, 1, 0))
    t["rpb_w"] = c_(np.stack([a["L1_attn_rpb"][:, c:c + K].T.reshape(-1) for c in range(K)]))
    pos = np.arange(L)
    first = np.clip(pos - K // 2, 0, L - K) - pos + K - 1
    t["posc"] = c_(np.tile((first[None] == np.arange(K)[:, None]).astype(f), (1, CB)))
    v = a["L1_ffn_W1"]
    t["v1"] = c_(v.transpose(1, 0, 2))
    t["v2"] = c_(a["L1_ffn_W2"][:, :2 * D].reshape(NE, 2, D, D).transpose(2, 0, 1, 3))
    t["v2b"] = c_(a["L1_ffn_W2"][:, 2 * D:].transpose(1, 0, 2))
    t["b1b"] = c_(b1[:, 2 * D:].T)
    t["b2"] = a["L1_ffn_b2"]
    parts = [(6,), (5, 1), (4, 2), (4, 1, 1), (3, 3), (3, 2, 1), (3, 1, 1, 1), (2, 2, 2), (2, 2, 1, 1),
             (2, 1, 1, 1, 1), (1, 1, 1, 1, 1, 1)]
    pw = np.zeros((11, NE), f)
    for i, p in enumerate(parts):
        for j, q in enumerate(p):
            pw[i, j] = q / 6
    t["pw"] = pw
    t["pwb"] = c_(np.broadcast_to(pw[:, :, None], (11, NE, D)))

    nc = bacc.Bacc("TRN2", target_bir_lowering=False, num_devices=1)
    f32 = mybir.dt.float32
    aps = {k: nc.dram_tensor("in_" + k, v.shape, f32, kind="ExternalInput").ap() for k, v in t.items()}
    out = nc.dram_tensor("out_0", (B, L, D), f32, kind="ExternalOutput").ap()
    audio_tower(nc, aps, out)
    r = run_bass_kernel_spmd(nc, [{"in_" + k: v for k, v in t.items()}], core_ids=[0])
    return r.results[0]["out_0"]
```
